# Optimizing a Trainium2 kernel written in Bass

```python
import numpy as np
import jax
import jax.numpy as jnp

def _softmax(x, axis=-1):
    return jax.nn.softmax(x, axis=axis)

def _gelu(x):
    return jax.nn.gelu(x, approximate=True)

def _silu(x):
    return jax.nn.silu(x)

def _sigmoid(x):
    return jax.nn.sigmoid(x)

def _layernorm(x, axis=-1, eps=1e-05):
    m = jnp.mean(x, axis=axis, keepdims=True)
    v = jnp.var(x, axis=axis, keepdims=True)
    return (x - m) / jnp.sqrt(v + eps)

def _scatter_add(tgt, idx, src, axis=0):
    return tgt.at[idx].add(src)

def _segment_sum(src, seg, n):
    return jax.ops.segment_sum(src, seg, n)
kernel_name = 'mk_decoder_preln_d1_seqx_r4_be807f'

def setup_inputs(seed: int=0):
    np.random.seed(seed)
    _w = jnp.asarray

    def _rec_inputs():
        import jax
        import jax.numpy as jnp
        _rk = jax.random.key(seed)
        x = -0.0002928 + 1 * jax.random.normal(jax.random.fold_in(_rk, 1), (16, 256, 256), jnp.float32)
        _lenS = 256 - jax.random.randint(jax.random.fold_in(_rk, 7), (16,), 0, max(1, 256 // 4) + 1, jnp.int32)
        _lenS2 = 120 - jax.random.randint(jax.random.fold_in(_rk, 8), (16,), 0, max(1, 120 // 4) + 1, jnp.int32)
        _ctx_1024P = jax.random.normal(jax.random.fold_in(_rk, 11), (16, 16, 256), jnp.float32)
        _ctx_1024c = jax.random.dirichlet(jax.random.fold_in(_rk, 511), 0.3 * jnp.ones((16,), jnp.float32), (16, 120))
        _ctx_1024t = jnp.einsum('bsk,bkd->bsd', _ctx_1024c, _ctx_1024P)
        _ctx_1024t = _ctx_1024t * jax.lax.rsqrt(jnp.mean(jnp.square(_ctx_1024t)) + 1e-12) * 0.953939
        ctx_1024 = -1.39393e-06 + 0.999914 * (_ctx_1024t + 0.3 * jax.random.normal(jax.random.fold_in(_rk, 611), (16, 120, 256), jnp.float32))
        return (x, ctx_1024)
    x, ctx_1024 = _rec_inputs()

    def _L0_attn_setup():
        import jax, jax.numpy as jnp
        import numpy as np
        D_MODEL = 256
        LN_EPS = 1e-05
        DEN_EPS = 1e-06

        def _layer_norm(x, g, b):
            mu = jnp.mean(x, axis=-1, keepdims=True)
            var = jnp.mean(jnp.square(x - mu), axis=-1, keepdims=True)
            return (x - mu) * jax.lax.rsqrt(var + LN_EPS) * g + b
        key = jax.random.key(seed)
        ks = jax.random.split(key, 7)
        s = 1.0 / np.sqrt(D_MODEL)
        x = jax.random.normal(ks[0], (4, 512, D_MODEL), dtype=jnp.float32)
        qkv_w = jax.random.uniform(ks[1], (D_MODEL, 3 * D_MODEL), jnp.float32, -s, s)
        qkv_b = jax.random.uniform(ks[2], (3 * D_MODEL,), jnp.float32, -s, s)
        gate_w = jax.random.uniform(ks[3], (D_MODEL, D_MODEL), jnp.float32, -s, s)
        gate_b = jax.random.uniform(ks[4], (D_MODEL,), jnp.float32, -s, s)
        ln_g = jnp.ones((D_MODEL,), jnp.float32)
        ln_b = jnp.zeros((D_MODEL,), jnp.float32)
        return {'x': x, 'qkv_w': qkv_w, 'qkv_b': qkv_b, 'gate_w': gate_w, 'gate_b': gate_b, 'ln_g': ln_g, 'ln_b': ln_b}
    _L0_attn_all = _L0_attn_setup()
    _L0_attn_in = {k: v for k, v in _L0_attn_all.items() if k in ('qkv_w', 'qkv_b', 'gate_w', 'gate_b', 'ln_g', 'ln_b')}
    del _L0_attn_all

    def _L0_xattn_setup():
        import jax, jax.numpy as jnp
        import numpy as np
        D_MODEL = 256
        N_HEADS = 16
        D_KEYS = D_MODEL // N_HEADS
        key = jax.random.key(seed)
        ks = jax.random.split(key, 11)
        B, L, S = (2, 512, 512)
        inp = {'queries': jax.random.normal(ks[0], (B, L, D_MODEL), dtype=jnp.float32), 'keys': jax.random.normal(ks[1], (B, S, D_MODEL), dtype=jnp.float32), 'values': jax.random.normal(ks[2], (B, S, D_MODEL), dtype=jnp.float32), 'Wq': jax.random.normal(ks[3], (D_MODEL, D_MODEL), dtype=jnp.float32) / np.sqrt(D_MODEL), 'bq': jax.random.normal(ks[4], (D_MODEL,), dtype=jnp.float32) / np.sqrt(D_MODEL), 'Wk': jax.random.normal(ks[5], (D_MODEL, D_MODEL), dtype=jnp.float32) / np.sqrt(D_MODEL), 'bk': jax.random.normal(ks[6], (D_MODEL,), dtype=jnp.float32) / np.sqrt(D_MODEL), 'Wv': jax.random.normal(ks[7], (D_MODEL, D_MODEL), dtype=jnp.float32) / np.sqrt(D_MODEL), 'bv': jax.random.normal(ks[8], (D_MODEL,), dtype=jnp.float32) / np.sqrt(D_MODEL), 'Wo': jax.random.normal(ks[9], (D_MODEL, D_MODEL), dtype=jnp.float32) / np.sqrt(D_MODEL), 'bo': jax.random.normal(ks[10], (D_MODEL,), dtype=jnp.float32) / np.sqrt(D_MODEL)}
        return inp
    _L0_xattn_all = _L0_xattn_setup()
    _L0_xattn_in = {k: v for k, v in _L0_xattn_all.items() if k in ('Wq', 'bq', 'Wk', 'bk', 'Wv', 'bv', 'Wo', 'bo')}
    del _L0_xattn_all

    def _L0_ffn_setup():
        import jax, jax.numpy as jnp
        import numpy as np
        DIM = 256
        HIDDEN = 256
        NUM_EXPERTS = 8
        TOP_K = 2
        key = jax.random.key(seed)
        ks = jax.random.split(key, 8)
        std = 0.02
        x = jax.random.normal(ks[0], (2, 256, DIM), dtype=jnp.float32)
        gate_w = jax.random.normal(ks[1], (NUM_EXPERTS, DIM), dtype=jnp.float32) * std
        w1 = jax.random.normal(ks[2], (NUM_EXPERTS, DIM, HIDDEN), dtype=jnp.float32) * std
        w2 = jax.random.normal(ks[3], (NUM_EXPERTS, HIDDEN, DIM), dtype=jnp.float32) * std
        w3 = jax.random.normal(ks[4], (NUM_EXPERTS, DIM, HIDDEN), dtype=jnp.float32) * std
        w1s = jax.random.normal(ks[5], (1, DIM, HIDDEN), dtype=jnp.float32) * std
        w2s = jax.random.normal(ks[6], (1, HIDDEN, DIM), dtype=jnp.float32) * std
        w3s = jax.random.normal(ks[7], (1, DIM, HIDDEN), dtype=jnp.float32) * std
        return {'x': x, 'gate_w': gate_w, 'w1': w1, 'w2': w2, 'w3': w3, 'w1s': w1s, 'w2s': w2s, 'w3s': w3s}
    _L0_ffn_all = _L0_ffn_setup()
    _L0_ffn_in = {k: v for k, v in _L0_ffn_all.items() if k in ('gate_w', 'w1', 'w2', 'w3', 'w1s', 'w2s', 'w3s')}
    del _L0_ffn_all
    return {'x': x, 'ctx_1024': ctx_1024, 'L0_attn_qkv_w': _L0_attn_in['qkv_w'], 'L0_attn_qkv_b': _L0_attn_in['qkv_b'], 'L0_attn_gate_w': _L0_attn_in['gate_w'], 'L0_attn_gate_b': _L0_attn_in['gate_b'], 'L0_attn_ln_g': _L0_attn_in['ln_g'], 'L0_attn_ln_b': _L0_attn_in['ln_b'], 'L0_xattn_Wq': _L0_xattn_in['Wq'], 'L0_xattn_bq': _L0_xattn_in['bq'], 'L0_xattn_Wk': _L0_xattn_in['Wk'], 'L0_xattn_bk': _L0_xattn_in['bk'], 'L0_xattn_Wv': _L0_xattn_in['Wv'], 'L0_xattn_bv': _L0_xattn_in['bv'], 'L0_xattn_Wo': _L0_xattn_in['Wo'], 'L0_xattn_bo': _L0_xattn_in['bo'], 'L0_ffn_gate_w': _L0_ffn_in['gate_w'], 'L0_ffn_w1': _L0_ffn_in['w1'], 'L0_ffn_w2': _L0_ffn_in['w2'], 'L0_ffn_w3': _L0_ffn_in['w3'], 'L0_ffn_w1s': _L0_ffn_in['w1s'], 'L0_ffn_w2s': _L0_ffn_in['w2s'], 'L0_ffn_w3s': _L0_ffn_in['w3s']}

def reference(x, ctx_1024, L0_attn_qkv_w, L0_attn_qkv_b, L0_attn_gate_w, L0_attn_gate_b, L0_attn_ln_g, L0_attn_ln_b, L0_xattn_Wq, L0_xattn_bq, L0_xattn_Wk, L0_xattn_bk, L0_xattn_Wv, L0_xattn_bv, L0_xattn_Wo, L0_xattn_bo, L0_ffn_gate_w, L0_ffn_w1, L0_ffn_w2, L0_ffn_w3, L0_ffn_w1s, L0_ffn_w2s, L0_ffn_w3s):
    import jax
    import jax.numpy as jnp

    def _L0_attn_ref(x, qkv_w, qkv_b, gate_w, gate_b, ln_g, ln_b):
        import jax, jax.numpy as jnp
        import numpy as np
        D_MODEL = 256
        LN_EPS = 1e-05
        DEN_EPS = 1e-06

        def _layer_norm(x, g, b):
            mu = jnp.mean(x, axis=-1, keepdims=True)
            var = jnp.mean(jnp.square(x - mu), axis=-1, keepdims=True)
            return (x - mu) * jax.lax.rsqrt(var + LN_EPS) * g + b
        B, T, D = x.shape
        xn = _layer_norm(x, ln_g, ln_b)
        qkv = xn @ qkv_w + qkv_b
        q, k, v = jnp.split(qkv, 3, axis=-1)
        gate = jax.nn.sigmoid(xn @ gate_w + gate_b)
        k = k * gate
        q = jax.nn.elu(q) + 1.0
        k = jax.nn.elu(k) + 1.0
        attn = jnp.einsum('btd,bsd->bts', q, k)
        mask = jnp.tril(jnp.ones((T, T), dtype=attn.dtype))
        attn = attn * mask
        out_num = jnp.einsum('bts,bsd->btd', attn, v)
        k_cumsum = jnp.cumsum(k, axis=1)
        out_den = jnp.sum(q * k_cumsum, axis=-1, keepdims=True) + DEN_EPS
        return out_num / out_den

    def _L0_xattn_ref(queries, keys, values, Wq, bq, Wk, bk, Wv, bv, Wo, bo):
        import jax, jax.numpy as jnp
        import numpy as np
        D_MODEL = 256
        N_HEADS = 16
        D_KEYS = D_MODEL // N_HEADS
        B, L, _ = queries.shape
        S = keys.shape[1]
        H, E = (N_HEADS, D_KEYS)
        scale = E ** (-0.5)
        q = (queries @ Wq.T + bq).reshape(B, L, H, E)
        k = (keys @ Wk.T + bk).reshape(B, S, H, E)
        v = (values @ Wv.T + bv).reshape(B, S, H, E)
        scores = jnp.einsum('blhe,bshe->bhls', q, k)
        attn = jax.nn.softmax(scores * scale, axis=-1)
        out = jnp.einsum('bhls,bshe->blhe', attn, v).reshape(B, L, H * E)
        return out @ Wo.T + bo

    def _L0_ffn_ref(x, gate_w, w1, w2, w3, w1s, w2s, w3s):
        import jax, jax.numpy as jnp
        import numpy as np
        DIM = 256
        HIDDEN = 256
        NUM_EXPERTS = 8
        TOP_K = 2
        bs, slen, dim = x.shape
        xt = x.reshape(bs * slen, dim)
        logits = xt @ gate_w.T
        scores = jax.nn.softmax(logits.astype(jnp.float32), axis=1).astype(x.dtype)
        top_scores, sel = jax.lax.top_k(scores, TOP_K)
        sel_flat = sel.reshape(-1)
        order = jnp.argsort(sel_flat, stable=True)
        top_scores_sorted = top_scores.reshape(-1)[order]
        token_idx = order // TOP_K
        eid = sel_flat[order]
        routed_in = xt[token_idx] * top_scores_sorted[:, None]
        out_routed = jnp.zeros_like(routed_in)
        for e in range(NUM_EXPERTS):
            m = (eid == e)[:, None]
            xe = jnp.where(m, routed_in, 0.0)
            h = jax.nn.silu(xe @ w1[e]) * (xe @ w3[e])
            out_routed = out_routed + jnp.where(m, h @ w2[e], 0.0)
        hs = jax.nn.silu(xt @ w1s[0]) * (xt @ w3s[0])
        out = hs @ w2s[0]
        out = out.at[token_idx].add(out_routed)
        return out.reshape(bs, slen, dim)
    x = x + _L0_attn_ref(_layernorm(x, axis=-1), L0_attn_qkv_w, L0_attn_qkv_b, L0_attn_gate_w, L0_attn_gate_b, L0_attn_ln_g, L0_attn_ln_b)
    x = x + _L0_xattn_ref(_layernorm(x, axis=-1), ctx_1024, ctx_1024, L0_xattn_Wq, L0_xattn_bq, L0_xattn_Wk, L0_xattn_bk, L0_xattn_Wv, L0_xattn_bv, L0_xattn_Wo, L0_xattn_bo)
    x = x + _L0_ffn_ref(_layernorm(x, axis=-1), L0_ffn_gate_w, L0_ffn_w1, L0_ffn_w2, L0_ffn_w3, L0_ffn_w1s, L0_ffn_w2s, L0_ffn_w3s)
    return x

_drawn_inputs = setup_inputs


def setup_inputs(seed=0):
    import zlib

    import numpy as np

    out = dict(_drawn_inputs(seed))
    spreads = {'L0_attn_ln_g': (1.0, 0.6), 'L0_attn_ln_b': (0.0, 0.1)}
    factors = {'L0_attn_gate_w': 8.0,
     'L0_attn_gate_b': 8.0,
     'L0_xattn_bq': 4.574,
     'L0_xattn_bk': 8.0,
     'L0_ffn_gate_w': 8.0,
     'L0_ffn_w1': 8.0,
     'L0_ffn_w2': 8.0,
     'L0_ffn_w3': 8.0,
     'L0_ffn_w1s': 3.918,
     'L0_ffn_w2s': 3.872,
     'L0_ffn_w3s': 3.864}
    for name, (base, spread) in spreads.items():
        noise = np.random.default_rng([zlib.crc32(name.encode()), seed]).standard_normal(out[name].shape)
        drawn = base * np.exp(spread * noise) if base else spread * noise
        out[name] = jnp.asarray(drawn.astype(out[name].dtype))
    for name, factor in factors.items():
        out[name] = (out[name] * factor).astype(out[name].dtype)
    return out
```

```python
from contextlib import ExitStack

import concourse.bass as bass
from concourse import mybir

P = 128
ALU = mybir.AluOpType
ACT = mybir.ActivationFunctionType
AX = mybir.AxisListType
F32 = mybir.dt.float32
BF16 = mybir.dt.bfloat16
I32 = mybir.dt.int32
U32 = mybir.dt.uint32

LN_EPS = 1e-5
DEN_EPS = 1e-6
TOP_K = 2


def decoder_layer_kernel(
    nc: bass.Bass,
    x: bass.AP,
    ctx_mem: bass.AP,
    w_qkv: bass.AP,
    b_qkv: bass.AP,
    w_gate: bass.AP,
    b_gate: bass.AP,
    ln_g: bass.AP,
    ln_b: bass.AP,
    wq_t: bass.AP,
    bq: bass.AP,
    wk_t: bass.AP,
    bk: bass.AP,
    wv_t: bass.AP,
    bv: bass.AP,
    wo_t: bass.AP,
    bo: bass.AP,
    router_t: bass.AP,
    w13: bass.AP,
    w2: bass.AP,
    w13s: bass.AP,
    w2s: bass.AP,
    out: bass.AP,
):
    B, T, D = x.shape
    S = ctx_mem.shape[1]
    E = w13.shape[0]
    HEADS = 16
    HD = D // HEADS
    KC = D // P
    TT = T // P
    NT = B * TT
    HC = P // HD
    QH = HC // 2
    UNITS = TT * KC * 2
    SCALE = float(HD) ** -0.5
    REGION = B * T + P
    IDLE_ROW = E * REGION
    EXPERT_TILES = TOP_K * NT + E
    PR = 4

    rows_in = nc.dram_tensor("rows_in", (IDLE_ROW + P, D), F32, kind="Internal").ap()
    rows_out = nc.dram_tensor("rows_out", (EXPERT_TILES * P, D), F32, kind="Internal").ap()

    with ExitStack() as ctx:
        def sb(name, shape, dt=F32):
            return ctx.enter_context(nc.sbuf_tensor(name, shape, dt))

        def sem(name):
            return ctx.enter_context(nc.semaphore(name))

        banks = [ctx.enter_context(nc.psum_tensor(f"bank{i}", [P, 512], F32)) for i in range(8)]
        A, BB, C, DD, EE, FF, GG, HH = banks

        def half(bank):
            return bank[:].rearrange("p (a n) -> p a n", a=2)

        wqkv_sb = sb("wqkv_sb", [P, KC, 3 * D])
        wg_sb = sb("wg_sb", [P, KC, D])
        wq_sb = sb("wq_sb", [P, KC, D])
        wk_sb = sb("wk_sb", [P, KC, D])
        wv_sb = sb("wv_sb", [P, KC, D])
        wo_sb = sb("wo_sb", [P, KC, D])
        router_sb = sb("router_sb", [P, KC, E])
        w13_sb = sb("w13_sb", [P, E, KC, 2 * D])
        cols = sb("cols", [P, 8, KC])
        G_, B_, BQ, BK, BG, BQ2, BK2 = range(7)
        cols2 = sb("cols2", [P, 3, KC])
        bv_row = sb("bv_row", [P, D])
        bv2_row = sb("bv2_row", [P, D])
        bo_row = sb("bo_row", [P, D])
        ident = sb("ident", [P, P])
        causal3 = sb("causal3", [P, 3, P])
        before = sb("before", [P, P], BF16)
        ones_b = sb("ones_b", [P, P], BF16)
        head_mask = sb("head_mask", [P, HC])
        pair_ones = sb("pair_ones", [S, 2, 2 * HD])
        minus_half = sb("minus_half", [P, TT])
        iota_e = sb("iota_e", [P, E])
        zeros = sb("zeros", [P, D])

        x_all = sb("x_all", [P, NT, D])
        x3n_t = sb("x3n_t", [P, KC, B * T])
        pos_f = sb("pos_f", [P, NT, TOP_K])
        pos_all = sb("pos_all", [P, NT, TOP_K], I32)

        stats1 = sb("stats1", [P, TT, 6])
        mv1 = sb("mv1", [P, TT, 2])
        var1 = sb("var1", [P, TT])
        rstd1 = sb("rstd1", [P, TT])
        z1 = sb("z1", [P, TT, D])
        xn_t = sb("xn_t", [P, KC, T])
        th = sb("th", [P, KC, T])
        gate = sb("gate", [P, KC, T])
        kg = sb("kg", [P, KC, T])
        kg1 = sb("kg1", [P, KC, T])
        ek = sb("ek", [P, KC, T])
        eq = sb("eq", [P, KC, T])
        q1 = sb("q1", [P, KC, T])
        q_t, k_t = q1, kg1
        v_ext = sb("v_ext", [P, TT, D + 1])
        at = sb("at", [P, 3, P])
        den = sb("den", [P, TT])
        rden = sb("rden", [P, TT])

        ctx_sb = sb("ctx_sb", [S, D])
        ctx_t = sb("ctx_t", [P, KC, S])
        k2 = sb("k2", [P, KC, S])
        k_blk = sb("k_blk", [P, KC, HC, S])
        v_pad = sb("v_pad", [S, HEADS // 2, 2, 2 * HD])
        stats2 = sb("stats2", [P, TT, 6])
        mv2 = sb("mv2", [P, TT, 2])
        var2 = sb("var2", [P, TT])
        rstd2 = sb("rstd2", [P, TT])
        z2 = sb("z2", [P, TT, D])
        z2_t = sb("z2_t", [P, KC, T])
        q2_t = sb("q2_t", [P, KC, T])
        mx = sb("mx", [P, 2, QH])
        pr = sb("pr", [P, PR, QH, S])
        p_full = sb("p_full", [P, HEADS, T])
        p_t = p_full[0:S]
        assert E * KC * D <= HEADS * T
        w2_sb = p_full[:].rearrange("p h t -> p (h t)")[:, 0:E * KC * D].rearrange("p (e c n) -> p e c n", e=E, c=KC)
        o_t = sb("o_t", [P, KC, T])

        stats3 = sb("stats3", [P, TT, 6])
        mv3 = sb("mv3", [P, TT, 2])
        var3 = sb("var3", [P, TT])
        rstd3 = sb("rstd3", [P, TT])
        z3 = sb("z3", [P, TT, D])
        lg_t = sb("lg_t", [E, T])
        lg = sb("lg", [P, TT, E])
        top = sb("top", [P, TT, 8])
        top_i = sb("top_i", [P, TT, 8], U32)
        top_f = sb("top_f", [P, TT, TOP_K])
        diff = sb("diff", [P, TT, E + TOP_K])
        ediff = sb("ediff", [P, TT, E + TOP_K])
        esum = sb("esum", [P, TT])
        erec = sb("erec", [P, TT])
        score = sb("score", [P, TT, TOP_K])
        pick = sb("pick", [P, TT, TOP_K, E])
        pick_b = sb("pick_b", [P, TT, E], BF16)
        base = sb("base", [P, E])
        posx = sb("posx", [P, TT, E])
        posm = sb("posm", [P, TT, TOP_K, E])
        pos_cur = sb("pos_cur", [P, TT, TOP_K], I32)
        xs = sb("xs", [P, TT, TOP_K, D])
        iota_p = sb("iota_p", [P, 1])
        ebase = sb("ebase", [P, E])
        pad_i = sb("pad_i", [P, E], I32)

        cnt = sb("cnt", [P, E])
        tiles_i = sb("tiles_i", [P, E], I32)
        tiles = sb("tiles", [P, E])
        tile_end = sb("tile_end", [P, E])
        coef = sb("coef", [P, E])
        iota_t = sb("iota_t", [1, EXPERT_TILES])
        tile_e = sb("tile_e", [1, EXPERT_TILES])
        tile_r = sb("tile_r", [1, EXPERT_TILES])
        tab_e = sb("tab_e", [1, EXPERT_TILES], I32)
        tab_r = sb("tab_r", [1, EXPERT_TILES], I32)

        assert EXPERT_TILES * E <= 2 * KC * T and KC * 3 * D <= KC * HC * S
        pr_flat = pr[:].rearrange("p a h s -> p (a h s)")
        past, past_c = (pr_flat[0:1, k * EXPERT_TILES * E:(k + 1) * EXPERT_TILES * E]
                        .rearrange("p (n e) -> p n e", e=E) for k in range(2))
        assert NT * TOP_K * (E - 1) <= KC * T and 2 * EXPERT_TILES * E + NT * TOP_K <= PR * QH * S
        beyond, beyond_c = (t[:].rearrange("p c t -> p (c t)")[:, 0:NT * TOP_K * (E - 1)]
                            .rearrange("p (n e) -> p n e", e=E - 1) for t in (ek, q1))
        moved = pr_flat[:, 2 * EXPERT_TILES * E:2 * EXPERT_TILES * E + NT * TOP_K]

        k_blk_flat = k_blk[:].rearrange("p c h s -> p (c h s)")
        w13s_sb = k_blk_flat[:, 0:KC * 2 * D].rearrange("p (c n) -> p c n", c=KC)
        w2s_sb = k_blk_flat[:, KC * 2 * D:KC * 3 * D].rearrange("p (c n) -> p c n", c=KC)

        xe, xe_t, eth, eu, eh, eh_t, ey = (t[:] for t in (z1, xn_t, th, gate, kg, kg1, ek))
        xe_t = xe_t.rearrange("p s (c t) -> p s c t", c=KC)
        eh_t = eh_t.rearrange("p s (c t) -> p s c t", c=KC)

        sth, su, sh, sum1, sum2, fin = (t[:] for t in (eq, q1, q_t, k_t, z2, z3))
        got = xs[:].rearrange("p j k d -> p (j k) d")
        pos_now = sb("pos_now", [P, TT, TOP_K], I32)

        x_in, ctx_in, w_in, cols_in, exp_w_in = (sem(n) for n in ("x_in", "ctx_in", "w_in", "cols_in", "exp_w_in"))
        cols_ready, const, zeroed = sem("cols_ready"), sem("const"), sem("zeroed")
        stats1_s, mv1_s, var1_s, rstd1_s, z1_s, z1t_p, xnt_s = (
            sem(n) for n in ("stats1_s", "mv1_s", "var1_s", "rstd1_s", "z1_s", "z1t_p", "xnt_s"))
        gate_p, k_p, q_p, v_p, sc_p, av_p = (sem(n) for n in ("gate_p", "k_p", "q_p", "v_p", "sc_p", "av_p"))
        th_s, gate_s, kg_s, kg1_s, ek_s, q1_s, qt_s, kt_s, v_s, at_s, den_s, rden_s, x2_s = (
            sem(n) for n in ("th_s", "gate_s", "kg_s", "kg1_s", "ek_s", "q1_s", "qt_s", "kt_s", "v_s", "at_s", "den_s",
                             "rden_s", "x2_s"))
        ctxt_p, k2_p, v2_p, z2t_p, q2_p, s_p, pt_p, o_p, den2_p, y_p = (
            sem(n) for n in ("ctxt_p", "k2_p", "v2_p", "z2t_p", "q2_p", "s_p", "pt_p", "o_p", "den2_p", "y_p"))
        ctxt_s, k2_s, kblk_s, vpad_s, stats2_s, mv2_s, var2_s, rstd2_s, z2_s, z2t_s, q2t_s = (
            sem(n) for n in ("ctxt_s", "k2_s", "kblk_s", "vpad_s", "stats2_s", "mv2_s", "var2_s", "rstd2_s", "z2_s",
                             "z2t_s", "q2t_s"))
        max_s, sub_s, exp_s, pt_s, rec_s, ot_s, xb_s, x3_s = (
            sem(n) for n in ("max_s", "sub_s", "exp_s", "pt_s", "rec_s", "ot_s", "xb_s", "x3_s"))
        stats3_s, mv3_s, var3_s, rstd3_s, z3_s, z3t_p, x3t_s, lgt_p, lgt_s, lg_p, lg_s = (
            sem(n) for n in ("stats3_s", "mv3_s", "var3_s", "rstd3_s", "z3_s", "z3t_p", "x3t_s", "lgt_p", "lgt_s",
                             "lg_p", "lg_s"))
        top_s, topi_s, topf_s, diff_s, ediff_s, esum_s, erec_s, score_s, pick_s, pickb_s, rank_p = (
            sem(n) for n in ("top_s", "topi_s", "topf_s", "diff_s", "ediff_s", "esum_s", "erec_s", "score_s", "pick_s",
                             "pickb_s", "rank_p"))
        posx_s, base_s, posm_s, posf_s, pos_s, xs_s, scattered = (
            sem(n) for n in ("posx_s", "base_s", "posm_s", "posf_s", "pos_s", "xs_s", "scattered"))
        base0_s, vones_s, padi_s, padded, idle_in, tab_step, tab_s = (
            sem(n) for n in ("base0_s", "vones_s", "padi_s", "padded", "idle_in", "tab_step", "tab_s"))
        moved_s = sem("moved_s")
        shared_in, w2_in = sem("shared_in"), sem("w2_in")
        xe_in = [sem("xe_in0"), sem("xe_in1")]
        xet_p, xet_s, h_p, eth_s, eu_s, eh_s, eht_p, eht_s, ey_p, ey_s, ey_out = (
            sem(n) for n in ("xet_p", "xet_s", "h_p", "eth_s", "eu_s", "eh_s", "eht_p", "eht_s", "ey_p", "ey_s",
                             "ey_out"))
        a_p, b_p, sth_s, su_s, sh_s, sy_p, posn_s, got_s, sum1_s, sum2_s, fin_s, fin_out = (
            sem(n) for n in ("a_p", "b_p", "sth_s", "su_s", "sh_s", "sy_p", "posn_s", "got_s", "sum1_s", "sum2_s",
                             "fin_s", "fin_out"))

        x_v = x.rearrange("b (j p) d -> b p j d", p=P)
        out_v = out.rearrange("b (j p) d -> b p j d", p=P)
        weights = ((wg_sb, w_gate), (wqkv_sb, w_qkv), (wk_sb, wk_t), (wv_sb, wv_t), (wq_sb, wq_t), (wo_sb, wo_t),
                   (router_sb, router_t))
        shared_weights = ((w13s_sb, w13s), (w2s_sb, w2s))
        vectors = (ln_g, ln_b, b_qkv[0:D], b_qkv[D:2 * D], b_gate, bq, bk)
        rows = ((bv_row, b_qkv[2 * D:3 * D]), (bv2_row, bv), (bo_row, bo))
        N_COLS = 16 * (len(vectors) + len(rows))
        N_CONST = 14

        block = ctx.enter_context(nc.Block())

        def after(eng, s, count):
            if not isinstance(count, int) or count > 0:
                eng.wait_ge(s, count)

        def apart(eng):
            eng.nop(nofuse=True)

        @block.sync
        def _(sp):
            sp.dma_start(x_all[:, 0:TT, :], x_v[0]).then_inc(x_in, 16)
            sp.dma_start(ctx_sb[:], ctx_mem[0]).then_inc(ctx_in, 16)
            for dst, src in weights:
                sp.dma_start(dst[:], src.rearrange("(c p) n -> p c n", p=P)).then_inc(w_in, 16)
            with sp.Fori(1, B) as b:
                sp.wait_ge(x_in, 16 * b)
                sp.dma_start(x_all[:, bass.ds(b * TT, TT), :], x_v[bass.ds(b, 1)].squeeze(0)).then_inc(x_in, 16)
                sp.wait_ge(ctxt_p, b)
                sp.dma_start(ctx_sb[:], ctx_mem[bass.ds(b, 1)].squeeze(0)).then_inc(ctx_in, 16)
            sp.wait_ge(den2_p, B)
            sp.dma_start(w2_sb, w2.rearrange("e (c p) n -> p e c n", p=P)).then_inc(w2_in, 16)
            sp.wait_ge(s_p, UNITS * B)
            for dst, src in shared_weights:
                sp.dma_start(dst, src.rearrange("(c p) n -> p c n", p=P)).then_inc(shared_in, 16)
            sp.wait_ge(scattered, 16 * B * TT * TOP_K)
            sp.wait_ge(padded, 16 * E)
            sp.wait_ge(idle_in, 16)
            sp.wait_ge(tab_s, 1)

            def load_tile(n, s):
                row = nc.sync.value_load(tab_r[0:1, bass.ds(n, 1)], min_val=0, max_val=IDLE_ROW)
                after(sp, xet_p, n - 1)
                sp.dma_start(xe[:, s, :], rows_in[bass.ds(row, P), :]).then_inc(xe_in[s], 16)

            load_tile(0, 0)
            load_tile(1, 1)
            with sp.Fori(1, EXPERT_TILES // 2) as m:
                load_tile(2 * m, 0)
                load_tile(2 * m + 1, 1)
            with sp.Fori(0, B) as b:
                sp.wait_ge(fin_s, b + 1)
                sp.dma_start(out_v[bass.ds(b, 1)].squeeze(0), fin).then_inc(fin_out, 16)
            sp.wait_ge(fin_out, 16 * B)

        @block.scalar
        def _(act):
            for i, v in enumerate(vectors):
                with nc.allow_non_contiguous_dma(reason="channels onto partitions, once"):
                    act.dma_start(cols[:, i, :], v.rearrange("(c p) -> p c", p=P)).then_inc(cols_in, 16)
            for dst, v in rows:
                act.dma_start(dst[:], v.rearrange("(a d) -> a d", a=1).to_broadcast([P, D])).then_inc(cols_in, 16)
            act.dma_start(w13_sb[:], w13.rearrange("e (c p) n -> p e c n", p=P)).then_inc(exp_w_in, 16)
            act.wait_ge(cols_in, N_COLS)
            act.wait_ge(cols_ready, 3)

            def norm_t(b):
                act.wait_ge(z1t_p, b + 1)
                after(act, v_p, b)
                for c in range(KC):
                    i = act.activation(xn_t[:, c, :], half(A)[:, c, :], ACT.Identity,
                                       bias=cols[:, B_, c:c + 1], scale=cols[:, G_, c:c + 1])
                i.then_inc(xnt_s, 1)

            def gate_tanh(b):
                act.wait_ge(gate_p, b + 1)
                after(act, gate_s, b)
                for c in range(KC):
                    i = act.activation(th[:, c, :], half(BB)[:, c, :], ACT.Tanh, bias=cols2[:, 1, c:c + 1], scale=0.5)
                i.then_inc(th_s, 1)

            def q_exp(b):
                act.wait_ge(q_p, b + 1)
                after(act, qt_s, b)
                after(act, sc_p, b)
                for c in range(KC):
                    act.activation(eq[:, c, :], half(DD)[:, c, :], ACT.Exp, bias=cols[:, BQ, c:c + 1])
                for c in range(KC):
                    i = act.activation(q1[:, c, :], half(DD)[:, c, :], ACT.Identity, bias=cols2[:, 0, c:c + 1])
                i.then_inc(q1_s, 1)

            def k_exp(b):
                act.wait_ge(kg_s, b + 1)
                after(act, kt_s, b)
                act.activation(ek[:], kg[:], ACT.Exp).then_inc(ek_s, 1)

            def ctx_copy(b):
                act.wait_ge(ctxt_p, b + 1)
                after(act, v2_p, b)
                act.copy(ctx_t[:].rearrange("p c s -> p (c s)"), EE[:, 0:KC * S]).then_inc(ctxt_s, 1)

            def k2_bias(b):
                act.wait_ge(k2_p, b + 1)
                after(act, kblk_s, b)
                for c in range(KC):
                    i = act.activation(k2[:, c, :], half(FF)[:, c, 0:S], ACT.Identity, bias=cols[:, BK2, c:c + 1])
                i.then_inc(k2_s, 1)

            def z2_copy(b):
                act.wait_ge(z2t_p, b + 1)
                after(act, q2_p, b)
                act.copy(z2_t[:], half(GG)).then_inc(z2t_s, 1)

            def q2_scale(b):
                act.wait_ge(q2_p, b + 1)
                after(act, s_p, UNITS * b)
                for c in range(KC):
                    i = act.activation(q2_t[:, c, :], half(HH)[:, c, :], ACT.Identity, bias=cols2[:, 2, c:c + 1],
                                       scale=SCALE)
                i.then_inc(q2t_s, 1)

            def soft_exp(b, u):
                act.wait_ge(sub_s, UNITS * b + u + 1)
                act.activation(pr[:, u % PR], pr[:, u % PR], ACT.Exp).then_inc(exp_s, 1)

            def p_copy(b, u):
                j, h0 = u // 4, (u % 4) * QH
                act.wait_ge(pt_p, UNITS * b + u + 1)
                if u == 0:
                    after(act, den2_p, b)
                bank = (GG, HH)[u % 2]
                act.copy(p_t[:, h0:h0 + QH, j * P:(j + 1) * P],
                         bank[0:S, :].rearrange("s (h t) -> s h t", h=QH)).then_inc(pt_s, 1)

            def x3_copy(b):
                act.wait_ge(z3t_p, b + 1)
                act.copy(x3n_t[:, :, bass.ds(b * T, T)], half(HH)).then_inc(x3t_s, 1)

            def router_exp(b):
                act.wait_ge(diff_s, b + 1)
                after(act, score_s, b)
                act.activation(ediff[:], diff[:], ACT.Exp).then_inc(ediff_s, 1)

            def turn(i, first, last):
                j = i - 1
                if not first:
                    ctx_copy(j)
                    k2_bias(j)
                if not last:
                    norm_t(i)
                if not first:
                    z2_copy(j)
                    q2_scale(j)
                    for u in range(UNITS + 2):
                        if u < UNITS:
                            soft_exp(j, u)
                        if u == 2 and not last:
                            gate_tanh(i)
                        if u == 6 and not last:
                            q_exp(i)
                        if u == 8 and not last:
                            k_exp(i)
                        if u >= 2:
                            p_copy(j, u - 2)
                    x3_copy(j)
                    router_exp(j)
                else:
                    gate_tanh(i)
                    q_exp(i)
                    k_exp(i)

            turn(0, True, False)
            turn(1, False, False)
            with act.Fori(2, B) as i:
                turn(i, False, False)
            turn(B, False, True)

            def tile_copy_x(n, s):
                act.wait_ge(xet_p, n + 1)
                after(act, h_p, n - 1)
                act.copy(xe_t[:, s], (A, BB)[s][:, 0:D].rearrange("p (c t) -> p c t", c=KC)).then_inc(xet_s, 1)

            def tile_tanh(n, s):
                act.wait_ge(h_p, n + 1)
                after(act, eu_s, n - 1)
                act.activation(eth[:, s, :], (C, DD)[s][:, 0:D], ACT.Tanh, scale=0.5).then_inc(eth_s, 1)

            def tile_copy_h(n, s):
                act.wait_ge(eht_p, n + 1)
                after(act, ey_p, n - 1)
                act.copy(eh_t[:, s], (EE, FF)[s][:, 0:D].rearrange("p (c t) -> p c t", c=KC)).then_inc(eht_s, 1)

            def tile_step(n, s, ahead2=True, ahead1=True):
                if ahead2:
                    tile_copy_x(n + 2, s)
                tile_copy_h(n, s)
                if ahead1:
                    tile_tanh(n + 1, 1 - s)

            tile_copy_x(0, 0)
            tile_copy_x(1, 1)
            tile_tanh(0, 0)
            tile_step(0, 0)
            tile_step(1, 1)
            with act.Fori(1, EXPERT_TILES // 2 - 1) as m:
                n = 2 * m
                tile_step(n, 0)
                tile_step(n + 1, 1)
            tile_step(EXPERT_TILES - 2, 0, ahead2=False)
            tile_step(EXPERT_TILES - 1, 1, ahead2=False, ahead1=False)

            def shared_tanh(b):
                act.wait_ge(a_p, b + 1)
                after(act, su_s, b)
                act.activation(sth, half(A), ACT.Tanh, scale=0.5).then_inc(sth_s, 1)

            shared_tanh(0)
            with act.Fori(1, B) as b:
                shared_tanh(b)

        @block.gpsimd
        def _(pool):
            g = nc.gpsimd
            g.memset(ident[:], 1.0)
            g.memset(causal3[:], 1.0)
            g.memset(before[:], 1.0)
            g.memset(ones_b[:], 1.0)
            g.memset(head_mask[:], 1.0)
            g.memset(pair_ones[:], 0.0)
            g.memset(minus_half[:], -0.5)
            g.memset(v_pad[:], 0.0)
            g.memset(zeros[:], 0.0)
            g.iota(iota_e[:], [[1, E]], base=0, channel_multiplier=0, allow_small_or_imprecise_dtypes=True)
            g.iota(ebase[:], [[REGION, E]], base=0, channel_multiplier=0, allow_small_or_imprecise_dtypes=True)
            g.iota(iota_p[:], [[0, 1]], base=0, channel_multiplier=1, allow_small_or_imprecise_dtypes=True)
            g.iota(iota_t[:], [[1, EXPERT_TILES]], base=0, channel_multiplier=0,
                   allow_small_or_imprecise_dtypes=True)
            g.memset(v_ext[:, :, D:D + 1], 1.0).then_inc(zeroed, 1)
            pool.wait_ge(zeroed, 1)
            g.affine_select(out=ident[:], in_=ident[:], compare_op=ALU.is_equal, fill=0.0, base=0,
                            pattern=[[-1, P]], channel_multiplier=1)
            for d in (0, 2):
                g.affine_select(out=causal3[:, d], in_=causal3[:, d], compare_op=ALU.is_ge, fill=0.0, base=0,
                                pattern=[[1, P]], channel_multiplier=-1)
            g.affine_select(out=before[:], in_=before[:], compare_op=ALU.is_gt, fill=0.0, base=0,
                            pattern=[[1, P]], channel_multiplier=-1)
            for e in range(2):
                g.memset(pair_ones[:, e, e * HD:(e + 1) * HD], 1.0)
            g.affine_select(out=head_mask[:], in_=head_mask[:], compare_op=ALU.is_ge, fill=0.0, base=0,
                            pattern=[[-HD, HC]], channel_multiplier=1).then_inc(zeroed, 1)
            pool.wait_ge(zeroed, 2)
            g.affine_select(out=head_mask[:], in_=head_mask[:], compare_op=ALU.is_ge, fill=0.0, base=HD - 1,
                            pattern=[[HD, HC]], channel_multiplier=-1).then_inc(const, 1)
            pool.wait_ge(const, 1)
            g.dma_start(rows_in[IDLE_ROW:IDLE_ROW + P, :], zeros[:]).then_inc(idle_in, 16)
            pool.wait_ge(cols_in, N_COLS)
            g.tensor_scalar(cols2[:, 0, :], cols[:, BQ, :], 1.0, None, ALU.add).then_inc(cols_ready, 1)
            g.tensor_scalar(cols2[:, 1, :], cols[:, BG, :], 0.5, None, ALU.mult).then_inc(cols_ready, 1)
            g.tensor_scalar(cols2[:, 2, :], cols[:, BQ2, :], SCALE, None, ALU.mult).then_inc(cols_ready, 1)

            def rstd(b, mv, mv_s, var, var_s, out_, out_s, twice, readers):
                pool.wait_ge(mv_s, b + 1)
                apart(pool)
                scale, offset = (1.0 + LN_EPS, LN_EPS * LN_EPS) if twice else (1.0, LN_EPS)
                g.tensor_scalar(var[:], mv[:, :, 1], scale, offset, ALU.mult, ALU.add).then_inc(var_s, 1)
                pool.wait_ge(var_s, b + 1)
                after(pool, readers, b)
                g.tensor_tensor(out_[:], var[:], minus_half[:], ALU.pow).then_inc(out_s, 1)

            def gate_affine(b):
                pool.wait_ge(th_s, b + 1)
                after(pool, kg_s, b)
                apart(pool)
                g.tensor_scalar(gate[:], th[:], 0.5, 0.5, ALU.mult, ALU.add).then_inc(gate_s, 1)

            def kg_plus(b):
                pool.wait_ge(kg_s, b + 1)
                after(pool, sc_p, b)
                apart(pool)
                g.tensor_scalar(kg1[:], kg[:], 1.0, None, ALU.add).then_inc(kg1_s, 1)

            def k_blocks(b):
                pool.wait_ge(k2_s, b + 1)
                after(pool, s_p, UNITS * b)
                for c in range(KC):
                    i = g.tensor_tensor(k_blk[:, c], k2[:, c:c + 1, :].to_broadcast([P, HC, S]),
                                        head_mask[:].rearrange("p (h a) -> p h a", a=1).to_broadcast([P, HC, S]),
                                        ALU.mult)
                i.then_inc(kblk_s, 1)

            def residual_bias(b):
                pool.wait_ge(x2_s, b + 1)
                pool.wait_ge(z2_s, b + 1)
                x2 = x_all[:, bass.ds(b * TT, TT), :]
                g.tensor_tensor(x2, x2,
                                bo_row[:].rearrange("p (a d) -> p a d", a=1).to_broadcast([P, TT, D]),
                                ALU.add).then_inc(xb_s, 1)

            def scale_rows(b):
                pool.wait_ge(score_s, b + 1)
                pool.wait_ge(z3_s, b + 1)
                after(pool, scattered, 16 * TT * TOP_K * b)
                apart(pool)
                for j in range(TT):
                    for k in range(TOP_K):
                        i = g.tensor_scalar(xs[:, j, k, :], z3[:, j, :], score[:, j, k:k + 1], None, ALU.mult)
                i.then_inc(xs_s, 1)

            def scatter(b):
                pool.wait_ge(xs_s, b + 1)
                pool.wait_ge(pos_s, b + 1)
                apart(pool)
                for j in range(TT):
                    for k in range(TOP_K):
                        g.indirect_dma_start(
                            out=rows_in[:], out_offset=bass.IndirectOffsetOnAxis(ap=pos_cur[:, j, k:k + 1], axis=0),
                            in_=xs[:, j, k, :], in_offset=None).then_inc(scattered, 16)

            def turn(i, first, last):
                j = i - 1
                if not first:
                    rstd(j, mv2, mv2_s, var2, var2_s, rstd2, rstd2_s, False, z2_s)
                if not last:
                    rstd(i, mv1, mv1_s, var1, var1_s, rstd1, rstd1_s, True, z1_s)
                if not first:
                    k_blocks(j)
                if not last:
                    gate_affine(i)
                    kg_plus(i)
                if not first:
                    residual_bias(j)
                    rstd(j, mv3, mv3_s, var3, var3_s, rstd3, rstd3_s, False, z3_s)
                    scale_rows(j)
                    scatter(j)

            turn(0, True, False)
            turn(1, False, False)
            with pool.Fori(2, B) as i:
                turn(i, False, False)
            turn(B, False, True)

            pool.wait_ge(padi_s, 1)
            for e in range(E):
                g.indirect_dma_start(out=rows_in[:], out_offset=bass.IndirectOffsetOnAxis(ap=pad_i[:, e:e + 1], axis=0),
                                     in_=zeros[:], in_offset=None).then_inc(padded, 16)

            def store_tile(n, s):
                pool.wait_ge(ey_s, n + 1)
                after(pool, ey_out, 16 * n)
                g.dma_start(rows_out[bass.ds(n * P, P), :], ey[:, s, :]).then_inc(ey_out, 16)

            store_tile(0, 0)
            store_tile(1, 1)
            with pool.Fori(1, EXPERT_TILES // 2) as m:
                store_tile(2 * m, 0)
                store_tile(2 * m + 1, 1)

            pool.wait_ge(ey_out, 16 * EXPERT_TILES)
            pool.wait_ge(moved_s, 4)
            def gather(b):
                after(pool, got_s, 16 * TT * TOP_K * b)
                g.tensor_copy(pos_now[:], pos_all[:, bass.ds(b * TT, TT), :]).then_inc(posn_s, 1)
                pool.wait_ge(posn_s, b + 1)
                after(pool, sum1_s, b)
                apart(pool)
                for j in range(TT):
                    for k in range(TOP_K):
                        g.indirect_dma_start(
                            out=got[:, j * TOP_K + k, :], out_offset=None, in_=rows_out[:],
                            in_offset=bass.IndirectOffsetOnAxis(ap=pos_now[:, j, k:k + 1], axis=0),
                        ).then_inc(got_s, 16)
                pool.wait_ge(got_s, 16 * TT * TOP_K * (b + 1))
                g_v = got.rearrange("p (j k) d -> p j k d", k=TOP_K)
                g.tensor_tensor(sum1, g_v[:, :, 0, :], g_v[:, :, 1, :], ALU.add).then_inc(sum1_s, 1)
                pool.wait_ge(sum1_s, b + 1)
                after(pool, fin_s, b)
                g.tensor_tensor(sum2, sum1, x_all[:, bass.ds(b * TT, TT), :], ALU.add).then_inc(sum2_s, 1)

            gather(0)
            with pool.Fori(1, B) as b:
                gather(b)

        @block.tensor
        def _(pe):
            def project(bank, w, c0, src, n=T):
                for m in range(KC):
                    for c in range(KC):
                        i = pe.matmul(half(bank)[:, m, 0:n], w[:, c, c0 + m * P:c0 + (m + 1) * P], src[:, c, 0:n],
                                      start=(c == 0), stop=(c == KC - 1))
                return i

            def project_rows(bank, src, w, c0):
                for j in range(TT):
                    for c in range(KC):
                        i = pe.matmul(half(bank)[:, j, :], src[:, c, j * P:(j + 1) * P], w[:, c, c0:c0 + D],
                                      start=(c == 0), stop=(c == KC - 1))
                return i

            def turn_tiles(bank, src):
                for j in range(TT):
                    for c in range(KC):
                        i = pe.transpose(half(bank)[:, c, j * P:(j + 1) * P], src[:, j, c * P:(c + 1) * P], ident[:])
                return i

            def z1_turn(b):
                pe.wait_ge(z1_s, b + 1)
                after(pe, v_s, b)
                turn_tiles(A, z1).then_inc(z1t_p, 1)

            def gate_proj(b):
                pe.wait_ge(xnt_s, b + 1)
                after(pe, at_s, b)
                project(BB, wg_sb, 0, xn_t).then_inc(gate_p, 1)

            def k_proj(b):
                after(pe, x2_s, b)
                project(C, wqkv_sb, D, xn_t).then_inc(k_p, 1)

            def q_proj(b):
                project(DD, wqkv_sb, 0, xn_t).then_inc(q_p, 1)

            def v_proj(b):
                project_rows(A, xn_t, wqkv_sb, 2 * D).then_inc(v_p, 1)

            def scores(b):
                pe.wait_ge(kt_s, b + 1)
                pe.wait_ge(qt_s, b + 1)
                pe.wait_ge(th_s, b + 1)
                for s0, t0, o0 in ((0, 0, 0), (1, 1, 2)):
                    n = T - t0 * P
                    for c in range(KC):
                        i = pe.matmul(BB[:, o0 * P:o0 * P + n], k_t[:, c, s0 * P:(s0 + 1) * P], q_t[:, c, t0 * P:T],
                                      start=(c == 0), stop=(c == KC - 1))
                i.then_inc(sc_p, 1)

            def values(b):
                pe.wait_ge(at_s, b + 1)
                pe.wait_ge(v_s, b + 1)
                pe.wait_ge(kg_s, b + 1)
                pe.wait_ge(q1_s, b + 1)
                pe.matmul(C[:, 0:D + 1], at[:, 0, :], v_ext[:, 0, :], start=True, stop=True)
                pe.matmul(DD[:, 0:D + 1], at[:, 1, :], v_ext[:, 0, :], start=True, stop=False)
                pe.matmul(DD[:, 0:D + 1], at[:, 2, :], v_ext[:, 1, :], start=False, stop=True).then_inc(av_p, 1)

            def ctx_turn(b):
                pe.wait_ge(ctx_in, 16 * (b + 1))
                after(pe, lgt_s, b)
                for c in range(KC):
                    i = pe.transpose(EE[:, c * S:(c + 1) * S], ctx_sb[:, c * P:(c + 1) * P], ident[0:S, 0:S])
                i.then_inc(ctxt_p, 1)

            def k2_proj(b):
                pe.wait_ge(ctxt_s, b + 1)
                after(pe, base_s, b)
                project(FF, wk_sb, 0, ctx_t, S).then_inc(k2_p, 1)

            def v2_proj(b):
                for c in range(KC):
                    i = pe.matmul(EE[0:S, 0:D], ctx_t[:, c, :], wv_sb[:, c, :], start=(c == 0), stop=(c == KC - 1))
                i.then_inc(v2_p, 1)

            def z2_turn(b):
                pe.wait_ge(z2_s, b + 1)
                after(pe, x3_s, b)
                turn_tiles(GG, z2).then_inc(z2t_p, 1)

            def q2_proj(b):
                pe.wait_ge(z2t_s, b + 1)
                after(pe, x3t_s, b)
                project(HH, wq_sb, 0, z2_t).then_inc(q2_p, 1)

            def head_scores(b, u):
                j, c, h0 = u // 4, (u // 2) % 2, (u % 2) * QH
                if u == 0:
                    pe.wait_ge(q2t_s, b + 1)
                    pe.wait_ge(kblk_s, b + 1)
                    pe.wait_ge(vpad_s, b + 1)
                if u >= 2:
                    pe.wait_ge(sub_s, UNITS * b + u - 1)
                pe.matmul((EE, FF)[u % 2][:, 0:QH * S], q2_t[:, c, j * P:(j + 1) * P],
                          k_blk[:, c, h0:h0 + QH, :], start=True, stop=True).then_inc(s_p, 1)

            def p_turn(b, u):
                pe.wait_ge(exp_s, UNITS * b + u + 1)
                if u >= 2:
                    pe.wait_ge(pt_s, UNITS * b + u - 1)
                bank = (GG, HH)[u % 2]
                for h in range(QH):
                    i = pe.transpose(bank[0:S, h * P:(h + 1) * P], pr[:, u % PR, h, :], ident[:])
                i.then_inc(pt_p, 1)

            def head_values(b):
                pe.wait_ge(pt_s, UNITS * (b + 1))
                pe.wait_ge(sub_s, UNITS * (b + 1))
                for bank, w, done in ((EE, None, o_p), (FF, pair_ones, den2_p)):
                    for c in range(KC):
                        for e in range(2):
                            for s in range(4):
                                pair = c * 4 + s
                                lhs = v_pad[:, pair, e, :] if w is None else w[:, e, :]
                                i = pe.matmul(half(bank)[s * 32:(s + 1) * 32, c, :], lhs, p_t[:, 2 * pair + e, :],
                                              start=(e == 0), stop=(e == 1), skip_group_check=True)
                    i.then_inc(done, 1)

            def out_proj(b):
                pe.wait_ge(ot_s, b + 1)
                project_rows(GG, o_t, wo_sb, 0).then_inc(y_p, 1)

            def z3_turn(b):
                pe.wait_ge(z3_s, b + 1)
                turn_tiles(HH, z3).then_inc(z3t_p, 1)

            def logits_t(b):
                pe.wait_ge(x3t_s, b + 1)
                for c in range(KC):
                    i = pe.matmul(EE[0:E, 0:T], router_sb[:, c, :], x3n_t[:, c, bass.ds(b * T, T)],
                                  start=(c == 0), stop=(c == KC - 1))
                i.then_inc(lgt_p, 1)

            def logits(b):
                pe.wait_ge(lgt_s, b + 1)
                apart(pe)
                for j in range(TT):
                    i = pe.transpose(FF[:, j * E:(j + 1) * E], lg_t[:, j * P:(j + 1) * P], ident[0:E, 0:E])
                i.then_inc(lg_p, 1)

            def ranks(b):
                pe.wait_ge(pickb_s, b + 1)
                pe.wait_ge(lg_s, b + 1)
                pe.matmul(FF[:, 0:E], before[:], pick_b[:, 0, :], start=True, stop=True)
                pe.matmul(FF[:, E:2 * E], before[:], pick_b[:, 1, :], start=True, stop=False)
                pe.matmul(FF[:, E:2 * E], ones_b[:], pick_b[:, 0, :], start=False, stop=True)
                pe.matmul(FF[:, 2 * E:3 * E], ones_b[:], pick_b[:, 0, :], start=True, stop=False)
                pe.matmul(FF[:, 2 * E:3 * E], ones_b[:], pick_b[:, 1, :], start=False, stop=True).then_inc(rank_p, 1)

            def turn(i, first, last):
                j = i - 1
                if not first:
                    ctx_turn(j)
                if not last:
                    z1_turn(i)
                if not first:
                    k2_proj(j)
                    v2_proj(j)
                    z2_turn(j)
                    q2_proj(j)
                    for u in range(UNITS + 2):
                        if u < UNITS:
                            head_scores(j, u)
                        if u == 1 and not last:
                            gate_proj(i)
                        if u == 3 and not last:
                            q_proj_after_k(i)
                        if u == 6 and not last:
                            v_proj(i)
                        if u >= 2:
                            p_turn(j, u - 2)
                    if not last:
                        scores(i)
                    head_values(j)
                    if not last:
                        values(i)
                    out_proj(j)
                    z3_turn(j)
                    logits_t(j)
                    logits(j)
                    ranks(j)
                else:
                    gate_proj(i)
                    q_proj_after_k(i)
                    v_proj(i)
                    scores(i)
                    values(i)

            def q_proj_after_k(b):
                k_proj(b)
                q_proj(b)

            pe.wait_ge(const, 1)
            pe.wait_ge(w_in, 16 * len(weights))
            turn(0, True, False)
            turn(1, False, False)
            with pe.Fori(2, B) as i:
                turn(i, False, False)
            turn(B, False, True)

            pe.wait_ge(exp_w_in, 16)
            pe.wait_ge(w2_in, 16)
            pe.wait_ge(tab_s, 1)
            pe.wait_ge(base_s, B)
            pe.wait_ge(x3_s, B)

            def tile_turn_x(n, s):
                pe.wait_ge(xe_in[s], (n - s) * 8 + 16)
                after(pe, xet_s, n - 1)
                for c in range(KC):
                    i = pe.transpose((A, BB)[s][:, c * P:(c + 1) * P], xe[:, s, c * P:(c + 1) * P], ident[:])
                i.then_inc(xet_p, 1)

            def tile_up(n, s):
                e = nc.tensor.value_load(tab_e[0:1, bass.ds(n, 1)], min_val=0, max_val=E - 1)
                pe.wait_ge(xet_s, n + 1)
                after(pe, eh_s, n - 1)
                for c in range(KC):
                    i = pe.matmul((C, DD)[s][:], xe_t[:, s, c, :], w13_sb[:, bass.ds(e, 1), c, :].squeeze(1),
                                  start=(c == 0), stop=(c == KC - 1))
                i.then_inc(h_p, 1)

            def tile_turn_h(n, s):
                pe.wait_ge(eh_s, n + 1)
                after(pe, eht_s, n - 1)
                for c in range(KC):
                    i = pe.transpose((EE, FF)[s][:, c * P:(c + 1) * P], eh[:, s, c * P:(c + 1) * P], ident[:])
                i.then_inc(eht_p, 1)

            def tile_down(n, s):
                e = nc.tensor.value_load(tab_e[0:1, bass.ds(n, 1)], min_val=0, max_val=E - 1)
                pe.wait_ge(eht_s, n + 1)
                after(pe, ey_s, n - 1)
                for c in range(KC):
                    i = pe.matmul((GG, HH)[s][:, 0:D], eh_t[:, s, c, :], w2_sb[:, bass.ds(e, 1), c, :].squeeze(1),
                                  start=(c == 0), stop=(c == KC - 1))
                i.then_inc(ey_p, 1)

            def tile_step(n, s, ahead2=True, ahead1=True):
                if ahead2:
                    tile_turn_x(n + 2, s)
                tile_turn_h(n, s)
                if ahead1:
                    tile_up(n + 1, 1 - s)
                tile_down(n, s)

            tile_turn_x(0, 0)
            tile_turn_x(1, 1)
            tile_up(0, 0)
            tile_step(0, 0)
            tile_step(1, 1)
            with pe.Fori(1, EXPERT_TILES // 2 - 1) as m:
                n = 2 * m
                tile_step(n, 0)
                tile_step(n + 1, 1)
            tile_step(EXPERT_TILES - 2, 0, ahead2=False)
            tile_step(EXPERT_TILES - 1, 1, ahead2=False, ahead1=False)

            pe.wait_ge(shared_in, 32)
            pe.wait_ge(xet_s, EXPERT_TILES)
            def shared_up(b):
                after(pe, sh_s, b)
                for bank, w0, done in ((A, 0, a_p), (BB, D, b_p)):
                    for m in range(KC):
                        for c in range(KC):
                            i = pe.matmul(half(bank)[:, m, :], w13s_sb[:, c, w0 + m * P:w0 + (m + 1) * P],
                                          x3n_t[:, c, bass.ds(b * T, T)], start=(c == 0), stop=(c == KC - 1))
                    i.then_inc(done, 1)

            def shared_down(b):
                pe.wait_ge(sh_s, b + 1)
                after(pe, fin_s, b)
                project_rows(C, sh, w2s_sb, 0).then_inc(sy_p, 1)

            shared_up(0)
            shared_down(0)
            with pe.Fori(1, B) as b:
                shared_up(b)
                shared_down(b)

        @block.vector
        def _(dve):
            def moments(b, stats, stats_s, mv, mv_s, readers):
                after(dve, readers, b)
                apart(dve)
                for j in range(TT):
                    i = dve.bn_stats(stats[:, j, :], x_all[:, bass.ds(b * TT + j, 1), :].squeeze(1))
                i.then_inc(stats_s, 1)
                dve.wait_ge(stats_s, b + 1)
                apart(dve)
                for j in range(TT):
                    i = dve.bn_aggr(mv[:, j, :], stats[:, j, :])
                i.then_inc(mv_s, 1)

            def normalise(b, z, mv, rstd, rstd_s, z_s):
                dve.wait_ge(rstd_s, b + 1)
                for j in range(TT):
                    i = dve.tensor_scalar(z[:, j, :], x_all[:, bass.ds(b * TT + j, 1), :].squeeze(1),
                                          mv[:, j, 0:1], rstd[:, j:j + 1], ALU.subtract, ALU.mult)
                i.then_inc(z_s, 1)

            def moments1(b):
                dve.wait_ge(x_in, 16 * (b + 1))
                moments(b, stats1, stats1_s, mv1, mv1_s, z1_s)

            def norm1(b):
                after(dve, z1t_p, b)
                normalise(b, z1, mv1, rstd1, rstd1_s, z1_s)

            def k_gated(b):
                dve.wait_ge(k_p, b + 1)
                dve.wait_ge(gate_s, b + 1)
                after(dve, ek_s, b)
                after(dve, kg1_s, b)
                for c in range(KC):
                    i = dve.scalar_tensor_tensor(out=kg[:, c, :], in0=half(C)[:, c, :], scalar=cols[:, BK, c:c + 1],
                                                 in1=gate[:, c, :], op0=ALU.add, op1=ALU.mult)
                i.then_inc(kg_s, 1)

            def q_elu(b):
                dve.wait_ge(q1_s, b + 1)
                dve.scalar_tensor_tensor(out=q_t[:], in0=eq[:], scalar=1.0, in1=q1[:], op0=ALU.min,
                                         op1=ALU.max).then_inc(qt_s, 1)

            def k_elu(b):
                dve.wait_ge(ek_s, b + 1)
                dve.wait_ge(kg1_s, b + 1)
                dve.scalar_tensor_tensor(out=k_t[:], in0=ek[:], scalar=1.0, in1=kg1[:], op0=ALU.min,
                                         op1=ALU.max).then_inc(kt_s, 1)

            def v_bias(b):
                dve.wait_ge(v_p, b + 1)
                after(dve, av_p, b)
                dve.tensor_tensor(v_ext[:, :, 0:D], half(A),
                                  bv_row[:].rearrange("p (a d) -> p a d", a=1).to_broadcast([P, TT, D]),
                                  ALU.add).then_inc(v_s, 1)

            def mask(b):
                dve.wait_ge(sc_p, b + 1)
                after(dve, av_p, b)
                dve.tensor_tensor(at[:].rearrange("p a n -> p (a n)"), BB[:, 0:3 * P],
                                  causal3[:].rearrange("p a n -> p (a n)"), ALU.mult).then_inc(at_s, 1)

            def residual1(b):
                dve.wait_ge(av_p, b + 1)
                for j, bank in enumerate((C, DD)):
                    i = dve.tensor_scalar(den[:, j:j + 1], bank[:, D:D + 1], DEN_EPS, None, ALU.add)
                i.then_inc(den_s, 1)
                dve.wait_ge(den_s, b + 1)
                dve.reciprocal(rden[:], den[:]).then_inc(rden_s, 1)
                dve.wait_ge(rden_s, b + 1)
                for j, bank in enumerate((C, DD)):
                    xj = x_all[:, bass.ds(b * TT + j, 1), :].squeeze(1)
                    i = dve.scalar_tensor_tensor(out=xj, in0=bank[:, 0:D], scalar=rden[:, j:j + 1], in1=xj,
                                                 op0=ALU.mult, op1=ALU.add)
                i.then_inc(x2_s, 1)

            def moments2(b):
                dve.wait_ge(x2_s, b + 1)
                moments(b, stats2, stats2_s, mv2, mv2_s, z2_s)

            def norm2(b):
                after(dve, z2t_p, b)
                normalise(b, z2, mv2, rstd2, rstd2_s, z2_s)

            def v_place(b):
                dve.wait_ge(v2_p, b + 1)
                after(dve, o_p, b)
                src = EE[0:S, 0:D].rearrange("s (g e d) -> s g e d", e=2, d=HD)
                bias = bv2_row[0:S, :].rearrange("s (g e d) -> s g e d", e=2, d=HD)
                for e in range(2):
                    i = dve.tensor_tensor(v_pad[:, :, e, e * HD:(e + 1) * HD], src[:, :, e, :], bias[:, :, e, :],
                                          ALU.add)
                i.then_inc(vpad_s, 1)

            def soft_shift(b, u):
                bank = (EE, FF)[u % 2][:, 0:QH * S].rearrange("p (h s) -> p h s", h=QH)
                dve.wait_ge(s_p, UNITS * b + u + 1)
                dve.tensor_reduce(mx[:, u % 2, :], bank, AX.X, ALU.max).then_inc(max_s, 1)
                dve.wait_ge(max_s, UNITS * b + u + 1)
                if u < PR:
                    after(dve, den2_p, b)
                else:
                    dve.wait_ge(pt_p, UNITS * b + u + 1 - PR)
                dve.tensor_tensor(pr[:, u % PR], bank,
                                  mx[:, u % 2, :].rearrange("p (h a) -> p h a", a=1).to_broadcast([P, QH, S]),
                                  ALU.subtract).then_inc(sub_s, 1)

            def soft_divide(b):
                dve.wait_ge(den2_p, b + 1)
                after(dve, y_p, b)
                dve.reciprocal(o_t[:], half(FF)).then_inc(rec_s, 1)
                dve.wait_ge(rec_s, b + 1)
                dve.wait_ge(o_p, b + 1)
                dve.tensor_tensor(o_t[:], half(EE), o_t[:], ALU.mult).then_inc(ot_s, 1)

            def residual2(b):
                dve.wait_ge(y_p, b + 1)
                dve.wait_ge(xb_s, b + 1)
                x2 = x_all[:, bass.ds(b * TT, TT), :]
                dve.tensor_tensor(x2, half(GG), x2, ALU.add).then_inc(x3_s, 1)

            def moments3(b):
                dve.wait_ge(x3_s, b + 1)
                moments(b, stats3, stats3_s, mv3, mv3_s, z3_s)

            def norm3(b):
                after(dve, z3t_p, b)
                after(dve, xs_s, b)
                normalise(b, z3, mv3, rstd3, rstd3_s, z3_s)

            def logits_copy(b):
                dve.wait_ge(lgt_p, b + 1)
                after(dve, lg_p, b)
                dve.tensor_copy(lg_t[:], EE[0:E, 0:T]).then_inc(lgt_s, 1)

            def choose(b):
                dve.wait_ge(lg_p, b + 1)
                dve.tensor_copy(lg[:], FF[:, 0:TT * E].rearrange("p (j e) -> p j e", j=TT)).then_inc(lg_s, 1)
                dve.wait_ge(lg_s, b + 1)
                apart(dve)
                for j in range(TT):
                    i = dve.max(top[:, j, :], lg[:, j, :])
                i.then_inc(top_s, 1)
                dve.wait_ge(top_s, b + 1)
                apart(dve)
                for j in range(TT):
                    i = dve.max_index(top_i[:, j, :], top[:, j, :], lg[:, j, :])
                i.then_inc(topi_s, 1)
                after(dve, ediff_s, b)
                dve.tensor_tensor(diff[:, :, 0:E], lg[:], top[:, :, 0:1].to_broadcast([P, TT, E]), ALU.subtract)
                dve.tensor_tensor(diff[:, :, E:E + TOP_K], top[:, :, 0:TOP_K],
                                  top[:, :, 0:1].to_broadcast([P, TT, TOP_K]), ALU.subtract).then_inc(diff_s, 1)
                dve.wait_ge(topi_s, b + 1)
                dve.tensor_copy(top_f[:], top_i[:, :, 0:TOP_K]).then_inc(topf_s, 1)
                dve.wait_ge(topf_s, b + 1)
                for k in range(TOP_K):
                    i = dve.tensor_tensor(pick[:, :, k, :],
                                          iota_e[:].rearrange("p (a e) -> p a e", a=1).to_broadcast([P, TT, E]),
                                          top_f[:, :, k:k + 1].to_broadcast([P, TT, E]), ALU.is_equal)
                i.then_inc(pick_s, 1)
                dve.wait_ge(pick_s, b + 1)
                after(dve, rank_p, b)
                dve.tensor_tensor(pick_b[:], pick[:, :, 0, :], pick[:, :, 1, :], ALU.add).then_inc(pickb_s, 1)

            def score_rows(b):
                dve.wait_ge(ediff_s, b + 1)
                dve.tensor_reduce(esum[:], ediff[:, :, 0:E], AX.X, ALU.add).then_inc(esum_s, 1)
                dve.wait_ge(esum_s, b + 1)
                dve.reciprocal(erec[:], esum[:]).then_inc(erec_s, 1)
                dve.wait_ge(erec_s, b + 1)
                after(dve, xs_s, b)
                dve.tensor_tensor(score[:], ediff[:, :, E:E + TOP_K],
                                  erec[:].rearrange("p (j a) -> p j a", a=1).to_broadcast([P, TT, TOP_K]),
                                  ALU.mult).then_inc(score_s, 1)

            def place(b):
                dve.wait_ge(rank_p, b + 1)
                dve.tensor_tensor(posx[:], FF[:, 0:TT * E].rearrange("p (j e) -> p j e", j=TT),
                                  base[:].rearrange("p (a e) -> p a e", a=1).to_broadcast([P, TT, E]),
                                  ALU.add).then_inc(posx_s, 1)
                dve.wait_ge(posx_s, b + 1)
                dve.tensor_tensor(base[:], FF[:, 2 * E:3 * E], base[:], ALU.add).then_inc(base_s, 1)
                for k in range(TOP_K):
                    i = dve.tensor_tensor(posm[:, :, k, :], pick[:, :, k, :], posx[:], ALU.mult)
                i.then_inc(posm_s, 1)
                dve.wait_ge(posm_s, b + 1)
                pos_b = pos_f[:, bass.ds(b * TT, TT), :]
                dve.tensor_reduce(pos_b, posm[:], AX.X, ALU.add).then_inc(posf_s, 1)
                dve.wait_ge(posf_s, b + 1)
                after(dve, scattered, 16 * TT * TOP_K * b)
                apart(dve)
                dve.tensor_copy(pos_cur[:], pos_b).then_inc(pos_s, 1)

            def turn(i, first, last):
                j = i - 1
                if not first:
                    moments2(j)
                if not last:
                    moments1(i)
                if not first:
                    norm2(j)
                if not last:
                    norm1(i)
                if not first:
                    v_place(j)
                    for u in range(UNITS):
                        soft_shift(j, u)
                        if u == 5 and not last:
                            k_gated(i)
                        if u == 7 and not last:
                            q_elu(i)
                    if not last:
                        v_bias(i)
                        k_elu(i)
                        mask(i)
                    soft_divide(j)
                    if not last:
                        residual1(i)
                    residual2(j)
                    moments3(j)
                    norm3(j)
                    logits_copy(j)
                    choose(j)
                    score_rows(j)
                    place(j)
                else:
                    k_gated(i)
                    q_elu(i)
                    v_bias(i)
                    k_elu(i)
                    mask(i)
                    residual1(i)

            dve.wait_ge(const, 1)
            dve.wait_ge(cols_in, N_COLS)
            dve.tensor_copy(base[:], ebase[:]).then_inc(base0_s, 1)
            dve.wait_ge(base0_s, 1)
            turn(0, True, False)
            turn(1, False, False)
            with dve.Fori(2, B) as i:
                turn(i, False, False)
            turn(B, False, True)

            dve.wait_ge(base_s, B)
            dve.tensor_scalar(pad_i[:], base[:], iota_p[:, 0:1], None, ALU.add).then_inc(padi_s, 1)
            dve.tensor_tensor(cnt[:], base[:], ebase[:], ALU.subtract).then_inc(tab_step, 1)
            dve.wait_ge(tab_step, 1)
            dve.tensor_scalar(tiles_i[:], cnt[:], 1.0 / P, 0.5 - 0.5 / P, ALU.mult, ALU.add).then_inc(tab_step, 1)
            dve.wait_ge(tab_step, 2)
            dve.tensor_copy(tiles[:], tiles_i[:])
            dve.tensor_copy(tile_end[:], tiles_i[:]).then_inc(tab_step, 1)
            dve.wait_ge(tab_step, 3)
            for e in range(1, E):
                dve.tensor_tensor(tile_end[:, e:e + 1], tile_end[:, e:e + 1], tile_end[:, e - 1:e],
                                  ALU.add).then_inc(tab_step, 1)
                dve.wait_ge(tab_step, 3 + e)
            t0 = 2 + E
            dve.tensor_scalar(coef[:], tiles[:], -float(P), float(REGION), ALU.mult, ALU.add).then_inc(tab_step, 1)
            dve.tensor_tensor(past, iota_t[:].rearrange("p (n a) -> p n a", a=1).to_broadcast([1, EXPERT_TILES, E]),
                              tile_end[0:1].rearrange("p (a e) -> p a e", a=1).to_broadcast([1, EXPERT_TILES, E]),
                              ALU.is_ge).then_inc(tab_step, 1)
            dve.wait_ge(tab_step, t0 + 2)
            dve.tensor_tensor(past_c, past,
                              coef[0:1].rearrange("p (a e) -> p a e", a=1).to_broadcast([1, EXPERT_TILES, E]),
                              ALU.mult)
            dve.tensor_reduce(tile_e[:], past, AX.X, ALU.add).then_inc(tab_step, 1)
            dve.wait_ge(tab_step, t0 + 3)
            dve.tensor_reduce(tile_r[:], past_c, AX.X, ALU.add).then_inc(tab_step, 1)
            dve.tensor_scalar(tab_e[:], tile_e[:], float(E - 1), None, ALU.min).then_inc(tab_step, 1)
            dve.wait_ge(tab_step, t0 + 5)
            dve.scalar_tensor_tensor(out=tile_r[:], in0=iota_t[:], scalar=float(P), in1=tile_r[:], op0=ALU.mult,
                                     op1=ALU.add).then_inc(tab_step, 1)
            dve.wait_ge(tab_step, t0 + 6)
            dve.tensor_scalar(tab_r[:], tile_r[:], float(IDLE_ROW), None, ALU.min).then_inc(tab_s, 1)
            n_pos = NT * TOP_K
            pos_flat = pos_f[:].rearrange("p n k -> p (n k)")
            pos_wide = pos_flat.rearrange("p (n a) -> p n a", a=1).to_broadcast([P, n_pos, E - 1])
            dve.tensor_tensor(beyond, pos_wide,
                              ebase[:, 1:E].rearrange("p (a e) -> p a e", a=1).to_broadcast([P, n_pos, E - 1]),
                              ALU.is_ge).then_inc(moved_s, 1)
            dve.wait_ge(moved_s, 1)
            dve.tensor_tensor(beyond_c, beyond,
                              coef[:, 0:E - 1].rearrange("p (a e) -> p a e", a=1).to_broadcast([P, n_pos, E - 1]),
                              ALU.mult).then_inc(moved_s, 1)
            dve.wait_ge(moved_s, 2)
            dve.tensor_reduce(moved, beyond_c, AX.X, ALU.add).then_inc(moved_s, 1)
            dve.wait_ge(moved_s, 3)
            dve.tensor_tensor(pos_all[:].rearrange("p n k -> p (n k)"), pos_flat, moved,
                              ALU.subtract).then_inc(moved_s, 1)

            def tile_silu(n, s):
                bank = (C, DD)[s]
                dve.wait_ge(eth_s, n + 1)
                dve.scalar_tensor_tensor(out=eu[:, s, :], in0=eth[:, s, :], scalar=1.0, in1=bank[:, 0:D], op0=ALU.add,
                                         op1=ALU.mult).then_inc(eu_s, 1)
                dve.wait_ge(eu_s, n + 1)
                after(dve, eht_p, n - 1)
                dve.scalar_tensor_tensor(out=eh[:, s, :], in0=eu[:, s, :], scalar=0.5, in1=bank[:, D:2 * D],
                                         op0=ALU.mult, op1=ALU.mult).then_inc(eh_s, 1)

            def tile_copy_y(n, s):
                dve.wait_ge(ey_p, n + 1)
                after(dve, ey_out, 16 * (n - 1))
                dve.tensor_copy(ey[:, s, :], (GG, HH)[s][:, 0:D]).then_inc(ey_s, 1)

            dve.wait_ge(kt_s, B)
            dve.wait_ge(h_p, 1)
            tile_silu(0, 0)
            def tile_pair(n):
                tile_silu(n + 1, 1)
                tile_copy_y(n, 0)
                tile_silu(n + 2, 0)
                tile_copy_y(n + 1, 1)

            tile_pair(0)
            with dve.Fori(1, EXPERT_TILES // 2 - 1) as m:
                tile_pair(2 * m)
            tile_silu(EXPERT_TILES - 1, 1)
            tile_copy_y(EXPERT_TILES - 2, 0)
            tile_copy_y(EXPERT_TILES - 1, 1)

            def shared_expert(b):
                dve.wait_ge(sth_s, b + 1)
                dve.scalar_tensor_tensor(out=su, in0=sth, scalar=1.0, in1=half(A), op0=ALU.add,
                                         op1=ALU.mult).then_inc(su_s, 1)
                dve.wait_ge(su_s, b + 1)
                dve.wait_ge(b_p, b + 1)
                after(dve, sy_p, b)
                dve.scalar_tensor_tensor(out=sh, in0=su, scalar=0.5, in1=half(BB), op0=ALU.mult,
                                         op1=ALU.mult).then_inc(sh_s, 1)
                dve.wait_ge(sy_p, b + 1)
                dve.wait_ge(sum2_s, b + 1)
                after(dve, fin_out, 16 * b)
                dve.tensor_tensor(fin, half(C), sum2, ALU.add).then_inc(fin_s, 1)

            shared_expert(0)
            with dve.Fori(1, B) as b:
                shared_expert(b)



def kernel(**inputs):
    import numpy as _np
    import concourse.bacc as _bacc
    from concourse import mybir as _mybir
    from concourse.bass_utils import run_bass_kernel_spmd as _run

    def arr(name):
        return _np.ascontiguousarray(inputs[name])

    def turned(name):
        return _np.ascontiguousarray(_np.asarray(inputs[name]).T)

    def beside(a, b):
        return _np.ascontiguousarray(_np.concatenate([_np.asarray(inputs[a]), _np.asarray(inputs[b])], axis=-1))

    args = [
        ("x", arr("x")), ("ctx_mem", arr("ctx_1024")),
        ("w_qkv", arr("L0_attn_qkv_w")), ("b_qkv", arr("L0_attn_qkv_b")),
        ("w_gate", arr("L0_attn_gate_w")), ("b_gate", arr("L0_attn_gate_b")),
        ("ln_g", arr("L0_attn_ln_g")), ("ln_b", arr("L0_attn_ln_b")),
        ("wq_t", turned("L0_xattn_Wq")), ("bq", arr("L0_xattn_bq")),
        ("wk_t", turned("L0_xattn_Wk")), ("bk", arr("L0_xattn_bk")),
        ("wv_t", turned("L0_xattn_Wv")), ("bv", arr("L0_xattn_bv")),
        ("wo_t", turned("L0_xattn_Wo")), ("bo", arr("L0_xattn_bo")),
        ("router_t", turned("L0_ffn_gate_w")),
        ("w13", beside("L0_ffn_w1", "L0_ffn_w3")), ("w2", arr("L0_ffn_w2")),
        ("w13s", beside("L0_ffn_w1s", "L0_ffn_w3s")[0]), ("w2s", arr("L0_ffn_w2s")[0]),
    ]
    nc = _bacc.Bacc("TRN2", target_bir_lowering=False, num_devices=1)
    arrays, aps = {}, []
    for name, a in args:
        arrays[f"in_{name}"] = a
        aps.append(nc.dram_tensor(f"in_{name}", a.shape, _mybir.dt.from_np(a.dtype), kind="ExternalInput").ap())
    shape = inputs["x"].shape
    aps.append(nc.dram_tensor("out_0", shape, _mybir.dt.float32, kind="ExternalOutput").ap())
    decoder_layer_kernel(nc, *aps)
    r = _run(nc, [arrays], core_ids=[0])
    return r.results[0]["out_0"]
```

```python
from contextlib import ExitStack

import concourse.bass as bass
from concourse import mybir

P = 128
ALU = mybir.AluOpType
ACT = mybir.ActivationFunctionType
AX = mybir.AxisListType
F32 = mybir.dt.float32
BF16 = mybir.dt.bfloat16
I32 = mybir.dt.int32
U32 = mybir.dt.uint32

LN_EPS = 1e-5
DEN_EPS = 1e-6
TOP_K = 2


def decoder_layer_kernel(
    nc: bass.Bass,
    x: bass.AP,
    ctx_mem: bass.AP,
    w_qkv: bass.AP,
    b_qkv: bass.AP,
    w_gate: bass.AP,
    b_gate: bass.AP,
    ln_g: bass.AP,
    ln_b: bass.AP,
    wq_t: bass.AP,
    bq: bass.AP,
    wk_t: bass.AP,
    bk: bass.AP,
    wv_t: bass.AP,
    bv: bass.AP,
    wo_t: bass.AP,
    bo: bass.AP,
    router_t: bass.AP,
    w13: bass.AP,
    w2: bass.AP,
    w13s: bass.AP,
    w2s: bass.AP,
    out: bass.AP,
):
    B, T, D = x.shape
    S = ctx_mem.shape[1]
    E = w13.shape[0]
    HEADS = 16
    HD = D // HEADS
    KC = D // P
    TT = T // P
    NT = B * TT
    HC = P // HD
    QH = HC // 2
    UNITS = TT * KC * 2
    SCALE = float(HD) ** -0.5
    REGION = B * T + P
    IDLE_ROW = E * REGION
    EXPERT_TILES = TOP_K * NT + E
    PR = 4

    rows_in = nc.dram_tensor("rows_in", (IDLE_ROW + P, D), F32, kind="Internal").ap()
    rows_out = nc.dram_tensor("rows_out", (EXPERT_TILES * P, D), F32, kind="Internal").ap()

    with ExitStack() as ctx:
        def sb(name, shape, dt=F32):
            return ctx.enter_context(nc.sbuf_tensor(name, shape, dt))

        def sem(name):
            return ctx.enter_context(nc.semaphore(name))

        banks = [ctx.enter_context(nc.psum_tensor(f"bank{i}", [P, 512], F32)) for i in range(8)]
        A, BB, C, DD, EE, FF, GG, HH = banks

        def half(bank):
            return bank[:].rearrange("p (a n) -> p a n", a=2)

        wqkv_sb = sb("wqkv_sb", [P, KC, 3 * D])
        wg_sb = sb("wg_sb", [P, KC, D])
        wq_sb = sb("wq_sb", [P, KC, D])
        wk_sb = sb("wk_sb", [P, KC, D])
        wv_sb = sb("wv_sb", [P, KC, D])
        wo_sb = sb("wo_sb", [P, KC, D])
        router_sb = sb("router_sb", [P, KC, E])
        w13_sb = sb("w13_sb", [P, E, KC, 2 * D])
        cols = sb("cols", [P, 8, KC])
        G_, B_, BQ, BK, BG, BQ2, BK2 = range(7)
        cols2 = sb("cols2", [P, 4, KC])
        bv_row = sb("bv_row", [P, D])
        bv2_row = sb("bv2_row", [P, D])
        bo_row = sb("bo_row", [P, D])
        ident = sb("ident", [P, P])
        causal3 = sb("causal3", [P, 3, P])
        before = sb("before", [P, P], BF16)
        ones_b = sb("ones_b", [P, P], BF16)
        head_mask = sb("head_mask", [P, HC])
        pair_ones = sb("pair_ones", [S, 2, 2 * HD])
        minus_half = sb("minus_half", [P, TT])
        iota_e = sb("iota_e", [P, E])
        zeros = sb("zeros", [P, D])

        x_all = sb("x_all", [P, NT, D])
        x3n_t = sb("x3n_t", [P, KC, B * T])
        pos_f = sb("pos_f", [P, NT, TOP_K])
        pos_all = sb("pos_all", [P, NT, TOP_K], I32)

        stats1 = sb("stats1", [P, TT, 6])
        mv1 = sb("mv1", [P, TT, 2])
        var1 = sb("var1", [P, TT])
        rstd1 = sb("rstd1", [P, TT])
        z1 = sb("z1", [P, TT, D])
        xn_t = sb("xn_t", [P, KC, T])
        th = sb("th", [P, KC, T])
        gate = sb("gate", [P, KC, T])
        kg = sb("kg", [P, KC, T])
        kg1 = sb("kg1", [P, KC, T])
        ek = sb("ek", [P, KC, T])
        eq = sb("eq", [P, KC, T])
        q1 = sb("q1", [P, KC, T])
        q_t, k_t = q1, kg1
        v_ext = sb("v_ext", [P, TT, D + 1])
        at = sb("at", [P, 3, P])
        den = sb("den", [P, TT])
        rden = sb("rden", [P, TT])

        ctx_sb = sb("ctx_sb", [S, D])
        ctx_t = sb("ctx_t", [P, KC, S])
        k2 = sb("k2", [P, KC, S])
        k_blk = sb("k_blk", [P, KC, HC, S])
        v_pad = sb("v_pad", [S, HEADS // 2, 2, 2 * HD])
        stats2 = sb("stats2", [P, TT, 6])
        mv2 = sb("mv2", [P, TT, 2])
        var2 = sb("var2", [P, TT])
        rstd2 = sb("rstd2", [P, TT])
        z2 = sb("z2", [P, TT, D])
        z2_t = sb("z2_t", [P, KC, T])
        q2_t = sb("q2_t", [P, KC, T])
        mx = sb("mx", [P, 2, QH])
        pr = sb("pr", [P, PR, QH, S])
        p_full = sb("p_full", [P, HEADS, T])
        p_t = p_full[0:S]
        assert E * KC * D <= HEADS * T
        w2_sb = p_full[:].rearrange("p h t -> p (h t)")[:, 0:E * KC * D].rearrange("p (e c n) -> p e c n", e=E, c=KC)
        o_t = sb("o_t", [P, KC, T])

        stats3 = sb("stats3", [P, TT, 6])
        mv3 = sb("mv3", [P, TT, 2])
        var3 = sb("var3", [P, TT])
        rstd3 = sb("rstd3", [P, TT])
        z3 = sb("z3", [P, TT, D])
        lg_t = sb("lg_t", [E, T])
        lg = sb("lg", [P, TT, E])
        top = sb("top", [P, TT, 8])
        top_i = sb("top_i", [P, TT, 8], U32)
        top_f = sb("top_f", [P, TT, TOP_K])
        diff = sb("diff", [P, TT, E + TOP_K])
        ediff = sb("ediff", [P, TT, E + TOP_K])
        esum = sb("esum", [P, TT])
        erec = sb("erec", [P, TT])
        score = sb("score", [P, TT, TOP_K])
        pick = sb("pick", [P, TT, TOP_K, E])
        pick_b = sb("pick_b", [P, TT, E], BF16)
        base = sb("base", [P, E])
        posx = sb("posx", [P, TT, E])
        posm = sb("posm", [P, TT, TOP_K, E])
        pos_cur = sb("pos_cur", [P, TT, TOP_K], I32)
        xs = sb("xs", [P, TT, TOP_K, D])
        iota_p = sb("iota_p", [P, 1])
        ebase = sb("ebase", [P, E])
        pad_i = sb("pad_i", [P, E], I32)

        cnt = sb("cnt", [P, E])
        tiles_i = sb("tiles_i", [P, E], I32)
        tiles = sb("tiles", [P, E])
        tile_end = sb("tile_end", [P, E])
        coef = sb("coef", [P, E])
        iota_t = sb("iota_t", [1, EXPERT_TILES])
        tile_e = sb("tile_e", [1, EXPERT_TILES])
        tile_r = sb("tile_r", [1, EXPERT_TILES])
        tab_e = sb("tab_e", [1, EXPERT_TILES], I32)
        tab_r = sb("tab_r", [1, EXPERT_TILES], I32)

        assert EXPERT_TILES * E <= 2 * KC * T and KC * 3 * D <= KC * HC * S
        pr_flat = pr[:].rearrange("p a h s -> p (a h s)")
        past, past_c = (pr_flat[0:1, k * EXPERT_TILES * E:(k + 1) * EXPERT_TILES * E]
                        .rearrange("p (n e) -> p n e", e=E) for k in range(2))
        assert NT * TOP_K * (E - 1) <= KC * T and 2 * EXPERT_TILES * E + NT * TOP_K <= PR * QH * S
        beyond, beyond_c = (t[:].rearrange("p c t -> p (c t)")[:, 0:NT * TOP_K * (E - 1)]
                            .rearrange("p (n e) -> p n e", e=E - 1) for t in (ek, q1))
        moved = pr_flat[:, 2 * EXPERT_TILES * E:2 * EXPERT_TILES * E + NT * TOP_K]

        k_blk_flat = k_blk[:].rearrange("p c h s -> p (c h s)")
        w13s_sb = k_blk_flat[:, 0:KC * 2 * D].rearrange("p (c n) -> p c n", c=KC)
        w2s_sb = k_blk_flat[:, KC * 2 * D:KC * 3 * D].rearrange("p (c n) -> p c n", c=KC)

        xe, xe_t, eth, eu, eh, eh_t, ey = (t[:] for t in (z1, xn_t, th, gate, kg, kg1, ek))
        xe_t = xe_t.rearrange("p s (c t) -> p s c t", c=KC)
        eh_t = eh_t.rearrange("p s (c t) -> p s c t", c=KC)

        sth, su, sh, sum1, sum2, fin = (t[:] for t in (eq, q1, q_t, k_t, z2, z3))
        got = xs[:].rearrange("p j k d -> p (j k) d")
        pos_now = sb("pos_now", [P, TT, TOP_K], I32)

        x_in, ctx_in, w_in, cols_in, exp_w_in = (sem(n) for n in ("x_in", "ctx_in", "w_in", "cols_in", "exp_w_in"))
        cols_ready, const, zeroed = sem("cols_ready"), sem("const"), sem("zeroed")
        stats1_s, mv1_s, var1_s, rstd1_s, z1_s, z1t_p, xnt_s = (
            sem(n) for n in ("stats1_s", "mv1_s", "var1_s", "rstd1_s", "z1_s", "z1t_p", "xnt_s"))
        gate_p, k_p, q_p, v_p, sc_p, av_p = (sem(n) for n in ("gate_p", "k_p", "q_p", "v_p", "sc_p", "av_p"))
        th_s, gate_s, kg_s, kg1_s, ek_s, q1_s, qt_s, kt_s, v_s, at_s, den_s, rden_s, x2_s = (
            sem(n) for n in ("th_s", "gate_s", "kg_s", "kg1_s", "ek_s", "q1_s", "qt_s", "kt_s", "v_s", "at_s", "den_s",
                             "rden_s", "x2_s"))
        ctxt_p, k2_p, v2_p, z2t_p, q2_p, s_p, pt_p, o_p, den2_p, y_p = (
            sem(n) for n in ("ctxt_p", "k2_p", "v2_p", "z2t_p", "q2_p", "s_p", "pt_p", "o_p", "den2_p", "y_p"))
        ctxt_s, k2_s, kblk_s, vpad_s, stats2_s, mv2_s, var2_s, rstd2_s, z2_s, z2t_s, q2t_s = (
            sem(n) for n in ("ctxt_s", "k2_s", "kblk_s", "vpad_s", "stats2_s", "mv2_s", "var2_s", "rstd2_s", "z2_s",
                             "z2t_s", "q2t_s"))
        max_s, sub_s, exp_s, pt_s, rec_s, ot_s, xb_s, x3_s = (
            sem(n) for n in ("max_s", "sub_s", "exp_s", "pt_s", "rec_s", "ot_s", "xb_s", "x3_s"))
        stats3_s, mv3_s, var3_s, rstd3_s, z3_s, z3t_p, x3t_s, lgt_p, lgt_s, lg_p, lg_s = (
            sem(n) for n in ("stats3_s", "mv3_s", "var3_s", "rstd3_s", "z3_s", "z3t_p", "x3t_s", "lgt_p", "lgt_s",
                             "lg_p", "lg_s"))
        top_s, topi_s, topf_s, diff_s, ediff_s, esum_s, erec_s, score_s, pick_s, pickb_s, rank_p = (
            sem(n) for n in ("top_s", "topi_s", "topf_s", "diff_s", "ediff_s", "esum_s", "erec_s", "score_s", "pick_s",
                             "pickb_s", "rank_p"))
        posx_s, base_s, posm_s, posf_s, pos_s, xs_s, scattered = (
            sem(n) for n in ("posx_s", "base_s", "posm_s", "posf_s", "pos_s", "xs_s", "scattered"))
        base0_s, vones_s, padi_s, padded, idle_in, tab_step, tab_s = (
            sem(n) for n in ("base0_s", "vones_s", "padi_s", "padded", "idle_in", "tab_step", "tab_s"))
        moved_s = sem("moved_s")
        shared_in, w2_in = sem("shared_in"), sem("w2_in")
        xe_in = [sem("xe_in0"), sem("xe_in1")]
        xet_p, xet_s, h_p, eth_s, eu_s, eh_s, eht_p, eht_s, ey_p, ey_s, ey_out = (
            sem(n) for n in ("xet_p", "xet_s", "h_p", "eth_s", "eu_s", "eh_s", "eht_p", "eht_s", "ey_p", "ey_s",
                             "ey_out"))
        a_p, b_p, sth_s, su_s, sh_s, sy_p, posn_s, got_s, sum1_s, sum2_s, fin_s, fin_out = (
            sem(n) for n in ("a_p", "b_p", "sth_s", "su_s", "sh_s", "sy_p", "posn_s", "got_s", "sum1_s", "sum2_s",
                             "fin_s", "fin_out"))

        x_v = x.rearrange("b (j p) d -> b p j d", p=P)
        out_v = out.rearrange("b (j p) d -> b p j d", p=P)
        weights = ((wg_sb, w_gate), (wqkv_sb, w_qkv), (wk_sb, wk_t), (wv_sb, wv_t), (wq_sb, wq_t), (wo_sb, wo_t),
                   (router_sb, router_t))
        shared_weights = ((w13s_sb, w13s), (w2s_sb, w2s))
        vectors = (ln_g, ln_b, b_qkv[0:D], b_qkv[D:2 * D], b_gate, bq, bk)
        rows = ((bv_row, b_qkv[2 * D:3 * D]), (bv2_row, bv), (bo_row, bo))
        N_COLS = 16 * (len(vectors) + len(rows))
        N_CONST = 14

        block = ctx.enter_context(nc.Block())

        def after(eng, s, count):
            if not isinstance(count, int) or count > 0:
                eng.wait_ge(s, count)

        def apart(eng):
            eng.nop(nofuse=True)

        @block.sync
        def _(sp):
            sp.dma_start(x_all[:, 0:TT, :], x_v[0]).then_inc(x_in, 16)
            sp.dma_start(ctx_sb[:], ctx_mem[0]).then_inc(ctx_in, 16)
            for dst, src in weights:
                sp.dma_start(dst[:], src.rearrange("(c p) n -> p c n", p=P)).then_inc(w_in, 16)
            with sp.Fori(1, B) as b:
                sp.wait_ge(x_in, 16 * b)
                sp.dma_start(x_all[:, bass.ds(b * TT, TT), :], x_v[bass.ds(b, 1)].squeeze(0)).then_inc(x_in, 16)
                sp.wait_ge(ctxt_p, b)
                sp.dma_start(ctx_sb[:], ctx_mem[bass.ds(b, 1)].squeeze(0)).then_inc(ctx_in, 16)
            sp.wait_ge(o_p, B)
            sp.dma_start(w2_sb, w2.rearrange("e (c p) n -> p e c n", p=P)).then_inc(w2_in, 16)
            sp.wait_ge(s_p, UNITS * B)
            for dst, src in shared_weights:
                sp.dma_start(dst, src.rearrange("(c p) n -> p c n", p=P)).then_inc(shared_in, 16)
            sp.wait_ge(scattered, 16 * B * TT * TOP_K)
            sp.wait_ge(padded, 16 * E)
            sp.wait_ge(idle_in, 16)
            sp.wait_ge(tab_s, 1)

            def load_tile(n, s):
                row = nc.sync.value_load(tab_r[0:1, bass.ds(n, 1)], min_val=0, max_val=IDLE_ROW)
                after(sp, xet_p, n - 1)
                sp.dma_start(xe[:, s, :], rows_in[bass.ds(row, P), :]).then_inc(xe_in[s], 16)

            load_tile(0, 0)
            load_tile(1, 1)
            with sp.Fori(1, EXPERT_TILES // 2) as m:
                load_tile(2 * m, 0)
                load_tile(2 * m + 1, 1)
            with sp.Fori(0, B) as b:
                sp.wait_ge(fin_s, b + 1)
                sp.dma_start(out_v[bass.ds(b, 1)].squeeze(0), fin).then_inc(fin_out, 16)
            sp.wait_ge(fin_out, 16 * B)

        @block.scalar
        def _(act):
            for i, v in enumerate(vectors):
                with nc.allow_non_contiguous_dma(reason="channels onto partitions, once"):
                    act.dma_start(cols[:, i, :], v.rearrange("(c p) -> p c", p=P)).then_inc(cols_in, 16)
            for dst, v in rows:
                act.dma_start(dst[:], v.rearrange("(a d) -> a d", a=1).to_broadcast([P, D])).then_inc(cols_in, 16)
            act.dma_start(w13_sb[:], w13.rearrange("e (c p) n -> p e c n", p=P)).then_inc(exp_w_in, 16)
            act.wait_ge(cols_in, N_COLS)
            act.wait_ge(cols_ready, 4)

            def norm_t(b):
                act.wait_ge(z1t_p, b + 1)
                after(act, v_p, b)
                for c in range(KC):
                    i = act.activation(xn_t[:, c, :], half(A)[:, c, :], ACT.Identity,
                                       bias=cols[:, B_, c:c + 1], scale=cols[:, G_, c:c + 1])
                i.then_inc(xnt_s, 1)

            def gate_tanh(b):
                act.wait_ge(gate_p, b + 1)
                for c in range(KC):
                    i = act.activation(th[:, c, :], half(A)[:, c, :], ACT.Tanh, bias=cols2[:, 1, c:c + 1], scale=0.5)
                i.then_inc(th_s, 1)
                act.wait_ge(th_s, b + 1)
                after(act, kg_s, b)
                act.activation(gate[:], th[:], ACT.Identity, bias=cols2[:, 3, 0:1], scale=0.5).then_inc(gate_s, 1)

            def q_exp(b):
                act.wait_ge(q_p, b + 1)
                after(act, qt_s, b)
                after(act, sc_p, b)
                for c in range(KC):
                    act.activation(eq[:, c, :], half(A)[:, c, :], ACT.Exp, bias=cols[:, BQ, c:c + 1])
                for c in range(KC):
                    i = act.activation(q1[:, c, :], half(A)[:, c, :], ACT.Identity, bias=cols2[:, 0, c:c + 1])
                i.then_inc(q1_s, 1)

            def k_exp(b):
                act.wait_ge(kg_s, b + 1)
                after(act, kt_s, b)
                act.activation(ek[:], kg[:], ACT.Exp).then_inc(ek_s, 1)

            def ctx_copy(b):
                act.wait_ge(ctxt_p, b + 1)
                after(act, v2_p, b)
                act.copy(ctx_t[:].rearrange("p c s -> p (c s)"), A[:, 0:KC * S]).then_inc(ctxt_s, 1)

            def k2_bias(b):
                act.wait_ge(k2_p, b + 1)
                after(act, kblk_s, KC * b)
                for c in range(KC):
                    i = act.activation(k2[:, c, :], half(BB)[:, c, 0:S], ACT.Identity, bias=cols[:, BK2, c:c + 1])
                i.then_inc(k2_s, 1)

            def z2_copy(b):
                act.wait_ge(z2t_p, b + 1)
                after(act, q2_p, b)
                act.copy(z2_t[:], half(BB)).then_inc(z2t_s, 1)

            def q2_scale(b):
                act.wait_ge(q2_p, b + 1)
                after(act, s_p, UNITS * b)
                for c in range(KC):
                    i = act.activation(q2_t[:, c, :], half(DD)[:, c, :], ACT.Identity, bias=cols2[:, 2, c:c + 1],
                                       scale=SCALE)
                i.then_inc(q2t_s, 1)

            def soft_exp(b, u):
                act.wait_ge(sub_s, UNITS * b + u + 1)
                act.activation(pr[:, u % PR], pr[:, u % PR], ACT.Exp).then_inc(exp_s, 1)

            def p_copy(b, u):
                j, h0 = (u // 2) % 2, (u // 4) * HC + (u % 2) * QH
                act.wait_ge(pt_p, UNITS * b + u + 1)
                if u == 0:
                    after(act, o_p, b)
                bank = (GG, HH)[u % 2]
                act.copy(p_t[:, h0:h0 + QH, j * P:(j + 1) * P],
                         bank[0:S, :].rearrange("s (h t) -> s h t", h=QH)).then_inc(pt_s, 1)

            def x3_copy(b):
                act.wait_ge(z3t_p, b + 1)
                act.copy(x3n_t[:, :, bass.ds(b * T, T)], half(C)).then_inc(x3t_s, 1)

            def scale_rows(b):
                act.wait_ge(score_s, b + 1)
                after(act, scattered, 16 * TT * TOP_K * b)
                for j in range(TT):
                    for k in range(TOP_K):
                        i = act.activation(xs[:, j, k, :], z3[:, j, :], ACT.Copy, scale=score[:, j, k:k + 1])
                i.then_inc(xs_s, 1)

            def router_exp(b):
                act.wait_ge(diff_s, b + 1)
                after(act, score_s, b)
                act.activation(ediff[:], diff[:], ACT.Exp).then_inc(ediff_s, 1)

            def turn(i, has1, has2, has3, more1):
                j, l = i - 1, i - 2
                if has1:
                    ctx_copy(i)
                for u in range(UNITS + 1):
                    if has2 and u < UNITS:
                        soft_exp(j, u)
                    if has1 and u == 0:
                        gate_tanh(i)
                    if has1 and u == 1:
                        k2_bias(i)
                    if has1 and u == 3:
                        q_exp(i)
                    if has3 and u == 5:
                        x3_copy(l)
                    if has2 and 1 <= u < UNITS:
                        p_copy(j, u - 1)
                    if has1 and u == 1:
                        k_exp(i)
                    if more1 and u == 6:
                        norm_t(i + 1)
                if has1:
                    z2_copy(i)
                if has3:
                    router_exp(l)
                if has2:
                    p_copy(j, UNITS - 1)
                if has1:
                    q2_scale(i)
                if has3:
                    scale_rows(l)

            norm_t(0)
            for i in range(3):
                turn(i, True, i >= 1, i >= 2, True)
            with act.Fori(3, B - 1) as i:
                turn(i, True, True, True, True)
            turn(B - 1, True, True, True, False)
            turn(B, False, True, True, False)
            turn(B + 1, False, False, True, False)

            def tile_copy_x(n, s):
                act.wait_ge(xet_p, n + 1)
                after(act, h_p, n - 1)
                act.copy(xe_t[:, s], (A, BB)[s][:, 0:D].rearrange("p (c t) -> p c t", c=KC)).then_inc(xet_s, 1)

            def tile_tanh(n, s):
                act.wait_ge(h_p, n + 1)
                after(act, eu_s, n - 1)
                act.activation(eth[:, s, :], (C, DD)[s][:, 0:D], ACT.Tanh, scale=0.5).then_inc(eth_s, 1)

            def tile_copy_h(n, s):
                act.wait_ge(eht_p, n + 1)
                after(act, ey_p, n - 1)
                act.copy(eh_t[:, s], (EE, FF)[s][:, 0:D].rearrange("p (c t) -> p c t", c=KC)).then_inc(eht_s, 1)

            def tile_step(n, s, ahead2=True, ahead1=True):
                if ahead2:
                    tile_copy_x(n + 2, s)
                tile_copy_h(n, s)
                if ahead1:
                    tile_tanh(n + 1, 1 - s)

            tile_copy_x(0, 0)
            tile_copy_x(1, 1)
            tile_tanh(0, 0)
            tile_step(0, 0)
            tile_step(1, 1)
            with act.Fori(1, EXPERT_TILES // 2 - 1) as m:
                n = 2 * m
                tile_step(n, 0)
                tile_step(n + 1, 1)
            tile_step(EXPERT_TILES - 2, 0, ahead2=False)
            tile_step(EXPERT_TILES - 1, 1, ahead2=False, ahead1=False)

            def shared_tanh(b):
                act.wait_ge(a_p, b + 1)
                after(act, su_s, b)
                act.activation(sth, half(A), ACT.Tanh, scale=0.5).then_inc(sth_s, 1)

            shared_tanh(0)
            with act.Fori(1, B) as b:
                shared_tanh(b)

        @block.gpsimd
        def _(pool):
            g = nc.gpsimd
            g.memset(ident[:], 1.0)
            g.memset(causal3[:], 1.0)
            g.memset(before[:], 1.0)
            g.memset(ones_b[:], 1.0)
            g.memset(head_mask[:], 1.0)
            g.memset(pair_ones[:], 0.0)
            g.memset(minus_half[:], -0.5)
            g.memset(v_pad[:], 0.0)
            g.memset(zeros[:], 0.0)
            g.iota(iota_e[:], [[1, E]], base=0, channel_multiplier=0, allow_small_or_imprecise_dtypes=True)
            g.iota(ebase[:], [[REGION, E]], base=0, channel_multiplier=0, allow_small_or_imprecise_dtypes=True)
            g.iota(iota_p[:], [[0, 1]], base=0, channel_multiplier=1, allow_small_or_imprecise_dtypes=True)
            g.iota(iota_t[:], [[1, EXPERT_TILES]], base=0, channel_multiplier=0,
                   allow_small_or_imprecise_dtypes=True)
            g.memset(v_ext[:, :, D:D + 1], 1.0).then_inc(zeroed, 1)
            pool.wait_ge(zeroed, 1)
            g.affine_select(out=ident[:], in_=ident[:], compare_op=ALU.is_equal, fill=0.0, base=0,
                            pattern=[[-1, P]], channel_multiplier=1)
            for d in (0, 2):
                g.affine_select(out=causal3[:, d], in_=causal3[:, d], compare_op=ALU.is_ge, fill=0.0, base=0,
                                pattern=[[1, P]], channel_multiplier=-1)
            g.affine_select(out=before[:], in_=before[:], compare_op=ALU.is_gt, fill=0.0, base=0,
                            pattern=[[1, P]], channel_multiplier=-1)
            for e in range(2):
                g.memset(pair_ones[:, e, e * HD:(e + 1) * HD], 1.0)
            g.affine_select(out=head_mask[:], in_=head_mask[:], compare_op=ALU.is_ge, fill=0.0, base=0,
                            pattern=[[-HD, HC]], channel_multiplier=1).then_inc(zeroed, 1)
            pool.wait_ge(zeroed, 2)
            g.affine_select(out=head_mask[:], in_=head_mask[:], compare_op=ALU.is_ge, fill=0.0, base=HD - 1,
                            pattern=[[HD, HC]], channel_multiplier=-1).then_inc(const, 1)
            pool.wait_ge(const, 1)
            g.dma_start(rows_in[IDLE_ROW:IDLE_ROW + P, :], zeros[:]).then_inc(idle_in, 16)
            pool.wait_ge(cols_in, N_COLS)
            g.memset(cols2[:, 3, :], 0.5).then_inc(cols_ready, 1)
            g.tensor_scalar(cols2[:, 0, :], cols[:, BQ, :], 1.0, None, ALU.add).then_inc(cols_ready, 1)
            g.tensor_scalar(cols2[:, 1, :], cols[:, BG, :], 0.5, None, ALU.mult).then_inc(cols_ready, 1)
            g.tensor_scalar(cols2[:, 2, :], cols[:, BQ2, :], SCALE, None, ALU.mult).then_inc(cols_ready, 1)

            def rstd(b, mv, mv_s, var, var_s, out_, out_s, twice, readers):
                pool.wait_ge(mv_s, b + 1)
                apart(pool)
                scale, offset = (1.0 + LN_EPS, LN_EPS * LN_EPS) if twice else (1.0, LN_EPS)
                g.tensor_scalar(var[:], mv[:, :, 1], scale, offset, ALU.mult, ALU.add).then_inc(var_s, 1)
                pool.wait_ge(var_s, b + 1)
                after(pool, readers, b)
                g.tensor_tensor(out_[:], var[:], minus_half[:], ALU.pow).then_inc(out_s, 1)

            def k_blocks(b, c):
                pool.wait_ge(k2_s, b + 1)
                after(pool, s_p, UNITS * b - UNITS // KC * (KC - 1 - c))
                g.tensor_tensor(k_blk[:, c], k2[:, c:c + 1, :].to_broadcast([P, HC, S]),
                                head_mask[:].rearrange("p (h a) -> p h a", a=1).to_broadcast([P, HC, S]),
                                ALU.mult).then_inc(kblk_s, 1)

            def residual_bias(b):
                pool.wait_ge(x2_s, b + 1)
                pool.wait_ge(z2_s, b + 1)
                x2 = x_all[:, bass.ds(b * TT, TT), :]
                g.tensor_tensor(x2, x2,
                                bo_row[:].rearrange("p (a d) -> p a d", a=1).to_broadcast([P, TT, D]),
                                ALU.add).then_inc(xb_s, 1)

            def scatter(b):
                pool.wait_ge(xs_s, b + 1)
                pool.wait_ge(pos_s, b + 1)
                apart(pool)
                for j in range(TT):
                    for k in range(TOP_K):
                        g.indirect_dma_start(
                            out=rows_in[:], out_offset=bass.IndirectOffsetOnAxis(ap=pos_cur[:, j, k:k + 1], axis=0),
                            in_=xs[:, j, k, :], in_offset=None).then_inc(scattered, 16)

            def turn(i, has1, has2, has3, more1):
                j, l = i - 1, i - 2
                if more1:
                    rstd(i + 1, mv1, mv1_s, var1, var1_s, rstd1, rstd1_s, True, z1_s)
                if has2:
                    residual_bias(j)
                if has3:
                    rstd(l, mv3, mv3_s, var3, var3_s, rstd3, rstd3_s, False, z3_s)
                if has1:
                    k_blocks(i, 0)
                    rstd(i, mv2, mv2_s, var2, var2_s, rstd2, rstd2_s, False, z2_s)
                    k_blocks(i, 1)
                if has3:
                    scatter(l)

            rstd(0, mv1, mv1_s, var1, var1_s, rstd1, rstd1_s, True, z1_s)
            for i in range(3):
                turn(i, True, i >= 1, i >= 2, True)
            with pool.Fori(3, B - 1) as i:
                turn(i, True, True, True, True)
            turn(B - 1, True, True, True, False)
            turn(B, False, True, True, False)
            turn(B + 1, False, False, True, False)

            pool.wait_ge(padi_s, 1)
            for e in range(E):
                g.indirect_dma_start(out=rows_in[:], out_offset=bass.IndirectOffsetOnAxis(ap=pad_i[:, e:e + 1], axis=0),
                                     in_=zeros[:], in_offset=None).then_inc(padded, 16)

            def store_tile(n, s):
                pool.wait_ge(ey_s, n + 1)
                after(pool, ey_out, 16 * n)
                g.dma_start(rows_out[bass.ds(n * P, P), :], ey[:, s, :]).then_inc(ey_out, 16)

            store_tile(0, 0)
            store_tile(1, 1)
            with pool.Fori(1, EXPERT_TILES // 2) as m:
                store_tile(2 * m, 0)
                store_tile(2 * m + 1, 1)

            pool.wait_ge(ey_out, 16 * EXPERT_TILES)
            pool.wait_ge(moved_s, 4)
            def gather(b):
                after(pool, got_s, 16 * TT * TOP_K * b)
                g.tensor_copy(pos_now[:], pos_all[:, bass.ds(b * TT, TT), :]).then_inc(posn_s, 1)
                pool.wait_ge(posn_s, b + 1)
                after(pool, sum1_s, b)
                apart(pool)
                for j in range(TT):
                    for k in range(TOP_K):
                        g.indirect_dma_start(
                            out=got[:, j * TOP_K + k, :], out_offset=None, in_=rows_out[:],
                            in_offset=bass.IndirectOffsetOnAxis(ap=pos_now[:, j, k:k + 1], axis=0),
                        ).then_inc(got_s, 16)
                pool.wait_ge(got_s, 16 * TT * TOP_K * (b + 1))
                g_v = got.rearrange("p (j k) d -> p j k d", k=TOP_K)
                g.tensor_tensor(sum1, g_v[:, :, 0, :], g_v[:, :, 1, :], ALU.add).then_inc(sum1_s, 1)
                pool.wait_ge(sum1_s, b + 1)
                after(pool, fin_s, b)
                g.tensor_tensor(sum2, sum1, x_all[:, bass.ds(b * TT, TT), :], ALU.add).then_inc(sum2_s, 1)

            gather(0)
            with pool.Fori(1, B) as b:
                gather(b)

        @block.tensor
        def _(pe):
            def project(bank, w, c0, src, n=T):
                for m in range(KC):
                    for c in range(KC):
                        i = pe.matmul(half(bank)[:, m, 0:n], w[:, c, c0 + m * P:c0 + (m + 1) * P], src[:, c, 0:n],
                                      start=(c == 0), stop=(c == KC - 1))
                return i

            def project_rows(bank, src, w, c0):
                for j in range(TT):
                    for c in range(KC):
                        i = pe.matmul(half(bank)[:, j, :], src[:, c, j * P:(j + 1) * P], w[:, c, c0:c0 + D],
                                      start=(c == 0), stop=(c == KC - 1))
                return i

            def turn_tiles(bank, src):
                for j in range(TT):
                    for c in range(KC):
                        i = pe.transpose(half(bank)[:, c, j * P:(j + 1) * P], src[:, j, c * P:(c + 1) * P], ident[:])
                return i

            def z1_turn(b):
                pe.wait_ge(z1_s, b + 1)
                after(pe, x2_s, b)
                turn_tiles(A, z1).then_inc(z1t_p, 1)

            def gate_proj(b):
                pe.wait_ge(xnt_s, b + 1)
                pe.wait_ge(ctxt_s, b + 1)
                project(A, wg_sb, 0, xn_t).then_inc(gate_p, 1)

            def k_proj(b):
                if not isinstance(b, int) or b >= 2:
                    pe.wait_ge(rec_s, b - 1)
                elif b == 1:
                    pe.wait_ge(q2t_s, 1)
                project(DD, wqkv_sb, D, xn_t).then_inc(k_p, 1)

            def q_proj(b):
                pe.wait_ge(th_s, b + 1)
                project(A, wqkv_sb, 0, xn_t).then_inc(q_p, 1)

            def v_proj(b):
                pe.wait_ge(k2_s, b + 1)
                project_rows(BB, xn_t, wqkv_sb, 2 * D).then_inc(v_p, 1)

            def scores(b):
                pe.wait_ge(kt_s, b + 1)
                pe.wait_ge(qt_s, b + 1)
                pe.wait_ge(v_s, b + 1)
                for s0, t0, o0 in ((0, 0, 0), (1, 1, 2)):
                    n = T - t0 * P
                    for c in range(KC):
                        i = pe.matmul(BB[:, o0 * P:o0 * P + n], k_t[:, c, s0 * P:(s0 + 1) * P], q_t[:, c, t0 * P:T],
                                      start=(c == 0), stop=(c == KC - 1))
                i.then_inc(sc_p, 1)

            def values(b):
                pe.wait_ge(at_s, b + 1)
                pe.wait_ge(v_s, b + 1)
                pe.wait_ge(kg_s, b + 1)
                pe.wait_ge(q1_s, b + 1)
                pe.matmul(DD[:, 0:D + 1], at[:, 0, :], v_ext[:, 0, :], start=True, stop=True)
                pe.matmul(A[:, 0:D + 1], at[:, 1, :], v_ext[:, 0, :], start=True, stop=False)
                pe.matmul(A[:, 0:D + 1], at[:, 2, :], v_ext[:, 1, :], start=False, stop=True).then_inc(av_p, 1)

            def ctx_turn(b):
                pe.wait_ge(ctx_in, 16 * (b + 1))
                pe.wait_ge(xnt_s, b + 1)
                for c in range(KC):
                    i = pe.transpose(A[:, c * S:(c + 1) * S], ctx_sb[:, c * P:(c + 1) * P], ident[0:S, 0:S])
                i.then_inc(ctxt_p, 1)

            def k2_proj(b):
                pe.wait_ge(ctxt_s, b + 1)
                after(pe, vpad_s, b)
                project(BB, wk_sb, 0, ctx_t, S).then_inc(k2_p, 1)

            def v2_proj(b):
                pe.wait_ge(z2t_s, b + 1)
                for c in range(KC):
                    i = pe.matmul(BB[0:S, 0:D], ctx_t[:, c, :], wv_sb[:, c, :], start=(c == 0), stop=(c == KC - 1))
                i.then_inc(v2_p, 1)

            def z2_turn(b):
                pe.wait_ge(z2_s, b + 1)
                pe.wait_ge(at_s, b + 1)
                turn_tiles(BB, z2).then_inc(z2t_p, 1)

            def q2_proj(b):
                pe.wait_ge(z2t_s, b + 1)
                pe.wait_ge(x2_s, b + 1)
                project(DD, wq_sb, 0, z2_t).then_inc(q2_p, 1)

            def head_scores(b, u):
                c, j, h0 = u // 4, (u // 2) % 2, (u % 2) * QH
                if u == 0:
                    pe.wait_ge(q2t_s, b + 1)
                if u % 4 == 0:
                    pe.wait_ge(kblk_s, KC * b + c + 1)
                after(pe, sub_s, UNITS * b + u - 1)
                pe.matmul((EE, FF)[u % 2][:, 0:QH * S], q2_t[:, c, j * P:(j + 1) * P],
                          k_blk[:, c, h0:h0 + QH, :], start=True, stop=True).then_inc(s_p, 1)

            def p_turn(b, u):
                pe.wait_ge(exp_s, UNITS * b + u + 1)
                after(pe, pt_s, UNITS * b + u - 1)
                bank = (GG, HH)[u % 2]
                for h in range(QH):
                    i = pe.transpose(bank[0:S, h * P:(h + 1) * P], pr[:, u % PR, h, :], ident[:])
                i.then_inc(pt_p, 1)

            def head_values(b):
                pe.wait_ge(vpad_s, b + 1)
                pe.wait_ge(pt_s, UNITS * (b + 1))
                if not isinstance(b, int) or b + 2 <= B:
                    pe.wait_ge(q2t_s, b + 2 if not isinstance(b, int) else min(b + 2, B))
                for bank, w, done in ((DD, pair_ones, den2_p), (C, None, o_p)):
                    if w is None:
                        after(pe, base_s, b)
                    for c in range(KC):
                        for e in range(2):
                            for s in range(4):
                                pair = c * 4 + s
                                lhs = v_pad[:, pair, e, :] if w is None else w[:, e, :]
                                i = pe.matmul(half(bank)[s * 32:(s + 1) * 32, c, :], lhs, p_t[:, 2 * pair + e, :],
                                              start=(e == 0), stop=(e == 1), skip_group_check=True)
                    i.then_inc(done, 1)

            def out_proj(b):
                pe.wait_ge(ot_s, b + 1)
                project_rows(C, o_t, wo_sb, 0).then_inc(y_p, 1)

            def z3_turn(b):
                pe.wait_ge(z3_s, b + 1)
                turn_tiles(C, z3).then_inc(z3t_p, 1)

            def logits_t(b):
                pe.wait_ge(x3t_s, b + 1)
                for c in range(KC):
                    i = pe.matmul(C[0:E, 0:T], router_sb[:, c, :], x3n_t[:, c, bass.ds(b * T, T)],
                                  start=(c == 0), stop=(c == KC - 1))
                i.then_inc(lgt_p, 1)

            def logits(b):
                pe.wait_ge(lgt_s, b + 1)
                apart(pe)
                for j in range(TT):
                    i = pe.transpose(C[:, j * E:(j + 1) * E], lg_t[:, j * P:(j + 1) * P], ident[0:E, 0:E])
                i.then_inc(lg_p, 1)

            def ranks(b):
                pe.wait_ge(pickb_s, b + 1)
                pe.wait_ge(lg_s, b + 1)
                pe.matmul(C[:, 0:E], before[:], pick_b[:, 0, :], start=True, stop=True)
                pe.matmul(C[:, E:2 * E], before[:], pick_b[:, 1, :], start=True, stop=False)
                pe.matmul(C[:, E:2 * E], ones_b[:], pick_b[:, 0, :], start=False, stop=True)
                pe.matmul(C[:, 2 * E:3 * E], ones_b[:], pick_b[:, 0, :], start=True, stop=False)
                pe.matmul(C[:, 2 * E:3 * E], ones_b[:], pick_b[:, 1, :], start=False, stop=True).then_inc(rank_p, 1)

            def turn(i, has1, has2, has3, more1):
                j, l = i - 1, i - 2
                if has2:
                    v2_proj(j)
                if has1:
                    ctx_turn(i)
                if has3:
                    head_values(l)
                for u in range(UNITS + 1):
                    if has2 and u < UNITS:
                        head_scores(j, u)
                    if has1 and u == 0:
                        gate_proj(i)
                    if has1 and u == 1:
                        k2_proj(i)
                    if has3 and u == 5:
                        z3_turn(l)
                    if has1 and u == 3:
                        q_proj(i)
                    if has2 and 1 <= u < UNITS:
                        p_turn(j, u - 1)
                    if has1 and u == 1:
                        k_proj(i)
                    if has3 and u == 2:
                        out_proj(l)
                    if has1 and u == 3:
                        v_proj(i)
                    if has1 and u == 4:
                        scores(i)
                    if has1 and u == 5:
                        values(i)
                    if has3 and u == 6:
                        logits_t(l)
                    if more1 and u == 6:
                        z1_turn(i + 1)
                if has3:
                    logits(l)
                if has1:
                    z2_turn(i)
                if has2:
                    p_turn(j, UNITS - 1)
                if has1:
                    q2_proj(i)
                if has3:
                    ranks(l)

            pe.wait_ge(const, 1)
            pe.wait_ge(w_in, 16 * len(weights))
            z1_turn(0)
            for i in range(3):
                turn(i, True, i >= 1, i >= 2, True)
            with pe.Fori(3, B - 1) as i:
                turn(i, True, True, True, True)
            turn(B - 1, True, True, True, False)
            turn(B, False, True, True, False)
            turn(B + 1, False, False, True, False)

            pe.wait_ge(exp_w_in, 16)
            pe.wait_ge(w2_in, 16)
            pe.wait_ge(tab_s, 1)
            pe.wait_ge(base_s, B)
            pe.wait_ge(x3_s, B)

            def tile_turn_x(n, s):
                pe.wait_ge(xe_in[s], (n - s) * 8 + 16)
                after(pe, xet_s, n - 1)
                for c in range(KC):
                    i = pe.transpose((A, BB)[s][:, c * P:(c + 1) * P], xe[:, s, c * P:(c + 1) * P], ident[:])
                i.then_inc(xet_p, 1)

            def tile_up(n, s):
                e = nc.tensor.value_load(tab_e[0:1, bass.ds(n, 1)], min_val=0, max_val=E - 1)
                pe.wait_ge(xet_s, n + 1)
                after(pe, eh_s, n - 1)
                for c in range(KC):
                    i = pe.matmul((C, DD)[s][:], xe_t[:, s, c, :], w13_sb[:, bass.ds(e, 1), c, :].squeeze(1),
                                  start=(c == 0), stop=(c == KC - 1))
                i.then_inc(h_p, 1)

            def tile_turn_h(n, s):
                pe.wait_ge(eh_s, n + 1)
                after(pe, eht_s, n - 1)
                for c in range(KC):
                    i = pe.transpose((EE, FF)[s][:, c * P:(c + 1) * P], eh[:, s, c * P:(c + 1) * P], ident[:])
                i.then_inc(eht_p, 1)

            def tile_down(n, s):
                e = nc.tensor.value_load(tab_e[0:1, bass.ds(n, 1)], min_val=0, max_val=E - 1)
                pe.wait_ge(eht_s, n + 1)
                after(pe, ey_s, n - 1)
                for c in range(KC):
                    i = pe.matmul((GG, HH)[s][:, 0:D], eh_t[:, s, c, :], w2_sb[:, bass.ds(e, 1), c, :].squeeze(1),
                                  start=(c == 0), stop=(c == KC - 1))
                i.then_inc(ey_p, 1)

            def tile_step(n, s, ahead2=True, ahead1=True):
                if ahead2:
                    tile_turn_x(n + 2, s)
                tile_turn_h(n, s)
                if ahead1:
                    tile_up(n + 1, 1 - s)
                tile_down(n, s)

            tile_turn_x(0, 0)
            tile_turn_x(1, 1)
            tile_up(0, 0)
            tile_step(0, 0)
            tile_step(1, 1)
            with pe.Fori(1, EXPERT_TILES // 2 - 1) as m:
                n = 2 * m
                tile_step(n, 0)
                tile_step(n + 1, 1)
            tile_step(EXPERT_TILES - 2, 0, ahead2=False)
            tile_step(EXPERT_TILES - 1, 1, ahead2=False, ahead1=False)

            pe.wait_ge(shared_in, 32)
            pe.wait_ge(xet_s, EXPERT_TILES)
            def shared_up(b):
                after(pe, sh_s, b)
                for bank, w0, done in ((A, 0, a_p), (BB, D, b_p)):
                    for m in range(KC):
                        for c in range(KC):
                            i = pe.matmul(half(bank)[:, m, :], w13s_sb[:, c, w0 + m * P:w0 + (m + 1) * P],
                                          x3n_t[:, c, bass.ds(b * T, T)], start=(c == 0), stop=(c == KC - 1))
                    i.then_inc(done, 1)

            def shared_down(b):
                pe.wait_ge(sh_s, b + 1)
                after(pe, fin_s, b)
                project_rows(C, sh, w2s_sb, 0).then_inc(sy_p, 1)

            shared_up(0)
            shared_down(0)
            with pe.Fori(1, B) as b:
                shared_up(b)
                shared_down(b)

        @block.vector
        def _(dve):
            def moments(b, stats, stats_s, mv, mv_s, readers):
                after(dve, readers, b)
                apart(dve)
                for j in range(TT):
                    i = dve.bn_stats(stats[:, j, :], x_all[:, bass.ds(b * TT + j, 1), :].squeeze(1))
                i.then_inc(stats_s, 1)
                dve.wait_ge(stats_s, b + 1)
                apart(dve)
                for j in range(TT):
                    i = dve.bn_aggr(mv[:, j, :], stats[:, j, :])
                i.then_inc(mv_s, 1)

            def normalise(b, z, mv, rstd, rstd_s, z_s):
                dve.wait_ge(rstd_s, b + 1)
                for j in range(TT):
                    i = dve.tensor_scalar(z[:, j, :], x_all[:, bass.ds(b * TT + j, 1), :].squeeze(1),
                                          mv[:, j, 0:1], rstd[:, j:j + 1], ALU.subtract, ALU.mult)
                i.then_inc(z_s, 1)

            def moments1(b):
                dve.wait_ge(x_in, 16 * (b + 1))
                moments(b, stats1, stats1_s, mv1, mv1_s, z1_s)

            def norm1(b):
                after(dve, z1t_p, b)
                normalise(b, z1, mv1, rstd1, rstd1_s, z1_s)

            def k_gated(b):
                dve.wait_ge(k_p, b + 1)
                dve.wait_ge(gate_s, b + 1)
                after(dve, ek_s, b)
                for c in range(KC):
                    i = dve.scalar_tensor_tensor(out=kg[:, c, :], in0=half(DD)[:, c, :], scalar=cols[:, BK, c:c + 1],
                                                 in1=gate[:, c, :], op0=ALU.add, op1=ALU.mult)
                i.then_inc(kg_s, 1)

            def k_plus(b):
                dve.wait_ge(kg_s, b + 1)
                after(dve, sc_p, b)
                apart(dve)
                dve.tensor_scalar(kg1[:], kg[:], 1.0, None, ALU.add).then_inc(kg1_s, 1)

            def q_elu(b):
                dve.wait_ge(q1_s, b + 1)
                dve.scalar_tensor_tensor(out=q_t[:], in0=eq[:], scalar=1.0, in1=q1[:], op0=ALU.min,
                                         op1=ALU.max).then_inc(qt_s, 1)

            def k_elu(b):
                dve.wait_ge(ek_s, b + 1)
                dve.wait_ge(kg1_s, b + 1)
                dve.scalar_tensor_tensor(out=k_t[:], in0=ek[:], scalar=1.0, in1=kg1[:], op0=ALU.min,
                                         op1=ALU.max).then_inc(kt_s, 1)

            def v_bias(b):
                dve.wait_ge(v_p, b + 1)
                after(dve, av_p, b)
                dve.tensor_tensor(v_ext[:, :, 0:D], half(BB),
                                  bv_row[:].rearrange("p (a d) -> p a d", a=1).to_broadcast([P, TT, D]),
                                  ALU.add).then_inc(v_s, 1)

            def mask(b):
                dve.wait_ge(sc_p, b + 1)
                after(dve, av_p, b)
                dve.tensor_tensor(at[:].rearrange("p a n -> p (a n)"), BB[:, 0:3 * P],
                                  causal3[:].rearrange("p a n -> p (a n)"), ALU.mult).then_inc(at_s, 1)

            def residual1(b):
                dve.wait_ge(av_p, b + 1)
                for j, bank in enumerate((DD, A)):
                    i = dve.tensor_scalar(den[:, j:j + 1], bank[:, D:D + 1], DEN_EPS, None, ALU.add)
                i.then_inc(den_s, 1)
                dve.wait_ge(den_s, b + 1)
                dve.reciprocal(rden[:], den[:]).then_inc(rden_s, 1)
                dve.wait_ge(rden_s, b + 1)
                for j, bank in enumerate((DD, A)):
                    xj = x_all[:, bass.ds(b * TT + j, 1), :].squeeze(1)
                    i = dve.scalar_tensor_tensor(out=xj, in0=bank[:, 0:D], scalar=rden[:, j:j + 1], in1=xj,
                                                 op0=ALU.mult, op1=ALU.add)
                i.then_inc(x2_s, 1)

            def moments2(b):
                dve.wait_ge(x2_s, b + 1)
                moments(b, stats2, stats2_s, mv2, mv2_s, z2_s)

            def norm2(b):
                after(dve, z2t_p, b)
                normalise(b, z2, mv2, rstd2, rstd2_s, z2_s)

            def v_place(b):
                dve.wait_ge(v2_p, b + 1)
                after(dve, o_p, b)
                src = BB[0:S, 0:D].rearrange("s (g e d) -> s g e d", e=2, d=HD)
                bias = bv2_row[0:S, :].rearrange("s (g e d) -> s g e d", e=2, d=HD)
                for e in range(2):
                    i = dve.tensor_tensor(v_pad[:, :, e, e * HD:(e + 1) * HD], src[:, :, e, :], bias[:, :, e, :],
                                          ALU.add)
                i.then_inc(vpad_s, 1)

            def soft_shift(b, u):
                bank = (EE, FF)[u % 2][:, 0:QH * S].rearrange("p (h s) -> p h s", h=QH)
                dve.wait_ge(s_p, UNITS * b + u + 1)
                dve.tensor_reduce(mx[:, u % 2, :], bank, AX.X, ALU.max).then_inc(max_s, 1)
                dve.wait_ge(max_s, UNITS * b + u + 1)
                after(dve, pt_p, UNITS * b + u + 1 - PR)
                dve.tensor_tensor(pr[:, u % PR], bank,
                                  mx[:, u % 2, :].rearrange("p (h a) -> p h a", a=1).to_broadcast([P, QH, S]),
                                  ALU.subtract).then_inc(sub_s, 1)

            def soft_divide(b):
                dve.wait_ge(den2_p, b + 1)
                after(dve, y_p, b)
                dve.reciprocal(o_t[:], half(DD)).then_inc(rec_s, 1)
                dve.wait_ge(rec_s, b + 1)
                dve.wait_ge(o_p, b + 1)
                dve.tensor_tensor(o_t[:], half(C), o_t[:], ALU.mult).then_inc(ot_s, 1)

            def residual2(b):
                dve.wait_ge(y_p, b + 1)
                dve.wait_ge(xb_s, b + 1)
                x2 = x_all[:, bass.ds(b * TT, TT), :]
                dve.tensor_tensor(x2, half(C), x2, ALU.add).then_inc(x3_s, 1)

            def moments3(b):
                dve.wait_ge(x3_s, b + 1)
                moments(b, stats3, stats3_s, mv3, mv3_s, z3_s)

            def norm3(b):
                after(dve, z3t_p, b)
                after(dve, xs_s, b)
                normalise(b, z3, mv3, rstd3, rstd3_s, z3_s)

            def logits_copy(b):
                dve.wait_ge(lgt_p, b + 1)
                after(dve, lg_p, b)
                dve.tensor_copy(lg_t[:], C[0:E, 0:T]).then_inc(lgt_s, 1)

            def choose(b):
                dve.wait_ge(lg_p, b + 1)
                dve.tensor_copy(lg[:], C[:, 0:TT * E].rearrange("p (j e) -> p j e", j=TT)).then_inc(lg_s, 1)
                dve.wait_ge(lg_s, b + 1)
                apart(dve)
                for j in range(TT):
                    i = dve.max(top[:, j, :], lg[:, j, :])
                i.then_inc(top_s, 1)
                dve.wait_ge(top_s, b + 1)
                apart(dve)
                for j in range(TT):
                    i = dve.max_index(top_i[:, j, :], top[:, j, :], lg[:, j, :])
                i.then_inc(topi_s, 1)
                after(dve, ediff_s, b)
                dve.tensor_tensor(diff[:, :, 0:E], lg[:], top[:, :, 0:1].to_broadcast([P, TT, E]), ALU.subtract)
                dve.tensor_tensor(diff[:, :, E:E + TOP_K], top[:, :, 0:TOP_K],
                                  top[:, :, 0:1].to_broadcast([P, TT, TOP_K]), ALU.subtract).then_inc(diff_s, 1)
                dve.wait_ge(topi_s, b + 1)
                dve.tensor_copy(top_f[:], top_i[:, :, 0:TOP_K]).then_inc(topf_s, 1)
                dve.wait_ge(topf_s, b + 1)
                for k in range(TOP_K):
                    i = dve.tensor_tensor(pick[:, :, k, :],
                                          iota_e[:].rearrange("p (a e) -> p a e", a=1).to_broadcast([P, TT, E]),
                                          top_f[:, :, k:k + 1].to_broadcast([P, TT, E]), ALU.is_equal)
                i.then_inc(pick_s, 1)
                dve.wait_ge(pick_s, b + 1)
                after(dve, rank_p, b)
                dve.tensor_tensor(pick_b[:], pick[:, :, 0, :], pick[:, :, 1, :], ALU.add).then_inc(pickb_s, 1)

            def score_rows(b):
                dve.wait_ge(ediff_s, b + 1)
                dve.tensor_reduce(esum[:], ediff[:, :, 0:E], AX.X, ALU.add).then_inc(esum_s, 1)
                dve.wait_ge(esum_s, b + 1)
                dve.reciprocal(erec[:], esum[:]).then_inc(erec_s, 1)
                dve.wait_ge(erec_s, b + 1)
                after(dve, xs_s, b)
                dve.tensor_tensor(score[:], ediff[:, :, E:E + TOP_K],
                                  erec[:].rearrange("p (j a) -> p j a", a=1).to_broadcast([P, TT, TOP_K]),
                                  ALU.mult).then_inc(score_s, 1)

            def place(b):
                dve.wait_ge(rank_p, b + 1)
                dve.tensor_tensor(posx[:], C[:, 0:TT * E].rearrange("p (j e) -> p j e", j=TT),
                                  base[:].rearrange("p (a e) -> p a e", a=1).to_broadcast([P, TT, E]),
                                  ALU.add).then_inc(posx_s, 1)
                dve.wait_ge(posx_s, b + 1)
                dve.tensor_tensor(base[:], C[:, 2 * E:3 * E], base[:], ALU.add).then_inc(base_s, 1)
                for k in range(TOP_K):
                    i = dve.tensor_tensor(posm[:, :, k, :], pick[:, :, k, :], posx[:], ALU.mult)
                i.then_inc(posm_s, 1)
                dve.wait_ge(posm_s, b + 1)
                pos_b = pos_f[:, bass.ds(b * TT, TT), :]
                dve.tensor_reduce(pos_b, posm[:], AX.X, ALU.add).then_inc(posf_s, 1)
                dve.wait_ge(posf_s, b + 1)
                after(dve, scattered, 16 * TT * TOP_K * b)
                apart(dve)
                dve.tensor_copy(pos_cur[:], pos_b).then_inc(pos_s, 1)

            def turn(i, has1, has2, has3, more1):
                j, l = i - 1, i - 2
                if has3:
                    soft_divide(l)
                if has2:
                    v_place(j)
                for u in range(UNITS):
                    if has2:
                        soft_shift(j, u)
                    if more1 and u == 0:
                        moments1(i + 1)
                    if has1 and u == 1:
                        k_gated(i)
                        k_plus(i)
                    if has3 and u == 2:
                        residual2(l)
                        moments3(l)
                    if u == 3:
                        if more1:
                            norm1(i + 1)
                        if has1:
                            q_elu(i)
                            k_elu(i)
                        if has3:
                            norm3(l)
                        if has1:
                            v_bias(i)
                    if has1 and u == 4:
                        mask(i)
                    if has1 and u == 5:
                        residual1(i)
                        moments2(i)
                    if has3 and u == 6:
                        logits_copy(l)
                    if has1 and u == 6:
                        norm2(i)
                if has3:
                    choose(l)
                    score_rows(l)
                    place(l)

            dve.wait_ge(const, 1)
            dve.wait_ge(cols_in, N_COLS)
            dve.tensor_copy(base[:], ebase[:]).then_inc(base0_s, 1)
            dve.wait_ge(base0_s, 1)
            moments1(0)
            norm1(0)
            for i in range(3):
                turn(i, True, i >= 1, i >= 2, True)
            with dve.Fori(3, B - 1) as i:
                turn(i, True, True, True, True)
            turn(B - 1, True, True, True, False)
            turn(B, False, True, True, False)
            turn(B + 1, False, False, True, False)

            dve.wait_ge(base_s, B)
            dve.tensor_scalar(pad_i[:], base[:], iota_p[:, 0:1], None, ALU.add).then_inc(padi_s, 1)
            dve.tensor_tensor(cnt[:], base[:], ebase[:], ALU.subtract).then_inc(tab_step, 1)
            dve.wait_ge(tab_step, 1)
            dve.tensor_scalar(tiles_i[:], cnt[:], 1.0 / P, 0.5 - 0.5 / P, ALU.mult, ALU.add).then_inc(tab_step, 1)
            dve.wait_ge(tab_step, 2)
            dve.tensor_copy(tiles[:], tiles_i[:])
            dve.tensor_copy(tile_end[:], tiles_i[:]).then_inc(tab_step, 1)
            dve.wait_ge(tab_step, 3)
            for e in range(1, E):
                dve.tensor_tensor(tile_end[:, e:e + 1], tile_end[:, e:e + 1], tile_end[:, e - 1:e],
                                  ALU.add).then_inc(tab_step, 1)
                dve.wait_ge(tab_step, 3 + e)
            t0 = 2 + E
            dve.tensor_scalar(coef[:], tiles[:], -float(P), float(REGION), ALU.mult, ALU.add).then_inc(tab_step, 1)
            dve.tensor_tensor(past, iota_t[:].rearrange("p (n a) -> p n a", a=1).to_broadcast([1, EXPERT_TILES, E]),
                              tile_end[0:1].rearrange("p (a e) -> p a e", a=1).to_broadcast([1, EXPERT_TILES, E]),
                              ALU.is_ge).then_inc(tab_step, 1)
            dve.wait_ge(tab_step, t0 + 2)
            dve.tensor_tensor(past_c, past,
                              coef[0:1].rearrange("p (a e) -> p a e", a=1).to_broadcast([1, EXPERT_TILES, E]),
                              ALU.mult)
            dve.tensor_reduce(tile_e[:], past, AX.X, ALU.add).then_inc(tab_step, 1)
            dve.wait_ge(tab_step, t0 + 3)
            dve.tensor_reduce(tile_r[:], past_c, AX.X, ALU.add).then_inc(tab_step, 1)
            dve.tensor_scalar(tab_e[:], tile_e[:], float(E - 1), None, ALU.min).then_inc(tab_step, 1)
            dve.wait_ge(tab_step, t0 + 5)
            dve.scalar_tensor_tensor(out=tile_r[:], in0=iota_t[:], scalar=float(P), in1=tile_r[:], op0=ALU.mult,
                                     op1=ALU.add).then_inc(tab_step, 1)
            dve.wait_ge(tab_step, t0 + 6)
            dve.tensor_scalar(tab_r[:], tile_r[:], float(IDLE_ROW), None, ALU.min).then_inc(tab_s, 1)
            n_pos = NT * TOP_K
            pos_flat = pos_f[:].rearrange("p n k -> p (n k)")
            pos_wide = pos_flat.rearrange("p (n a) -> p n a", a=1).to_broadcast([P, n_pos, E - 1])
            dve.tensor_tensor(beyond, pos_wide,
                              ebase[:, 1:E].rearrange("p (a e) -> p a e", a=1).to_broadcast([P, n_pos, E - 1]),
                              ALU.is_ge).then_inc(moved_s, 1)
            dve.wait_ge(moved_s, 1)
            dve.tensor_tensor(beyond_c, beyond,
                              coef[:, 0:E - 1].rearrange("p (a e) -> p a e", a=1).to_broadcast([P, n_pos, E - 1]),
                              ALU.mult).then_inc(moved_s, 1)
            dve.wait_ge(moved_s, 2)
            dve.tensor_reduce(moved, beyond_c, AX.X, ALU.add).then_inc(moved_s, 1)
            dve.wait_ge(moved_s, 3)
            dve.tensor_tensor(pos_all[:].rearrange("p n k -> p (n k)"), pos_flat, moved,
                              ALU.subtract).then_inc(moved_s, 1)

            def tile_silu(n, s):
                bank = (C, DD)[s]
                dve.wait_ge(eth_s, n + 1)
                dve.scalar_tensor_tensor(out=eu[:, s, :], in0=eth[:, s, :], scalar=1.0, in1=bank[:, 0:D], op0=ALU.add,
                                         op1=ALU.mult).then_inc(eu_s, 1)
                dve.wait_ge(eu_s, n + 1)
                after(dve, eht_p, n - 1)
                dve.scalar_tensor_tensor(out=eh[:, s, :], in0=eu[:, s, :], scalar=0.5, in1=bank[:, D:2 * D],
                                         op0=ALU.mult, op1=ALU.mult).then_inc(eh_s, 1)

            def tile_copy_y(n, s):
                dve.wait_ge(ey_p, n + 1)
                after(dve, ey_out, 16 * (n - 1))
                dve.tensor_copy(ey[:, s, :], (GG, HH)[s][:, 0:D]).then_inc(ey_s, 1)

            dve.wait_ge(kt_s, B)
            dve.wait_ge(h_p, 1)
            tile_silu(0, 0)
            def tile_pair(n):
                tile_silu(n + 1, 1)
                tile_copy_y(n, 0)
                tile_silu(n + 2, 0)
                tile_copy_y(n + 1, 1)

            tile_pair(0)
            with dve.Fori(1, EXPERT_TILES // 2 - 1) as m:
                tile_pair(2 * m)
            tile_silu(EXPERT_TILES - 1, 1)
            tile_copy_y(EXPERT_TILES - 2, 0)
            tile_copy_y(EXPERT_TILES - 1, 1)

            def shared_expert(b):
                dve.wait_ge(sth_s, b + 1)
                dve.scalar_tensor_tensor(out=su, in0=sth, scalar=1.0, in1=half(A), op0=ALU.add,
                                         op1=ALU.mult).then_inc(su_s, 1)
                dve.wait_ge(su_s, b + 1)
                dve.wait_ge(b_p, b + 1)
                after(dve, sy_p, b)
                dve.scalar_tensor_tensor(out=sh, in0=su, scalar=0.5, in1=half(BB), op0=ALU.mult,
                                         op1=ALU.mult).then_inc(sh_s, 1)
                dve.wait_ge(sy_p, b + 1)
                dve.wait_ge(sum2_s, b + 1)
                after(dve, fin_out, 16 * b)
                dve.tensor_tensor(fin, half(C), sum2, ALU.add).then_inc(fin_s, 1)

            shared_expert(0)
            with dve.Fori(1, B) as b:
                shared_expert(b)



def kernel(**inputs):
    import numpy as _np
    import concourse.bacc as _bacc
    from concourse import mybir as _mybir
    from concourse.bass_utils import run_bass_kernel_spmd as _run

    def arr(name):
        return _np.ascontiguousarray(inputs[name])

    def turned(name):
        return _np.ascontiguousarray(_np.asarray(inputs[name]).T)

    def beside(a, b):
        return _np.ascontiguousarray(_np.concatenate([_np.asarray(inputs[a]), _np.asarray(inputs[b])], axis=-1))

    args = [
        ("x", arr("x")), ("ctx_mem", arr("ctx_1024")),
        ("w_qkv", arr("L0_attn_qkv_w")), ("b_qkv", arr("L0_attn_qkv_b")),
        ("w_gate", arr("L0_attn_gate_w")), ("b_gate", arr("L0_attn_gate_b")),
        ("ln_g", arr("L0_attn_ln_g")), ("ln_b", arr("L0_attn_ln_b")),
        ("wq_t", turned("L0_xattn_Wq")), ("bq", arr("L0_xattn_bq")),
        ("wk_t", turned("L0_xattn_Wk")), ("bk", arr("L0_xattn_bk")),
        ("wv_t", turned("L0_xattn_Wv")), ("bv", arr("L0_xattn_bv")),
        ("wo_t", turned("L0_xattn_Wo")), ("bo", arr("L0_xattn_bo")),
        ("router_t", turned("L0_ffn_gate_w")),
        ("w13", beside("L0_ffn_w1", "L0_ffn_w3")), ("w2", arr("L0_ffn_w2")),
        ("w13s", beside("L0_ffn_w1s", "L0_ffn_w3s")[0]), ("w2s", arr("L0_ffn_w2s")[0]),
    ]
    nc = _bacc.Bacc("TRN2", target_bir_lowering=False, num_devices=1)
    arrays, aps = {}, []
    for name, a in args:
        arrays[f"in_{name}"] = a
        aps.append(nc.dram_tensor(f"in_{name}", a.shape, _mybir.dt.from_np(a.dtype), kind="ExternalInput").ap())
    shape = inputs["x"].shape
    aps.append(nc.dram_tensor("out_0", shape, _mybir.dt.float32, kind="ExternalOutput").ap())
    decoder_layer_kernel(nc, *aps)
    r = _run(nc, [arrays], core_ids=[0])
    return r.results[0]["out_0"]
```

```python
from contextlib import ExitStack

import concourse.bass as bass
import numpy as np
from concourse import mybir

P = 128
ALU = mybir.AluOpType
ACT = mybir.ActivationFunctionType
AX = mybir.AxisListType
F32 = mybir.dt.float32
F32R = mybir.dt.float32r
BF16 = mybir.dt.bfloat16
I32 = mybir.dt.int32
U32 = mybir.dt.uint32

LN_EPS = 1e-5
DEN_EPS = 1e-6
TOP_K = 2


def decoder_layer_kernel(
    nc: bass.Bass,
    x: bass.AP,
    ctx_mem: bass.AP,
    w_qkv: bass.AP,
    b_qkv: bass.AP,
    w_gate: bass.AP,
    b_gate: bass.AP,
    ln_g: bass.AP,
    ln_b: bass.AP,
    wq_t: bass.AP,
    bq: bass.AP,
    wk_t: bass.AP,
    bk: bass.AP,
    wv_t: bass.AP,
    bv: bass.AP,
    wo_t: bass.AP,
    bo: bass.AP,
    router_t: bass.AP,
    w13: bass.AP,
    w2: bass.AP,
    w13s: bass.AP,
    w2s: bass.AP,
    out: bass.AP,
):
    B, T, D = x.shape
    S = ctx_mem.shape[1]
    E = w13.shape[0]
    HEADS = 16
    HD = D // HEADS
    KC = D // P
    TT = T // P
    NT = B * TT
    HC = P // HD
    QH = HC // 2
    UNITS = TT * KC * 2
    SCALE = float(HD) ** -0.5
    REGION = B * T + P
    IDLE_ROW = E * REGION
    ROW = D + 1
    RESULTS = B * T * TOP_K
    EXPERT_TILES = TOP_K * NT + E
    PR = 4

    rows_in = nc.dram_tensor("rows_in", (IDLE_ROW + P, ROW), F32, kind="Internal").ap()
    rows_out = nc.dram_tensor("rows_out", (RESULTS, D), F32, kind="Internal").ap()

    with ExitStack() as ctx:
        def sb(name, shape, dt=F32):
            return ctx.enter_context(nc.sbuf_tensor(name, shape, dt))

        def sem(name):
            return ctx.enter_context(nc.semaphore(name))

        banks = [ctx.enter_context(nc.psum_tensor(f"bank{i}", [P, 512], F32)) for i in range(8)]
        A, BB, C, DD, EE, FF, GG, HH = banks

        def half(bank):
            return bank[:].rearrange("p (a n) -> p a n", a=2)

        router_sb = sb("router_sb", [P, KC, E])
        w2s_sb = sb("w2s_sb", [P, KC, D])
        cols = sb("cols", [P, 8, KC])
        G_, B_, BQ, BK, BG, BQ2, BK2 = range(7)
        cols2 = sb("cols2", [P, 4, KC])
        bv_row = sb("bv_row", [P, D])
        bv2_row = sb("bv2_row", [P, D])
        bo_row = sb("bo_row", [P, D])
        ident = sb("ident", [P, P])
        causal3 = sb("causal3", [P, 3, P])
        before = sb("before", [P, P], BF16)
        ones_b = sb("ones_b", [P, P], BF16)
        head_mask = sb("head_mask", [P, HC])
        pair_ones = sb("pair_ones", [S, 2, 2 * HD])
        minus_half = sb("minus_half", [P, TT])
        iota_e = sb("iota_e", [P, E])
        pad_rows = sb("pad_rows", [P, ROW])

        x_all = sb("x_all", [P, NT, D])

        spare = sb("spare", [P, 2 * KC * T + TT * (D + 1)])
        stats1 = sb("stats1", [P, TT, 6])
        mv1 = sb("mv1", [P, TT, 2])
        var1 = sb("var1", [P, TT])
        rstd1 = sb("rstd1", [P, TT])
        th = sb("th", [P, KC, T])
        gate = sb("gate", [P, KC, T])
        kg = sb("kg", [P, KC, T])
        ek = sb("ek", [P, KC, T])
        eq = spare[:, 0:KC * T].rearrange("p (c t) -> p c t", c=KC)
        q1 = spare[:, KC * T:2 * KC * T].rearrange("p (c t) -> p c t", c=KC)
        v_ext = spare[:, 2 * KC * T:].rearrange("p (j d) -> p j d", j=TT)
        at = sb("at", [P, 3, P])
        den = sb("den", [P, TT])
        rden = sb("rden", [P, TT])

        ctx_sb = sb("ctx_sb", [S, D])
        ctx_t = sb("ctx_t", [P, KC, S])
        k2 = sb("k2", [P, KC, S])
        stats2 = sb("stats2", [P, TT, 6])
        mv2 = sb("mv2", [P, TT, 2])
        var2 = sb("var2", [P, TT])
        rstd2 = sb("rstd2", [P, TT])
        z2_t = sb("z2_t", [P, KC, T])
        q2_t = sb("q2_t", [P, KC, T])
        mx = sb("mx", [P, 2, QH])
        o_t = sb("o_t", [P, KC, T])

        stats3 = sb("stats3", [P, TT, 6])
        mv3 = sb("mv3", [P, TT, 2])
        var3 = sb("var3", [P, TT])
        rstd3 = sb("rstd3", [P, TT])
        z3 = sb("z3", [P, TT, D])
        vec_rows = z3[0:8, 0, :]
        lg_t = sb("lg_t", [E, T])
        lg = sb("lg", [P, TT, E])
        top = sb("top", [P, TT, 8])
        top_i = sb("top_i", [P, TT, 8], U32)
        top_f = sb("top_f", [P, TT, TOP_K])
        diff = sb("diff", [P, TT, E + TOP_K])
        ediff = sb("ediff", [P, TT, E + TOP_K])
        esum = sb("esum", [P, TT])
        erec = sb("erec", [P, TT])
        score = sb("score", [P, TT, TOP_K])
        pick = sb("pick", [P, TT, TOP_K, E])
        pick_b = sb("pick_b", [P, TT, E], BF16)
        base = sb("base", [P, E])
        posx = sb("posx", [P, TT, E])
        posm = sb("posm", [P, TT, TOP_K, E])
        pos_f = sb("pos_f", [P, TT, TOP_K])
        pos_cur = sb("pos_cur", [P, TT, TOP_K], I32)
        xs = sb("xs", [P, TT, TOP_K, ROW])
        dest = sb("dest", [P, TT, TOP_K])
        x3n_t = sb("x3n_t", [P, KC, T])

        sth = sb("sth", [P, KC, T])
        sh = sth
        ebase = sb("ebase", [P, E])
        pad_i = sb("pad_i", [1, E], I32)

        w13s_lo = sb("w13s_lo", [P, KC, 2 * D], F32R)
        self_lo = sb("self_lo", [P, KC * 4 * D], F32R)
        xn_hi = sb("xn_hi", [P, KC, T], F32R)
        xn_lo = sb("xn_lo", [P, KC, T], F32R)

        attention = ExitStack()

        def old(name, shape):
            return attention.enter_context(nc.sbuf_tensor(name, shape, F32))

        w13_sb = old("w13_sb", [P, E, KC, 2 * D])
        w2_sb = old("w2_sb", [P, E, KC, D])
        low_room = old("low_room", [P, 7 * KC * D + (PR * QH + KC * HC) * S + KC * D + HEADS * 2 * HD])
        room_used = 0

        def piece(*shape):
            nonlocal room_used
            n = int(np.prod(shape))
            names = "abcd"[:len(shape)]
            view = low_room[:, room_used:room_used + n].rearrange(
                f"p ({' '.join(names)}) -> p {' '.join(names)}", **dict(zip(names, shape)))
            room_used += n
            return view

        room_first = (KC * 3 * D, KC * D)
        wqkv_sb = piece(KC, 3 * D)
        wg_sb, wq_sb, wk_sb, wv_sb = (piece(KC, D) for _ in range(4))
        free_1 = room_used
        pr = piece(PR, QH, S)
        k_blk = piece(KC, HC, S)
        free_2 = room_used
        wo_sb = piece(KC, D)
        v_pad = piece(HEADS // 2, 2, 2 * HD)[0:S]
        p_full = old("p_full", [P, HEADS, T])
        p_t = p_full[0:S]
        xn_t = old("xn_t", [P, KC, T])
        kg1 = old("kg1", [P, KC, T])
        z1 = old("z1", [P, TT, D])
        z2 = old("z2", [P, TT, D])
        w13s_sb = old("w13s_sb", [P, KC, 2 * D])
        q_t, k_t = q1, kg1
        attention.close()

        high = ExitStack()
        for name, t in (("w13_hi", w13_sb), ("w2_hi", w2_sb)):
            high.enter_context(nc.sbuf_tensor(name + "_place2", list(t.shape), F32))
        self_hi = high.enter_context(nc.sbuf_tensor("self_hi", [P, KC * 4 * D], F32R))
        high.close()
        assert room_first == (KC * 3 * D, KC * D)
        wqkv_hi, wqkv_lo = (t[:, 0:KC * 3 * D].rearrange("p (c n) -> p c n", c=KC) for t in (self_hi, self_lo))
        wg_hi, wg_lo = (t[:, KC * 3 * D:].rearrange("p (c n) -> p c n", c=KC) for t in (self_hi, self_lo))

        raw = ExitStack()
        for name, t in (("w13_hi", w13_sb), ("w2_hi", w2_sb)):
            raw.enter_context(nc.sbuf_tensor(name + "_place", list(t.shape), F32))
        w13_raw = raw.enter_context(nc.sbuf_tensor("w13_raw", [P, E, KC, 2 * D], F32))
        raw.enter_context(nc.sbuf_tensor("room_rest", [P, low_room.shape[1] - E * KC * 2 * D], F32))
        w2_raw = raw.enter_context(nc.sbuf_tensor("w2_raw", [P, E, KC, D], F32))
        raw.close()

        w13_hi = sb("w13_hi", [P, E, KC, 2 * D], F32R)
        w2_hi = sb("w2_hi", [P, E, KC, D], F32R)
        w13_lo = sb("w13_lo", [P, E, KC, 2 * D], F32R)
        sb("room_rest_lo", [P, low_room.shape[1] - E * KC * 2 * D])
        w2_lo = sb("w2_lo", [P, E, KC, D], F32R)
        xe_hi, eh_hi, xe_lo, eh_lo = (sb(n, [P, 2, KC, P], F32R) for n in ("xe_hi", "eh_hi", "xe_lo", "eh_lo"))
        w13s_hi = sb("w13s_hi", [P, KC, 2 * D], F32R)
        low_pieces = (slice(0, free_1 // (KC * 2 * D)), slice(free_1 // (KC * 2 * D), free_2 // (KC * 2 * D)),
                      slice(free_2 // (KC * 2 * D), E))

        cnt = sb("cnt", [P, E])
        tiles_i = sb("tiles_i", [P, E], I32)
        tiles = sb("tiles", [P, E])
        tile_end = sb("tile_end", [P, E])
        coef = sb("coef", [P, E])
        iota_t = sb("iota_t", [1, EXPERT_TILES])
        tile_e = sb("tile_e", [1, EXPERT_TILES])
        tile_r = sb("tile_r", [1, EXPERT_TILES])
        tab_e = sb("tab_e", [1, EXPERT_TILES], I32)
        ROUND = 4
        ROUNDS = (EXPERT_TILES - 5) // ROUND
        digit = sb("digit", [1, 2 * ROUND])
        round_e = sb("round_e", [1, ROUNDS, 2 * ROUND])
        round_sum = sb("round_sum", [1, ROUNDS])
        tab_round = sb("tab_round", [1, ROUNDS], I32)
        assert E ** (2 * ROUND) <= 1 << 24
        tab_r = sb("tab_r", [1, EXPERT_TILES], I32)

        assert 2 * EXPERT_TILES * E <= spare.shape[1]
        past, past_c = (spare[0:1, k * EXPERT_TILES * E:(k + 1) * EXPERT_TILES * E]
                        .rearrange("p (n e) -> p n e", e=E) for k in range(2))

        xe = sb("xe", [P, 2, ROW])
        dest_all = sb("dest_all", [P, EXPERT_TILES])
        dest_i = sb("dest_i", [P, 2], I32)
        eth, eu, eh, ey = (t[:] for t in (th, gate, kg, ek))

        GOT = 4
        assert B % GOT == 0 and E * KC * D == HEADS * T
        got = w2_raw[:].rearrange("p e c n -> p (e c n)").rearrange(
            "p (g j k d) -> p g j k d", g=GOT, j=TT, k=TOP_K)

        x_in, ctx_in, w_in, cols_in, exp_w_in = (sem(n) for n in ("x_in", "ctx_in", "w_in", "cols_in", "exp_w_in"))
        cols_ready, const, zeroed = sem("cols_ready"), sem("const"), sem("zeroed")
        stats1_s, mv1_s, var1_s, rstd1_s, z1_s, z1t_p, xnt_s = (
            sem(n) for n in ("stats1_s", "mv1_s", "var1_s", "rstd1_s", "z1_s", "z1t_p", "xnt_s"))
        gate_p, k_p, q_p, v_p, sc_p, av_p = (sem(n) for n in ("gate_p", "k_p", "q_p", "v_p", "sc_p", "av_p"))
        th_s, gate_s, kg_s, kg1_s, ek_s, q1_s, qt_s, kt_s, v_s, at_s, den_s, rden_s, x2_s = (
            sem(n) for n in ("th_s", "gate_s", "kg_s", "kg1_s", "ek_s", "q1_s", "qt_s", "kt_s", "v_s", "at_s", "den_s",
                             "rden_s", "x2_s"))
        ctxt_p, k2_p, v2_p, z2t_p, q2_p, s_p, pt_p, o_p, den2_p, y_p = (
            sem(n) for n in ("ctxt_p", "k2_p", "v2_p", "z2t_p", "q2_p", "s_p", "pt_p", "o_p", "den2_p", "y_p"))
        ctxt_s, k2_s, kblk_s, vpad_s, stats2_s, mv2_s, var2_s, rstd2_s, z2_s, z2t_s, q2t_s = (
            sem(n) for n in ("ctxt_s", "k2_s", "kblk_s", "vpad_s", "stats2_s", "mv2_s", "var2_s", "rstd2_s", "z2_s",
                             "z2t_s", "q2t_s"))
        max_s, sub_s, exp_s, pt_s, rec_s, ot_s, xb_s, x3_s = (
            sem(n) for n in ("max_s", "sub_s", "exp_s", "pt_s", "rec_s", "ot_s", "xb_s", "x3_s"))
        stats3_s, mv3_s, var3_s, rstd3_s, z3_s, z3t_p, x3t_s, lgt_p, lgt_s, lg_p, lg_s = (
            sem(n) for n in ("stats3_s", "mv3_s", "var3_s", "rstd3_s", "z3_s", "z3t_p", "x3t_s", "lgt_p", "lgt_s",
                             "lg_p", "lg_s"))
        top_s, topi_s, topf_s, diff_s, ediff_s, esum_s, erec_s, score_s, pick_s, pickb_s, rank_p = (
            sem(n) for n in ("top_s", "topi_s", "topf_s", "diff_s", "ediff_s", "esum_s", "erec_s", "score_s", "pick_s",
                             "pickb_s", "rank_p"))
        posx_s, base_s, posm_s, posf_s, pos_s, xs_s, scattered = (
            sem(n) for n in ("posx_s", "base_s", "posm_s", "posf_s", "pos_s", "xs_s", "scattered"))
        base0_s, padi_s, padded, idle_in, tab_step, tab_s = (
            sem(n) for n in ("base0_s", "padi_s", "padded", "idle_in", "tab_step", "tab_s"))
        shared_in = sem("shared_in")
        xe_in = [sem("xe_in0"), sem("xe_in1")]
        ey_out = [sem("ey_out0"), sem("ey_out1")]
        xet_p, xet_s, h_p, eth_s, eu_s, eh_s, eht_p, eht_s, ey_p, ey_s, dest_s = (
            sem(n) for n in ("xet_p", "xet_s", "h_p", "eth_s", "eu_s", "eh_s", "eht_p", "eht_s", "ey_p", "ey_s",
                             "dest_s"))
        a_p, b_p, sth_s, su_s, sh_s, sy_p, x4_s = (
            sem(n) for n in ("a_p", "b_p", "sth_s", "su_s", "sh_s", "sy_p", "x4_s"))
        xdest_s, dstep_s, sum1_s, fin_s, fin_out = (
            sem(n) for n in ("xdest_s", "dstep_s", "sum1_s", "fin_s", "fin_out"))
        raw_in = [sem(f"raw_in{k}") for k in range(4)]
        w13s1_s, w13s_lo_s, w13s_hi_s, x3h_s, x3l_s = (
            sem(n) for n in ("w13s1_s", "w13s_lo_s", "w13s_hi_s", "x3h_s", "x3l_s"))
        self1_s, self_lo_s, self_hi_s, xnh_s, xnl_s = (
            sem(n) for n in ("self1_s", "self_lo_s", "self_hi_s", "xnh_s", "xnl_s"))
        cols_p, cols_s, rows_b_in, w_self_in = (sem(n) for n in ("cols_p", "cols_s", "rows_b_in", "w_self_in"))
        hi_s, lo_s, lo_pool_s, xlo_s, hlo_s = (sem(n) for n in ("hi_s", "lo_s", "lo_pool_s", "xlo_s", "hlo_s"))
        got_in = [sem(f"got_in{k}") for k in range(GOT)]

        x_v = x.rearrange("b (j p) d -> b p j d", p=P)
        out_v = out.rearrange("b (j p) d -> b p j d", p=P)
        got_v = rows_out.rearrange("(b j p k) d -> b p j k d", j=TT, p=P, k=TOP_K)
        self_weights = ((wg_sb, w_gate), (wqkv_sb, w_qkv))
        weights = ((wk_sb, wk_t), (wv_sb, wv_t), (wq_sb, wq_t), (wo_sb, wo_t),
                   (router_sb, router_t))
        shared_weights = ((w13s_sb, w13s), (w2s_sb, w2s))
        vectors = (ln_g, ln_b, b_qkv[0:2 * D], b_gate, bq, bk, bk)
        rows = ((bv_row, b_qkv[2 * D:3 * D]), (bv2_row, bv), (bo_row, bo))
        N_COLS = 16 * len(vectors)
        N_CONST = 14

        block = ctx.enter_context(nc.Block())

        def after(eng, s, count):
            if not isinstance(count, int) or count > 0:
                eng.wait_ge(s, count)

        def apart(eng):
            eng.nop(nofuse=True)

        def pad_regions(eng, nc_eng, experts):
            eng.wait_ge(padi_s, 1)
            for e in experts:
                row = nc_eng.value_load(pad_i[0:1, e:e + 1], min_val=0, max_val=IDLE_ROW)
                eng.dma_start(rows_in[bass.ds(row, P), :], pad_rows[:]).then_inc(padded, 16)

        @block.sync
        def _(sp):
            sp.dma_start(x_all[:, 0:TT, :], x_v[0]).then_inc(x_in, 16)
            sp.dma_start(ctx_sb[:], ctx_mem[0]).then_inc(ctx_in, 16)
            for dst, src in self_weights:
                sp.dma_start(dst[:], src.rearrange("(c p) n -> p c n", p=P)).then_inc(w_self_in, 16)
            for dst, src in weights:
                sp.dma_start(dst[:], src.rearrange("(c p) n -> p c n", p=P)).then_inc(w_in, 16)
            for dst, src in shared_weights:
                sp.dma_start(dst[:], src.rearrange("(c p) n -> p c n", p=P)).then_inc(shared_in, 16)
            def load_batch(b):
                sp.wait_ge(x_in, 16 * b)
                sp.dma_start(x_all[:, bass.ds(b * TT, TT), :], x_v[bass.ds(b, 1)].squeeze(0)).then_inc(x_in, 16)
                sp.wait_ge(ctxt_p, b)
                sp.dma_start(ctx_sb[:], ctx_mem[bass.ds(b, 1)].squeeze(0)).then_inc(ctx_in, 16)

            load_batch(1)
            sp.dma_start(w13_sb[:], w13.rearrange("e (c p) n -> p e c n", p=P)).then_inc(exp_w_in, 16)
            sp.dma_start(w2_sb[:], w2.rearrange("e (c p) n -> p e c n", p=P)).then_inc(exp_w_in, 16)
            with sp.Fori(2, B) as b:
                load_batch(b)
            for k, (free, count) in enumerate(((v2_p, B), (pt_p, UNITS * B), (y_p, B))):
                sp.wait_ge(free, count)
                sp.dma_start(w13_raw[:, low_pieces[k]],
                             w13[low_pieces[k]].rearrange("e (c p) n -> p e c n", p=P)).then_inc(raw_in[k], 16)
            sp.dma_start(w2_raw[:], w2.rearrange("e (c p) n -> p e c n", p=P)).then_inc(raw_in[3], 16)
            pad_regions(sp, nc.sync, range(0, E // 2))
            sp.wait_ge(scattered, 16 * B * TT * TOP_K)
            sp.wait_ge(padded, 16 * E)
            sp.wait_ge(idle_in, 16)
            sp.wait_ge(tab_s, 1)

            def load_tile(n, s):
                row = nc.sync.value_load(tab_r[0:1, bass.ds(n, 1)], min_val=0, max_val=IDLE_ROW)
                after(sp, xet_s, n - 1)
                sp.dma_start(xe[:, s, :], rows_in[bass.ds(row, P), :]).then_inc(xe_in[s], 16)

            load_tile(0, 0)
            load_tile(1, 1)
            with sp.Fori(1, EXPERT_TILES // 2) as m:
                load_tile(2 * m, 0)
                load_tile(2 * m + 1, 1)
            sp.wait_ge(ey_out[0], 8 * EXPERT_TILES)
            sp.wait_ge(ey_out[1], 8 * EXPERT_TILES)
            def load_got(b, k):
                after(sp, fin_s, b - GOT + 1)
                sp.dma_start(got[:, k], got_v[bass.ds(b, 1)].squeeze(0)).then_inc(got_in[k], 16)

            for b in range(GOT):
                load_got(b, b)
            with sp.Fori(1, B // GOT) as m:
                for k in range(GOT):
                    load_got(GOT * m + k, k)

        @block.scalar
        def _(act):
            k = 0
            for v in vectors:
                n = v.shape[0] // D
                act.dma_start(vec_rows[k:k + n, :], v.rearrange("(a d) -> a d", a=n)).then_inc(cols_in, 16)
                k += n
            for dst, v in rows:
                act.dma_start(dst[:], v.rearrange("(a d) -> a d", a=1).to_broadcast([P, D])).then_inc(rows_b_in, 16)
            act.wait_ge(cols_s, 1)

            HI = ([(w13_hi[:, e], w13_sb[:, e]) for e in range(E)] +
                  [(w2_hi[:, e:e + 2], w2_sb[:, e:e + 2]) for e in range(0, E, 2)])

            def high_parts(k):
                if k == 0:
                    act.wait_ge(exp_w_in, 32)
                for hi, w in HI[4 * k:4 * k + 4]:
                    act.copy(hi, w).then_inc(hi_s, 1)

            def norm_t(b):
                act.wait_ge(z1t_p, b + 1)
                after(act, v_p, min(b, 1) if isinstance(b, int) else 1)
                after(act, xnl_s, b - 1)
                for c in range(KC):
                    i = act.activation(xn_t[:, c, :], half(A)[:, c, :], ACT.Identity,
                                       bias=cols[:, B_, c:c + 1], scale=cols[:, G_, c:c + 1])
                i.then_inc(xnt_s, 1)

            def high_x(b):
                act.wait_ge(xnt_s, b + 1)
                after(act, v_p, b)
                after(act, b_p, b - 2)
                act.copy(xn_hi[:], xn_t[:]).then_inc(xnh_s, 1)

            def gate_tanh(b):
                act.wait_ge(gate_p, b + 1)
                for c in range(KC):
                    i = act.activation(th[:, c, :], half(A)[:, c, :], ACT.Tanh, bias=cols2[:, 1, c:c + 1], scale=0.5)
                i.then_inc(th_s, 1)
                act.wait_ge(th_s, b + 1)
                after(act, kg_s, b)
                act.activation(gate[:], th[:], ACT.Identity, bias=cols2[:, 3, 0:1], scale=0.5).then_inc(gate_s, 1)

            def q_exp(b):
                act.wait_ge(q_p, b + 1)
                after(act, qt_s, b)
                after(act, sc_p, b)
                for c in range(KC):
                    act.activation(eq[:, c, :], half(A)[:, c, :], ACT.Exp, bias=cols[:, BQ, c:c + 1])
                for c in range(KC):
                    i = act.activation(q1[:, c, :], half(A)[:, c, :], ACT.Identity, bias=cols2[:, 0, c:c + 1])
                i.then_inc(q1_s, 1)

            def k_exp(b):
                act.wait_ge(kg_s, b + 1)
                after(act, kt_s, b)
                act.activation(ek[:], kg[:], ACT.Exp).then_inc(ek_s, 1)

            def ctx_copy(b):
                act.wait_ge(ctxt_p, b + 1)
                after(act, v2_p, b)
                act.copy(ctx_t[:].rearrange("p c s -> p (c s)"), A[:, 0:KC * S]).then_inc(ctxt_s, 1)

            def k2_bias(b):
                act.wait_ge(k2_p, b + 1)
                after(act, kblk_s, KC * b)
                for c in range(KC):
                    i = act.activation(k2[:, c, :], half(BB)[:, c, 0:S], ACT.Identity, bias=cols[:, BK2, c:c + 1])
                i.then_inc(k2_s, 1)

            def z2_copy(b):
                act.wait_ge(z2t_p, b + 1)
                after(act, q2_p, b)
                act.copy(z2_t[:], half(BB)).then_inc(z2t_s, 1)

            def q2_scale(b):
                act.wait_ge(q2_p, b + 1)
                after(act, s_p, UNITS * b)
                for c in range(KC):
                    i = act.activation(q2_t[:, c, :], half(DD)[:, c, :], ACT.Identity, bias=cols2[:, 2, c:c + 1],
                                       scale=SCALE)
                i.then_inc(q2t_s, 1)

            def soft_exp(b, u):
                act.wait_ge(sub_s, UNITS * b + u + 1)
                act.activation(pr[:, u % PR], pr[:, u % PR], ACT.Exp).then_inc(exp_s, 1)

            def p_copy(b, u):
                j, h0 = (u // 2) % 2, (u // 4) * HC + (u % 2) * QH
                act.wait_ge(pt_p, UNITS * b + u + 1)
                if u == 0:
                    after(act, o_p, b)
                bank = (GG, HH)[u % 2]
                act.copy(p_t[:, h0:h0 + QH, j * P:(j + 1) * P],
                         bank[0:S, :].rearrange("s (h t) -> s h t", h=QH)).then_inc(pt_s, 1)

            def x3_copy(b):
                act.wait_ge(z3t_p, b + 1)
                after(act, b_p, b)
                act.copy(x3n_t[:], half(C)).then_inc(x3t_s, 1)

            def x3_high(b):
                act.wait_ge(x3t_s, b + 1)
                act.wait_ge(v_p, b + 3 if not isinstance(b, int) else min(b + 3, B))
                act.copy(xn_hi[:], x3n_t[:]).then_inc(x3h_s, 1)

            def scale_rows(b):
                act.wait_ge(score_s, b + 1)
                after(act, scattered, 16 * TT * TOP_K * b)
                for j in range(TT):
                    for k in range(TOP_K):
                        i = act.activation(xs[:, j, k, 0:D], z3[:, j, :], ACT.Copy, scale=score[:, j, k:k + 1])
                i.then_inc(xs_s, 1)

            def shared_tanh(b):
                act.wait_ge(a_p, b + 1)
                after(act, sy_p, b)
                act.activation(sth[:], half(EE), ACT.Tanh, scale=0.5).then_inc(sth_s, 1)

            def router_exp(b):
                act.wait_ge(diff_s, b + 1)
                after(act, score_s, b)
                act.activation(ediff[:], diff[:], ACT.Exp).then_inc(ediff_s, 1)

            def turn(i, has1, has2, has3, more1, has4=True):
                j, l = i - 1, i - 2
                if has1:
                    ctx_copy(i)
                if isinstance(i, int) and i == 2:
                    act.wait_ge(w13s_lo_s, 1)
                    act.copy(w13s_hi[:], w13s_sb[:]).then_inc(w13s_hi_s, 1)
                if isinstance(i, int) and 1 <= i < 4:
                    high_parts(i - 1)
                for u in range(UNITS + 1):
                    if has1 and u == 3:
                        q_exp(i)
                    if isinstance(i, int) and i == 0:
                        w_self = low_room[:, 0:KC * 4 * D]
                        if u == 2:
                            act.copy(self_lo[:], w_self).then_inc(self1_s, 1)
                        if u == 5:
                            act.wait_ge(v_p, 1)
                            act.wait_ge(self_lo_s, 1)
                            act.copy(self_hi[:], w_self).then_inc(self_hi_s, 1)
                    if isinstance(i, int) and i == 0 and u == 5:
                        act.wait_ge(shared_in, 16 * len(shared_weights))
                        act.copy(w13s_lo[:], w13s_sb[:]).then_inc(w13s1_s, 1)
                    if has3 and u == 6:
                        x3_high(l)
                    if has1 and u == UNITS - 1:
                        z2_copy(i)
                    if has2 and u < UNITS:
                        soft_exp(j, u)
                    if has1 and u == 0:
                        gate_tanh(i)
                    if has1 and u == 1:
                        k2_bias(i)
                    if has3 and u == 5:
                        x3_copy(l)
                    if has2 and 2 <= u < UNITS:
                        p_copy(j, u - 2)
                    if has1 and u == 1:
                        k_exp(i)
                    if more1 and u == 6:
                        norm_t(i + 1)
                if has3:
                    router_exp(l)
                if has2:
                    p_copy(j, UNITS - 2)
                if has3:
                    shared_tanh(l)
                if has1:
                    q2_scale(i)
                if has2:
                    p_copy(j, UNITS - 1)
                if more1:
                    high_x(i + 1)
                if has3:
                    scale_rows(l)

            norm_t(0)
            act.wait_ge(cols_ready, 4)
            for i in range(4):
                turn(i, True, i >= 1, i >= 2, True, i >= 3)
            with act.Fori(4, B - 1) as i:
                turn(i, True, True, True, True)
            turn(B - 1, True, True, True, False)
            turn(B, False, True, True, False)
            turn(B + 1, False, False, True, False)
            turn(B + 2, False, False, False, False)

            pad_regions(act, nc.scalar, range(E // 2, E))

            def tile_copy_x(n, s):
                act.wait_ge(xet_p, n + 1)
                after(act, h_p, n - 1)
                act.copy(dest_all[:, bass.ds(n, 1)], xe[:, s, D:D + 1])
                after(act, xlo_s, n - 1)
                act.copy(xe_hi[:, s], (A, BB)[s][:, 0:D].rearrange("p (c t) -> p c t", c=KC)).then_inc(xet_s, 1)

            def tile_tanh(n, s):
                act.wait_ge(h_p, n + 1)
                after(act, eu_s, n - 1)
                act.activation(eth[:, s, :], (C, DD)[s][:, 0:D], ACT.Tanh, scale=0.5).then_inc(eth_s, 1)

            def tile_copy_h(n, s):
                act.wait_ge(eht_p, n + 1)
                after(act, ey_p, n - 1)
                after(act, hlo_s, n - 1)
                act.copy(eh_hi[:, s], (EE, FF)[s][:, 0:D].rearrange("p (c t) -> p c t", c=KC)).then_inc(eht_s, 1)

            def tile_step(n, s, ahead3=True, ahead2=True):
                if ahead3:
                    tile_copy_x(n + 3, 1 - s)
                tile_copy_h(n, s)
                if ahead2:
                    tile_tanh(n + 2, s)

            tile_copy_x(0, 0)
            tile_copy_x(1, 1)
            tile_tanh(0, 0)
            tile_copy_x(2, 0)
            tile_tanh(1, 1)
            tile_step(0, 0)
            tile_step(1, 1)
            with act.Fori(1, EXPERT_TILES // 2 - 2) as m:
                n = 2 * m
                tile_step(n, 0)
                tile_step(n + 1, 1)
            tile_step(EXPERT_TILES - 4, 0)
            tile_step(EXPERT_TILES - 3, 1, ahead3=False)
            tile_step(EXPERT_TILES - 2, 0, ahead3=False, ahead2=False)
            tile_step(EXPERT_TILES - 1, 1, ahead3=False, ahead2=False)

            with act.Fori(0, B) as b:
                act.wait_ge(fin_s, b + 1)
                act.dma_start(out_v[bass.ds(b, 1)].squeeze(0), x_all[:, bass.ds(b * TT, TT), :]).then_inc(fin_out, 16)
            act.wait_ge(fin_out, 16 * B)

        @block.gpsimd
        def _(pool):
            g = nc.gpsimd
            g.memset(ident[:], 1.0)
            g.memset(causal3[:], 1.0)
            g.memset(before[:], 1.0)
            g.memset(ones_b[:], 1.0)
            g.memset(head_mask[:], 1.0)
            g.memset(pair_ones[:], 0.0)
            g.memset(minus_half[:], -0.5)
            for k in range(2 * ROUND):
                g.memset(digit[:, k:k + 1], float(E ** k))
            g.memset(v_pad[:], 0.0)
            g.memset(pad_rows[:], 0.0)
            g.iota(dest[:], [[P * TOP_K, TT], [1, TOP_K]], base=0, channel_multiplier=TOP_K,
                   allow_small_or_imprecise_dtypes=True)
            g.iota(iota_e[:], [[1, E]], base=0, channel_multiplier=0, allow_small_or_imprecise_dtypes=True)
            g.iota(ebase[:], [[REGION, E]], base=0, channel_multiplier=0, allow_small_or_imprecise_dtypes=True)
            g.iota(iota_t[:], [[1, EXPERT_TILES]], base=0, channel_multiplier=0,
                   allow_small_or_imprecise_dtypes=True)
            g.memset(v_ext[:, :, D:D + 1], 1.0).then_inc(zeroed, 1)
            pool.wait_ge(zeroed, 1)
            g.iota(pad_rows[:, D:ROW], [[0, 1]], base=RESULTS, channel_multiplier=1,
                   allow_small_or_imprecise_dtypes=True)
            g.affine_select(out=ident[:], in_=ident[:], compare_op=ALU.is_equal, fill=0.0, base=0,
                            pattern=[[-1, P]], channel_multiplier=1)
            for d in (0, 2):
                g.affine_select(out=causal3[:, d], in_=causal3[:, d], compare_op=ALU.is_ge, fill=0.0, base=0,
                                pattern=[[1, P]], channel_multiplier=-1)
            g.affine_select(out=before[:], in_=before[:], compare_op=ALU.is_gt, fill=0.0, base=0,
                            pattern=[[1, P]], channel_multiplier=-1)
            for e in range(2):
                g.memset(pair_ones[:, e, e * HD:(e + 1) * HD], 1.0)
            g.affine_select(out=head_mask[:], in_=head_mask[:], compare_op=ALU.is_ge, fill=0.0, base=0,
                            pattern=[[-HD, HC]], channel_multiplier=1).then_inc(zeroed, 1)
            pool.wait_ge(zeroed, 2)
            g.affine_select(out=head_mask[:], in_=head_mask[:], compare_op=ALU.is_ge, fill=0.0, base=HD - 1,
                            pattern=[[HD, HC]], channel_multiplier=-1).then_inc(const, 1)
            pool.wait_ge(const, 1)
            g.dma_start(rows_in[IDLE_ROW:IDLE_ROW + P, :], pad_rows[:]).then_inc(idle_in, 16)
            def rstd(b, mv, mv_s, var, var_s, out_, out_s, twice, readers):
                pool.wait_ge(mv_s, b + 1)
                apart(pool)
                scale, offset = (1.0 + LN_EPS, LN_EPS * LN_EPS) if twice else (1.0, LN_EPS)
                g.tensor_scalar(var[:], mv[:, :, 1], scale, offset, ALU.mult, ALU.add).then_inc(var_s, 1)
                pool.wait_ge(var_s, b + 1)
                after(pool, readers, b)
                g.tensor_tensor(out_[:], var[:], minus_half[:], ALU.pow).then_inc(out_s, 1)

            def low_x(b):
                pool.wait_ge(xnh_s, b)
                after(pool, v_p, b)
                after(pool, b_p, b - 2)
                g.tensor_tensor(xn_lo[:], xn_t[:], xn_hi[:], ALU.subtract).then_inc(xnl_s, 1)

            def x3_low(b):
                pool.wait_ge(x3h_s, b + 1)
                g.tensor_tensor(xn_lo[:], x3n_t[:], xn_hi[:], ALU.subtract).then_inc(x3l_s, 1)

            def k_plus(b):
                pool.wait_ge(kg_s, b + 1)
                after(pool, sc_p, b)
                apart(pool)
                g.tensor_scalar(kg1[:], kg[:], 1.0, None, ALU.add).then_inc(kg1_s, 1)

            def k_blocks(b, c):
                pool.wait_ge(k2_s, b + 1)
                after(pool, s_p, UNITS * b - UNITS // KC * (KC - 1 - c))
                g.tensor_tensor(k_blk[:, c], k2[:, c:c + 1, :].to_broadcast([P, HC, S]),
                                head_mask[:].rearrange("p (h a) -> p h a", a=1).to_broadcast([P, HC, S]),
                                ALU.mult).then_inc(kblk_s, 1)

            def residual_bias(b):
                pool.wait_ge(x2_s, b + 1)
                pool.wait_ge(z2_s, b + 1)
                x2 = x_all[:, bass.ds(b * TT, TT), :]
                g.tensor_tensor(x2, x2,
                                bo_row[:].rearrange("p (a d) -> p a d", a=1).to_broadcast([P, TT, D]),
                                ALU.add).then_inc(xb_s, 1)

            def mark_rows(b):
                after(pool, scattered, 16 * TT * TOP_K * b)
                after(pool, dstep_s, b)
                apart(pool)
                g.tensor_copy(xs[:, :, :, D:ROW].squeeze(3), dest[:]).then_inc(xdest_s, 1)
                pool.wait_ge(xdest_s, b + 1)
                apart(pool)
                g.tensor_scalar(dest[:], dest[:], float(T * TOP_K), None, ALU.add).then_inc(dstep_s, 1)

            def scatter(b):
                pool.wait_ge(xdest_s, b + 1)
                pool.wait_ge(xs_s, b + 1)
                pool.wait_ge(pos_s, b + 1)
                apart(pool)
                for j in range(TT):
                    for k in range(TOP_K):
                        g.indirect_dma_start(
                            out=rows_in[:], out_offset=bass.IndirectOffsetOnAxis(ap=pos_cur[:, j, k:k + 1], axis=0),
                            in_=xs[:, j, k, :], in_offset=None).then_inc(scattered, 16)

            def turn(i, has1, has2, has3, more1, has4=True):
                j, l = i - 1, i - 2
                if isinstance(i, int) and i == 1:
                    pool.wait_ge(w13s1_s, 1)
                    g.tensor_tensor(w13s_lo[:], w13s_sb[:], w13s_lo[:], ALU.subtract).then_inc(w13s_lo_s, 1)
                if isinstance(i, int) and i == B + 1:
                    pool.wait_ge(hi_s, 4 * len(low_pieces))
                    pool.wait_ge(raw_in[1], 16)
                    es = low_pieces[1]
                    g.tensor_tensor(w13_lo[:, es], w13_raw[:, es], w13_hi[:, es], ALU.subtract).then_inc(lo_pool_s, 1)
                if has2:
                    residual_bias(j)
                if more1:
                    rstd(i + 1, mv1, mv1_s, var1, var1_s, rstd1, rstd1_s, True, z1_s)
                if has1:
                    k_plus(i)
                if has3:
                    rstd(l, mv3, mv3_s, var3, var3_s, rstd3, rstd3_s, False, z3_s)
                if has1:
                    k_blocks(i, 0)
                if has3:
                    x3_low(l)
                if has1:
                    rstd(i, mv2, mv2_s, var2, var2_s, rstd2, rstd2_s, False, z2_s)
                    k_blocks(i, 1)
                if has3:
                    mark_rows(l)
                if more1:
                    low_x(i + 1)
                if has3:
                    scatter(l)

            rstd(0, mv1, mv1_s, var1, var1_s, rstd1, rstd1_s, True, z1_s)
            pool.wait_ge(rows_b_in, 16 * len(rows))
            pool.wait_ge(cols_s, 1)
            apart(pool)
            g.memset(cols2[:, 3, :], 0.5).then_inc(cols_ready, 1)
            g.tensor_scalar(cols2[:, 0, :], cols[:, BQ, :], 1.0, None, ALU.add).then_inc(cols_ready, 1)
            g.tensor_scalar(cols2[:, 1, :], cols[:, BG, :], 0.5, None, ALU.mult).then_inc(cols_ready, 1)
            g.tensor_scalar(cols2[:, 2, :], cols[:, BQ2, :], SCALE, None, ALU.mult).then_inc(cols_ready, 1)
            for i in range(4):
                turn(i, True, i >= 1, i >= 2, True, i >= 3)
            with pool.Fori(4, B - 1) as i:
                turn(i, True, True, True, True)
            turn(B - 1, True, True, True, False)
            turn(B, False, True, True, False)
            turn(B + 1, False, False, True, False)
            turn(B + 2, False, False, False, False)

            def store_tile(n, s):
                pool.wait_ge(xet_s, n + 1)
                after(pool, ey_out[s], (n - s) * 8)
                apart(pool)
                g.tensor_copy(dest_i[:, s:s + 1], dest_all[:, bass.ds(n, 1)]).then_inc(dest_s, 1)
                pool.wait_ge(dest_s, n + 1)
                pool.wait_ge(ey_s, n + 1)
                apart(pool)
                g.indirect_dma_start(out=rows_out[:],
                                     out_offset=bass.IndirectOffsetOnAxis(ap=dest_i[:, s:s + 1], axis=0),
                                     in_=ey[:, s, :], in_offset=None,
                                     bounds_check=RESULTS - 1, oob_is_err=False).then_inc(ey_out[s], 16)

            store_tile(0, 0)
            store_tile(1, 1)
            with pool.Fori(1, EXPERT_TILES // 2) as m:
                store_tile(2 * m, 0)
                store_tile(2 * m + 1, 1)

        @block.tensor
        def _(pe):
            def project(bank, w, c0, src, n=T):
                for m in range(KC):
                    for c in range(KC):
                        i = pe.matmul(half(bank)[:, m, 0:n], w[:, c, c0 + m * P:c0 + (m + 1) * P], src[:, c, 0:n],
                                      start=(c == 0), stop=(c == KC - 1))
                return i

            def project_rows(bank, src, w, c0):
                for j in range(TT):
                    for c in range(KC):
                        i = pe.matmul(half(bank)[:, j, :], src[:, c, j * P:(j + 1) * P], w[:, c, c0:c0 + D],
                                      start=(c == 0), stop=(c == KC - 1))
                return i

            def split_project(bank, w_hi, w_lo, c0):
                steps = [(c, w, x) for c in range(KC) for w, x in ((w_hi, xn_hi), (w_hi, xn_lo), (w_lo, xn_hi))]
                for m in range(KC):
                    for k, (c, w, x_) in enumerate(steps):
                        i = pe.matmul(half(bank)[:, m, :], w[:, c, c0 + m * P:c0 + (m + 1) * P], x_[:, c, :],
                                      start=(k == 0), stop=(k == len(steps) - 1))
                return i

            def split_project_rows(bank, w_hi, w_lo, c0):
                steps = [(c, x, w) for c in range(KC) for x, w in ((xn_hi, w_hi), (xn_hi, w_lo), (xn_lo, w_hi))]
                for j in range(TT):
                    for k, (c, x_, w) in enumerate(steps):
                        i = pe.matmul(half(bank)[:, j, :], x_[:, c, j * P:(j + 1) * P], w[:, c, c0:c0 + D],
                                      start=(k == 0), stop=(k == len(steps) - 1))
                return i

            def whole(b):
                return isinstance(b, int) and b == 0

            def turn_tiles(bank, src):
                for j in range(TT):
                    for c in range(KC):
                        i = pe.transpose(half(bank)[:, c, j * P:(j + 1) * P], src[:, j, c * P:(c + 1) * P], ident[:])
                return i

            def z1_turn(b):
                pe.wait_ge(z1_s, b + 1)
                after(pe, x2_s, b)
                turn_tiles(A, z1).then_inc(z1t_p, 1)

            def gate_proj(b):
                pe.wait_ge(xnt_s, b + 1)
                pe.wait_ge(ctxt_s, b + 1)
                if whole(b):
                    i = project(A, wg_sb, 0, xn_t)
                else:
                    pe.wait_ge(self_hi_s, 1)
                    pe.wait_ge(xnl_s, b)
                    i = split_project(A, wg_hi, wg_lo, 0)
                i.then_inc(gate_p, 1)

            def k_proj(b):
                if not isinstance(b, int) or b >= 2:
                    pe.wait_ge(rec_s, b - 1)
                elif b == 1:
                    pe.wait_ge(q2t_s, 1)
                i = project(DD, wqkv_sb, D, xn_t) if whole(b) else split_project(DD, wqkv_hi, wqkv_lo, D)
                i.then_inc(k_p, 1)

            def q_proj(b):
                pe.wait_ge(th_s, b + 1)
                i = project(A, wqkv_sb, 0, xn_t) if whole(b) else split_project(A, wqkv_hi, wqkv_lo, 0)
                i.then_inc(q_p, 1)

            def v_proj(b):
                pe.wait_ge(k2_s, b + 1)
                i = (project_rows(BB, xn_t, wqkv_sb, 2 * D) if whole(b) else
                     split_project_rows(BB, wqkv_hi, wqkv_lo, 2 * D))
                i.then_inc(v_p, 1)

            def scores(b):
                pe.wait_ge(kt_s, b + 1)
                pe.wait_ge(qt_s, b + 1)
                pe.wait_ge(v_s, b + 1)
                for s0, t0, o0 in ((0, 0, 0), (1, 1, 2)):
                    n = T - t0 * P
                    for c in range(KC):
                        i = pe.matmul(BB[:, o0 * P:o0 * P + n], k_t[:, c, s0 * P:(s0 + 1) * P], q_t[:, c, t0 * P:T],
                                      start=(c == 0), stop=(c == KC - 1))
                i.then_inc(sc_p, 1)

            def values(b):
                pe.wait_ge(at_s, b + 1)
                pe.wait_ge(v_s, b + 1)
                pe.wait_ge(kg_s, b + 1)
                after(pe, x4_s, b - 2)
                pe.wait_ge(q1_s, b + 1)
                pe.matmul(DD[:, 0:D + 1], at[:, 0, :], v_ext[:, 0, :], start=True, stop=True)
                pe.matmul(A[:, 0:D + 1], at[:, 1, :], v_ext[:, 0, :], start=True, stop=False)
                pe.matmul(A[:, 0:D + 1], at[:, 2, :], v_ext[:, 1, :], start=False, stop=True).then_inc(av_p, 1)

            def ctx_turn(b):
                pe.wait_ge(ctx_in, 16 * (b + 1))
                pe.wait_ge(xnt_s, b + 1)
                for c in range(KC):
                    i = pe.transpose(A[:, c * S:(c + 1) * S], ctx_sb[:, c * P:(c + 1) * P], ident[0:S, 0:S])
                i.then_inc(ctxt_p, 1)

            def k2_proj(b):
                pe.wait_ge(ctxt_s, b + 1)
                after(pe, vpad_s, b)
                project(BB, wk_sb, 0, ctx_t, S).then_inc(k2_p, 1)

            def v2_proj(b):
                pe.wait_ge(z2t_s, b + 1)
                for c in range(KC):
                    i = pe.matmul(BB[0:S, 0:D], ctx_t[:, c, :], wv_sb[:, c, :], start=(c == 0), stop=(c == KC - 1))
                i.then_inc(v2_p, 1)

            def z2_turn(b):
                pe.wait_ge(z2_s, b + 1)
                pe.wait_ge(at_s, b + 1)
                turn_tiles(BB, z2).then_inc(z2t_p, 1)

            def q2_proj(b):
                pe.wait_ge(z2t_s, b + 1)
                pe.wait_ge(x2_s, b + 1)
                project(DD, wq_sb, 0, z2_t).then_inc(q2_p, 1)

            def head_scores(b, u):
                c, j, h0 = u // 4, (u // 2) % 2, (u % 2) * QH
                if u == 0:
                    pe.wait_ge(q2t_s, b + 1)
                if u % 4 == 0:
                    pe.wait_ge(kblk_s, KC * b + c + 1)
                after(pe, sub_s, UNITS * b + u - 1)
                if u < 2:
                    after(pe, (su_s, sh_s)[u], b - 1)
                pe.matmul((EE, FF)[u % 2][:, 0:QH * S], q2_t[:, c, j * P:(j + 1) * P],
                          k_blk[:, c, h0:h0 + QH, :], start=True, stop=True).then_inc(s_p, 1)

            def p_turn(b, u):
                pe.wait_ge(exp_s, UNITS * b + u + 1)
                after(pe, pt_s, UNITS * b + u - 1)
                bank = (GG, HH)[u % 2]
                for h in range(QH):
                    i = pe.transpose(bank[0:S, h * P:(h + 1) * P], pr[:, u % PR, h, :], ident[:])
                i.then_inc(pt_p, 1)

            def head_values(b):
                pe.wait_ge(vpad_s, b + 1)
                pe.wait_ge(pt_s, UNITS * (b + 1))
                if not isinstance(b, int) or b + 2 <= B:
                    pe.wait_ge(q2t_s, b + 2 if not isinstance(b, int) else min(b + 2, B))
                if isinstance(b, int):
                    after(pe, x4_s, b - 1)
                for bank, w, done in ((DD, pair_ones, den2_p), (C, None, o_p)):
                    if w is None:
                        after(pe, base_s, b)
                    for c in range(KC):
                        for e in range(2):
                            for s in range(4):
                                pair = c * 4 + s
                                lhs = v_pad[:, pair, e, :] if w is None else w[:, e, :]
                                i = pe.matmul(half(bank)[s * 32:(s + 1) * 32, c, :], lhs, p_t[:, 2 * pair + e, :],
                                              start=(e == 0), stop=(e == 1), skip_group_check=True)
                    i.then_inc(done, 1)

            def out_proj(b):
                pe.wait_ge(ot_s, b + 1)
                project_rows(C, o_t, wo_sb, 0).then_inc(y_p, 1)

            def z3_turn(b):
                pe.wait_ge(z3_s, b + 1)
                turn_tiles(C, z3).then_inc(z3t_p, 1)

            def logits_t(b):
                pe.wait_ge(x3t_s, b + 1)
                for c in range(KC):
                    i = pe.matmul(C[0:E, 0:T], router_sb[:, c, :], x3n_t[:, c, :],
                                  start=(c == 0), stop=(c == KC - 1))
                i.then_inc(lgt_p, 1)

            def logits(b):
                pe.wait_ge(lgt_s, b + 1)
                apart(pe)
                for j in range(TT):
                    i = pe.transpose(C[:, j * E:(j + 1) * E], lg_t[:, j * P:(j + 1) * P], ident[0:E, 0:E])
                i.then_inc(lg_p, 1)

            def ranks(b):
                pe.wait_ge(pickb_s, b + 1)
                pe.wait_ge(lg_s, b + 1)
                pe.matmul(C[:, 0:E], before[:], pick_b[:, 0, :], start=True, stop=True)
                pe.matmul(C[:, E:2 * E], before[:], pick_b[:, 1, :], start=True, stop=False)
                pe.matmul(C[:, E:2 * E], ones_b[:], pick_b[:, 0, :], start=False, stop=True)
                pe.matmul(C[:, 2 * E:3 * E], ones_b[:], pick_b[:, 0, :], start=True, stop=False)
                pe.matmul(C[:, 2 * E:3 * E], ones_b[:], pick_b[:, 1, :], start=False, stop=True).then_inc(rank_p, 1)

            def shared_up(b, bank, w0, done):
                pe.wait_ge(w13s_hi_s, 1)
                pe.wait_ge(x3l_s, b + 1)
                last = 1 if bank is EE else 0
                pe.wait_ge(sub_s, (UNITS * (b + 2) if not isinstance(b, int) else UNITS * min(b + 2, B)) - last)
                split_project(bank, w13s_hi, w13s_lo, w0).then_inc(done, 1)

            def shared_down(b):
                pe.wait_ge(sh_s, b + 1)
                pe.wait_ge(kg_s, b + 4 if not isinstance(b, int) else min(b + 4, B))
                if isinstance(b, int):
                    pe.wait_ge(rec_s, min(b + 2, B))
                project_rows(DD, sh, w2s_sb, 0).then_inc(sy_p, 1)

            def turn(i, has1, has2, has3, more1, has4=True):
                j, l = i - 1, i - 2
                if has2:
                    v2_proj(j)
                if has1:
                    ctx_turn(i)
                if has3:
                    head_values(l)
                for u in range(UNITS + 1):
                    if has2 and u < UNITS:
                        head_scores(j, u)
                    if has1 and u == 0:
                        gate_proj(i)
                    if isinstance(i, int) and i == 0 and u == 1:
                        pe.wait_ge(w_in, 16 * len(weights))
                    if has1 and u == 1:
                        k2_proj(i)
                    if has3 and u == 5:
                        z3_turn(l)
                    if has1 and u == 3:
                        q_proj(i)
                    if has2 and 2 <= u < UNITS:
                        p_turn(j, u - 2)
                    if has1 and u == 1:
                        k_proj(i)
                    if has3 and u == 2:
                        out_proj(l)
                    if has1 and u == 3:
                        v_proj(i)
                    if has4 and u == 4:
                        shared_down(i - 3)
                    if has1 and u == 4:
                        scores(i)
                    if has1 and u == 5:
                        values(i)
                    if has3 and u == 6:
                        logits_t(l)
                    if more1 and u == 6:
                        z1_turn(i + 1)
                if has3:
                    shared_up(l, EE, 0, a_p)
                    logits(l)
                if has1:
                    z2_turn(i)
                if has2:
                    p_turn(j, UNITS - 2)
                if has3:
                    shared_up(l, FF, D, b_p)
                if has1:
                    q2_proj(i)
                if has2:
                    p_turn(j, UNITS - 1)
                if has3:
                    ranks(l)

            pe.wait_ge(const, 1)
            z1_turn(0)
            pe.wait_ge(cols_in, N_COLS)
            apart(pe)
            for c in range(KC):
                i = pe.transpose(GG[:, c * 8:(c + 1) * 8], vec_rows[:, c * P:(c + 1) * P], ident[0:8, 0:8])
            i.then_inc(cols_p, 1)
            pe.wait_ge(w_self_in, 16 * len(self_weights))
            for i in range(4):
                turn(i, True, i >= 1, i >= 2, True, i >= 3)
            with pe.Fori(4, B - 1) as i:
                turn(i, True, True, True, True)
            turn(B - 1, True, True, True, False)
            turn(B, False, True, True, False)
            turn(B + 1, False, False, True, False)
            turn(B + 2, False, False, False, False)

            pe.wait_ge(exp_w_in, 32)
            pe.wait_ge(tab_s, 1)
            pe.wait_ge(base_s, B)
            pe.wait_ge(x4_s, B)

            pe.wait_ge(hi_s, len(low_pieces) * 4)
            pe.wait_ge(lo_pool_s, 1)
            pe.wait_ge(lo_s, len(low_pieces) - 1)

            def split_product(out_, x_hi, x_lo, w_hi, w_lo, e):
                steps = [(c, a, w) for c in range(KC) for a, w in ((x_hi, w_hi), (x_hi, w_lo), (x_lo, w_hi))]
                for k, (c, a, w) in enumerate(steps):
                    i = pe.matmul(out_, a[:, c, :], w[:, bass.ds(e, 1), c, :].squeeze(1),
                                  start=(k == 0), stop=(k == len(steps) - 1))
                return i

            def tile_turn_x(n, s):
                pe.wait_ge(xe_in[s], (n - s) * 8 + 16)
                after(pe, xlo_s, n - 1)
                for c in range(KC):
                    i = pe.transpose((A, BB)[s][:, c * P:(c + 1) * P], xe[:, s, c * P:(c + 1) * P], ident[:])
                i.then_inc(xet_p, 1)

            def tile_expert(n):
                return nc.tensor.value_load(tab_e[0:1, bass.ds(n, 1)], min_val=0, max_val=E - 1)

            def tile_up(n, s, e):
                pe.wait_ge(xlo_s, n + 1)
                after(pe, eh_s, n - 1)
                split_product((C, DD)[s][:], xe_hi[:, s], xe_lo[:, s], w13_hi, w13_lo, e).then_inc(h_p, 1)

            def tile_turn_h(n, s):
                pe.wait_ge(eh_s, n + 1)
                after(pe, hlo_s, n - 1)
                for c in range(KC):
                    i = pe.transpose((EE, FF)[s][:, c * P:(c + 1) * P], eh[:, s, c * P:(c + 1) * P], ident[:])
                i.then_inc(eht_p, 1)

            def tile_down(n, s, e):
                pe.wait_ge(hlo_s, n + 1)
                after(pe, ey_s, n - 1)
                split_product((GG, HH)[s][:, 0:D], eh_hi[:, s], eh_lo[:, s], w2_hi, w2_lo, e).then_inc(ey_p, 1)

            def tile_step(n, s, ahead3=True, ahead2=True, behind=True, e_up=None, e_down=None):
                if isinstance(n, int):
                    e_down = tile_expert(n - 1) if behind else None
                    e_up = tile_expert(n + 2) if ahead2 else None
                if ahead3:
                    tile_turn_x(n + 3, 1 - s)
                tile_turn_h(n, s)
                if behind:
                    tile_down(n - 1, 1 - s, e_down)
                if ahead2:
                    tile_up(n + 2, s, e_up)

            tile_turn_x(0, 0)
            tile_turn_x(1, 1)
            tile_up(0, 0, tile_expert(0))
            tile_turn_x(2, 0)
            tile_up(1, 1, tile_expert(1))
            tile_step(0, 0, behind=False)
            pe.wait_ge(lo_s, len(low_pieces))
            tile_step(1, 1)
            with pe.Fori(0, ROUNDS) as m:
                digits = nc.tensor.value_load(tab_round[0:1, bass.ds(m, 1)], min_val=0, max_val=E ** (2 * ROUND) - 1)
                for k in range(ROUND):
                    tile_step(ROUND * m + 2 + k, k % 2, e_up=digits // E ** k % E,
                              e_down=digits // E ** (ROUND + k) % E)
            for n in range(2 + ROUND * ROUNDS, EXPERT_TILES):
                tile_step(n, n % 2, ahead3=n + 3 < EXPERT_TILES, ahead2=n + 2 < EXPERT_TILES)
            tile_down(EXPERT_TILES - 1, 1, tile_expert(EXPERT_TILES - 1))

        @block.vector
        def _(dve):
            def moments(b, stats, stats_s, mv, mv_s, readers):
                after(dve, readers, b)
                apart(dve)
                for j in range(TT):
                    i = dve.bn_stats(stats[:, j, :], x_all[:, bass.ds(b * TT + j, 1), :].squeeze(1))
                i.then_inc(stats_s, 1)
                dve.wait_ge(stats_s, b + 1)
                apart(dve)
                for j in range(TT):
                    i = dve.bn_aggr(mv[:, j, :], stats[:, j, :])
                i.then_inc(mv_s, 1)

            def normalise(b, z, mv, rstd, rstd_s, z_s):
                dve.wait_ge(rstd_s, b + 1)
                for j in range(TT):
                    i = dve.tensor_scalar(z[:, j, :], x_all[:, bass.ds(b * TT + j, 1), :].squeeze(1),
                                          mv[:, j, 0:1], rstd[:, j:j + 1], ALU.subtract, ALU.mult)
                i.then_inc(z_s, 1)

            def moments1(b):
                dve.wait_ge(x_in, 16 * (b + 1))
                moments(b, stats1, stats1_s, mv1, mv1_s, z1_s)

            def norm1(b):
                after(dve, z1t_p, b)
                normalise(b, z1, mv1, rstd1, rstd1_s, z1_s)

            def k_gated(b):
                dve.wait_ge(k_p, b + 1)
                dve.wait_ge(gate_s, b + 1)
                after(dve, ek_s, b)
                for c in range(KC):
                    i = dve.scalar_tensor_tensor(out=kg[:, c, :], in0=half(DD)[:, c, :], scalar=cols[:, BK, c:c + 1],
                                                 in1=gate[:, c, :], op0=ALU.add, op1=ALU.mult)
                i.then_inc(kg_s, 1)

            def q_elu(b):
                dve.wait_ge(q1_s, b + 1)
                dve.scalar_tensor_tensor(out=q_t[:], in0=eq[:], scalar=1.0, in1=q1[:], op0=ALU.min,
                                         op1=ALU.max).then_inc(qt_s, 1)

            def k_elu(b):
                dve.wait_ge(ek_s, b + 1)
                dve.wait_ge(kg1_s, b + 1)
                dve.scalar_tensor_tensor(out=k_t[:], in0=ek[:], scalar=1.0, in1=kg1[:], op0=ALU.min,
                                         op1=ALU.max).then_inc(kt_s, 1)

            def v_bias(b):
                dve.wait_ge(v_p, b + 1)
                after(dve, av_p, b)
                dve.tensor_tensor(v_ext[:, :, 0:D], half(BB),
                                  bv_row[:].rearrange("p (a d) -> p a d", a=1).to_broadcast([P, TT, D]),
                                  ALU.add).then_inc(v_s, 1)

            def mask(b):
                dve.wait_ge(sc_p, b + 1)
                after(dve, av_p, b)
                dve.tensor_tensor(at[:].rearrange("p a n -> p (a n)"), BB[:, 0:3 * P],
                                  causal3[:].rearrange("p a n -> p (a n)"), ALU.mult).then_inc(at_s, 1)

            def residual1(b):
                dve.wait_ge(av_p, b + 1)
                for j, bank in enumerate((DD, A)):
                    i = dve.tensor_scalar(den[:, j:j + 1], bank[:, D:D + 1], DEN_EPS, None, ALU.add)
                i.then_inc(den_s, 1)
                dve.wait_ge(den_s, b + 1)
                dve.reciprocal(rden[:], den[:]).then_inc(rden_s, 1)
                dve.wait_ge(rden_s, b + 1)
                for j, bank in enumerate((DD, A)):
                    xj = x_all[:, bass.ds(b * TT + j, 1), :].squeeze(1)
                    i = dve.scalar_tensor_tensor(out=xj, in0=bank[:, 0:D], scalar=rden[:, j:j + 1], in1=xj,
                                                 op0=ALU.mult, op1=ALU.add)
                i.then_inc(x2_s, 1)

            def moments2(b):
                dve.wait_ge(x2_s, b + 1)
                moments(b, stats2, stats2_s, mv2, mv2_s, z2_s)

            def norm2(b):
                after(dve, z2t_p, b)
                normalise(b, z2, mv2, rstd2, rstd2_s, z2_s)

            def v_place(b):
                dve.wait_ge(v2_p, b + 1)
                after(dve, o_p, b)
                src = BB[0:S, 0:D].rearrange("s (g e d) -> s g e d", e=2, d=HD)
                bias = bv2_row[0:S, :].rearrange("s (g e d) -> s g e d", e=2, d=HD)
                for e in range(2):
                    i = dve.tensor_tensor(v_pad[:, :, e, e * HD:(e + 1) * HD], src[:, :, e, :], bias[:, :, e, :],
                                          ALU.add)
                i.then_inc(vpad_s, 1)

            def soft_shift(b, u):
                bank = (EE, FF)[u % 2][:, 0:QH * S].rearrange("p (h s) -> p h s", h=QH)
                dve.wait_ge(s_p, UNITS * b + u + 1)
                dve.tensor_reduce(mx[:, u % 2, :], bank, AX.X, ALU.max).then_inc(max_s, 1)
                dve.wait_ge(max_s, UNITS * b + u + 1)
                after(dve, pt_p, UNITS * b + u + 1 - PR)
                dve.tensor_tensor(pr[:, u % PR], bank,
                                  mx[:, u % 2, :].rearrange("p (h a) -> p h a", a=1).to_broadcast([P, QH, S]),
                                  ALU.subtract).then_inc(sub_s, 1)

            def soft_divide(b):
                dve.wait_ge(den2_p, b + 1)
                after(dve, y_p, b)
                dve.reciprocal(o_t[:], half(DD)).then_inc(rec_s, 1)
                dve.wait_ge(rec_s, b + 1)
                dve.wait_ge(o_p, b + 1)
                dve.tensor_tensor(o_t[:], half(C), o_t[:], ALU.mult).then_inc(ot_s, 1)

            def residual2(b):
                dve.wait_ge(y_p, b + 1)
                dve.wait_ge(xb_s, b + 1)
                x2 = x_all[:, bass.ds(b * TT, TT), :]
                dve.tensor_tensor(x2, half(C), x2, ALU.add).then_inc(x3_s, 1)

            def moments3(b):
                dve.wait_ge(x3_s, b + 1)
                moments(b, stats3, stats3_s, mv3, mv3_s, z3_s)

            def norm3(b):
                after(dve, z3t_p, b)
                after(dve, xs_s, b)
                normalise(b, z3, mv3, rstd3, rstd3_s, z3_s)

            def logits_copy(b):
                dve.wait_ge(lgt_p, b + 1)
                after(dve, lg_p, b)
                dve.tensor_copy(lg_t[:], C[0:E, 0:T]).then_inc(lgt_s, 1)

            def choose(b):
                dve.wait_ge(lg_p, b + 1)
                dve.tensor_copy(lg[:], C[:, 0:TT * E].rearrange("p (j e) -> p j e", j=TT)).then_inc(lg_s, 1)
                dve.wait_ge(lg_s, b + 1)
                apart(dve)
                for j in range(TT):
                    i = dve.max(top[:, j, :], lg[:, j, :])
                i.then_inc(top_s, 1)
                dve.wait_ge(top_s, b + 1)
                apart(dve)
                for j in range(TT):
                    i = dve.max_index(top_i[:, j, :], top[:, j, :], lg[:, j, :])
                i.then_inc(topi_s, 1)
                after(dve, ediff_s, b)
                dve.tensor_tensor(diff[:, :, 0:E], lg[:], top[:, :, 0:1].to_broadcast([P, TT, E]), ALU.subtract)
                dve.tensor_tensor(diff[:, :, E:E + TOP_K], top[:, :, 0:TOP_K],
                                  top[:, :, 0:1].to_broadcast([P, TT, TOP_K]), ALU.subtract).then_inc(diff_s, 1)
                dve.wait_ge(topi_s, b + 1)
                dve.tensor_copy(top_f[:], top_i[:, :, 0:TOP_K]).then_inc(topf_s, 1)
                dve.wait_ge(topf_s, b + 1)
                for k in range(TOP_K):
                    i = dve.tensor_tensor(pick[:, :, k, :],
                                          iota_e[:].rearrange("p (a e) -> p a e", a=1).to_broadcast([P, TT, E]),
                                          top_f[:, :, k:k + 1].to_broadcast([P, TT, E]), ALU.is_equal)
                i.then_inc(pick_s, 1)
                dve.wait_ge(pick_s, b + 1)
                after(dve, rank_p, b)
                dve.tensor_tensor(pick_b[:], pick[:, :, 0, :], pick[:, :, 1, :], ALU.add).then_inc(pickb_s, 1)

            def score_rows(b):
                dve.wait_ge(ediff_s, b + 1)
                dve.tensor_reduce(esum[:], ediff[:, :, 0:E], AX.X, ALU.add).then_inc(esum_s, 1)
                dve.wait_ge(esum_s, b + 1)
                dve.reciprocal(erec[:], esum[:]).then_inc(erec_s, 1)
                dve.wait_ge(erec_s, b + 1)
                after(dve, xs_s, b)
                dve.tensor_tensor(score[:], ediff[:, :, E:E + TOP_K],
                                  erec[:].rearrange("p (j a) -> p j a", a=1).to_broadcast([P, TT, TOP_K]),
                                  ALU.mult).then_inc(score_s, 1)

            def place(b):
                dve.wait_ge(rank_p, b + 1)
                dve.tensor_tensor(posx[:], C[:, 0:TT * E].rearrange("p (j e) -> p j e", j=TT),
                                  base[:].rearrange("p (a e) -> p a e", a=1).to_broadcast([P, TT, E]),
                                  ALU.add).then_inc(posx_s, 1)
                dve.wait_ge(posx_s, b + 1)
                dve.tensor_tensor(base[:], C[:, 2 * E:3 * E], base[:], ALU.add).then_inc(base_s, 1)
                for k in range(TOP_K):
                    i = dve.tensor_tensor(posm[:, :, k, :], pick[:, :, k, :], posx[:], ALU.mult)
                i.then_inc(posm_s, 1)
                dve.wait_ge(posm_s, b + 1)
                dve.tensor_reduce(pos_f[:], posm[:], AX.X, ALU.add).then_inc(posf_s, 1)
                dve.wait_ge(posf_s, b + 1)
                after(dve, scattered, 16 * TT * TOP_K * b)
                apart(dve)
                dve.tensor_copy(pos_cur[:], pos_f[:]).then_inc(pos_s, 1)

            def shared_gate(b):
                dve.wait_ge(sth_s, b + 1)
                dve.scalar_tensor_tensor(out=sth[:], in0=sth[:], scalar=1.0, in1=half(EE), op0=ALU.add,
                                         op1=ALU.mult).then_inc(su_s, 1)

            def shared_mult(b):
                dve.wait_ge(su_s, b + 1)
                dve.wait_ge(b_p, b + 1)
                after(dve, sy_p, b)
                dve.scalar_tensor_tensor(out=sh[:], in0=sth[:], scalar=0.5, in1=half(FF), op0=ALU.mult,
                                         op1=ALU.mult).then_inc(sh_s, 1)

            def residual3(b):
                dve.wait_ge(sy_p, b + 1)
                x3 = x_all[:, bass.ds(b * TT, TT), :]
                dve.tensor_tensor(x3, half(DD), x3, ALU.add).then_inc(x4_s, 1)

            def turn(i, has1, has2, has3, more1, has4=True):
                j, l = i - 1, i - 2
                if has3:
                    soft_divide(l)
                if has2:
                    v_place(j)
                for u in range(UNITS):
                    if has2:
                        soft_shift(j, u)
                    if more1 and u == 0:
                        moments1(i + 1)
                    if has1 and u == 1:
                        k_gated(i)
                    if has3 and u == 2:
                        residual2(l)
                        moments3(l)
                    if u == 3:
                        if more1:
                            norm1(i + 1)
                        if has1:
                            q_elu(i)
                            k_elu(i)
                        if has1:
                            v_bias(i)
                        if has3:
                            norm3(l)
                        if isinstance(i, int) and i == 0:
                            dve.wait_ge(self1_s, 1)
                            dve.tensor_tensor(self_lo[:], low_room[:, 0:KC * 4 * D], self_lo[:],
                                              ALU.subtract).then_inc(self_lo_s, 1)
                    if has1 and u == 4:
                        mask(i)
                    if has4 and u == 4:
                        residual3(i - 3)
                    if has1 and u == 5:
                        residual1(i)
                        moments2(i)
                    if has3 and u == 6:
                        logits_copy(l)
                    if has1 and u == 6:
                        norm2(i)
                if has3:
                    choose(l)
                    score_rows(l)
                    shared_gate(l)
                    place(l)
                    shared_mult(l)

            def low_parts(k):
                dve.wait_ge(hi_s, 4 * len(low_pieces))
                dve.wait_ge(raw_in[k], 16)
                es = low_pieces[k]
                dve.tensor_tensor(w13_lo[:, es], w13_raw[:, es], w13_hi[:, es], ALU.subtract).then_inc(lo_s, 1)

            dve.wait_ge(const, 1)
            dve.tensor_copy(base[:], ebase[:]).then_inc(base0_s, 1)
            dve.wait_ge(base0_s, 1)
            moments1(0)
            norm1(0)
            dve.wait_ge(cols_p, 1)
            dve.tensor_copy(cols[:], GG[:, 0:8 * KC].rearrange("p (c v) -> p v c", c=KC)).then_inc(cols_s, 1)
            dve.wait_ge(cols_s, 1)
            dve.wait_ge(rows_b_in, 16 * len(rows))
            for i in range(4):
                turn(i, True, i >= 1, i >= 2, True, i >= 3)
            with dve.Fori(4, B - 1) as i:
                turn(i, True, True, True, True)
            turn(B - 1, True, True, True, False)
            turn(B, False, True, True, False)
            low_parts(0)
            turn(B + 1, False, False, True, False)
            dve.wait_ge(base_s, B)
            dve.tensor_copy(pad_i[:], base[0:1, :]).then_inc(padi_s, 1)
            dve.tensor_tensor(cnt[:], base[:], ebase[:], ALU.subtract).then_inc(tab_step, 1)
            dve.wait_ge(tab_step, 1)
            dve.tensor_scalar(tiles_i[:], cnt[:], 1.0 / P, 0.5 - 0.5 / P, ALU.mult, ALU.add).then_inc(tab_step, 1)
            dve.wait_ge(tab_step, 2)
            dve.tensor_copy(tiles[:], tiles_i[:])
            dve.tensor_copy(tile_end[:], tiles_i[:]).then_inc(tab_step, 1)
            dve.wait_ge(tab_step, 3)
            for e in range(1, E):
                dve.tensor_tensor(tile_end[:, e:e + 1], tile_end[:, e:e + 1], tile_end[:, e - 1:e],
                                  ALU.add).then_inc(tab_step, 1)
                dve.wait_ge(tab_step, 3 + e)
            t0 = 2 + E
            dve.tensor_scalar(coef[:], tiles[:], -float(P), float(REGION), ALU.mult, ALU.add).then_inc(tab_step, 1)
            dve.tensor_tensor(past, iota_t[:].rearrange("p (n a) -> p n a", a=1).to_broadcast([1, EXPERT_TILES, E]),
                              tile_end[0:1].rearrange("p (a e) -> p a e", a=1).to_broadcast([1, EXPERT_TILES, E]),
                              ALU.is_ge).then_inc(tab_step, 1)
            dve.wait_ge(tab_step, t0 + 2)
            dve.tensor_tensor(past_c, past,
                              coef[0:1].rearrange("p (a e) -> p a e", a=1).to_broadcast([1, EXPERT_TILES, E]),
                              ALU.mult)
            dve.tensor_reduce(tile_e[:], past, AX.X, ALU.add).then_inc(tab_step, 1)
            dve.wait_ge(tab_step, t0 + 3)
            dve.tensor_reduce(tile_r[:], past_c, AX.X, ALU.add).then_inc(tab_step, 1)
            dve.tensor_scalar(tab_e[:], tile_e[:], float(E - 1), None, ALU.min).then_inc(tab_step, 1)
            dve.wait_ge(tab_step, t0 + 5)
            dve.scalar_tensor_tensor(out=tile_r[:], in0=iota_t[:], scalar=float(P), in1=tile_r[:], op0=ALU.mult,
                                     op1=ALU.add).then_inc(tab_step, 1)
            dve.wait_ge(tab_step, t0 + 6)
            for k, first in ((0, 4), (ROUND, 1)):
                i = dve.tensor_tensor(round_e[:, :, k:k + ROUND],
                                      tab_e[:, first:first + ROUND * ROUNDS].rearrange("p (m k) -> p m k", k=ROUND),
                                      digit[:, k:k + ROUND].rearrange("p (a k) -> p a k", a=1).to_broadcast(
                                          [1, ROUNDS, ROUND]), ALU.mult)
            i.then_inc(tab_step, 1)
            dve.wait_ge(tab_step, t0 + 7)
            dve.tensor_reduce(round_sum[:], round_e[:], AX.X, ALU.add).then_inc(tab_step, 1)
            dve.wait_ge(tab_step, t0 + 8)
            dve.tensor_copy(tab_round[:], round_sum[:])
            dve.tensor_scalar(tab_r[:], tile_r[:], float(IDLE_ROW), None, ALU.min).then_inc(tab_s, 1)

            turn(B + 2, False, False, False, False)

            def tile_low_x(n, s):
                dve.wait_ge(xet_s, n + 1)
                after(dve, h_p, n - 1)
                dve.tensor_tensor(xe_lo[:, s], (A, BB)[s][:, 0:D].rearrange("p (c t) -> p c t", c=KC), xe_hi[:, s],
                                  ALU.subtract).then_inc(xlo_s, 1)

            def tile_low_h(n, s):
                dve.wait_ge(eht_s, n + 1)
                after(dve, ey_p, n - 1)
                dve.tensor_tensor(eh_lo[:, s], (EE, FF)[s][:, 0:D].rearrange("p (c t) -> p c t", c=KC), eh_hi[:, s],
                                  ALU.subtract).then_inc(hlo_s, 1)

            def tile_silu(n, s):
                bank = (C, DD)[s]
                dve.wait_ge(eth_s, n + 1)
                dve.scalar_tensor_tensor(out=eu[:, s, :], in0=eth[:, s, :], scalar=1.0, in1=bank[:, 0:D], op0=ALU.add,
                                         op1=ALU.mult).then_inc(eu_s, 1)
                dve.wait_ge(eu_s, n + 1)
                after(dve, eht_p, n - 1)
                dve.scalar_tensor_tensor(out=eh[:, s, :], in0=eu[:, s, :], scalar=0.5, in1=bank[:, D:2 * D],
                                         op0=ALU.mult, op1=ALU.mult).then_inc(eh_s, 1)

            def tile_copy_y(n, s):
                dve.wait_ge(ey_p, n + 1)
                after(dve, ey_out[s], (n - s) * 8)
                dve.tensor_copy(ey[:, s, :], (GG, HH)[s][:, 0:D]).then_inc(ey_s, 1)

            dve.wait_ge(kt_s, B)
            def tile_step(n, s, ahead3=True, ahead2=True, behind=True):
                if ahead3:
                    tile_low_x(n + 3, 1 - s)
                tile_low_h(n, s)
                if behind:
                    tile_copy_y(n - 1, 1 - s)
                if ahead2:
                    tile_silu(n + 2, s)

            low_parts(2)
            tile_low_x(0, 0)
            tile_low_x(1, 1)
            dve.wait_ge(raw_in[3], 16)
            for e in range(0, E, 2):
                i = dve.tensor_tensor(w2_lo[:, e:e + 2], w2_raw[:, e:e + 2], w2_hi[:, e:e + 2], ALU.subtract)
            i.then_inc(lo_s, 1)
            dve.wait_ge(h_p, 1)
            tile_silu(0, 0)
            tile_low_x(2, 0)
            tile_silu(1, 1)
            tile_step(0, 0, behind=False)
            tile_step(1, 1)
            with dve.Fori(1, EXPERT_TILES // 2 - 2) as m:
                tile_step(2 * m, 0)
                tile_step(2 * m + 1, 1)
            tile_step(EXPERT_TILES - 4, 0)
            tile_step(EXPERT_TILES - 3, 1, ahead3=False)
            tile_step(EXPERT_TILES - 2, 0, ahead3=False, ahead2=False)
            tile_step(EXPERT_TILES - 1, 1, ahead3=False, ahead2=False)
            tile_copy_y(EXPERT_TILES - 1, 1)

            def add_got(b, k):
                dve.wait_ge(got_in[k], (b - k) * (16 // GOT) + 16)
                x4 = x_all[:, bass.ds(b * TT, TT), :]
                apart(dve)
                dve.tensor_tensor(x4, got[:, k, :, 0, :], x4, ALU.add).then_inc(sum1_s, 1)
                dve.wait_ge(sum1_s, b + 1)
                dve.tensor_tensor(x4, got[:, k, :, 1, :], x4, ALU.add).then_inc(fin_s, 1)

            for b in range(GOT):
                add_got(b, b)
            with dve.Fori(1, B // GOT) as m:
                for k in range(GOT):
                    add_got(GOT * m + k, k)



def kernel(**inputs):
    import numpy as _np
    import concourse.bacc as _bacc
    from concourse import mybir as _mybir
    from concourse.bass_utils import run_bass_kernel_spmd as _run

    def arr(name):
        return _np.ascontiguousarray(inputs[name])

    def turned(name):
        return _np.ascontiguousarray(_np.asarray(inputs[name]).T)

    def beside(a, b):
        return _np.ascontiguousarray(_np.concatenate([_np.asarray(inputs[a]), _np.asarray(inputs[b])], axis=-1))

    args = [
        ("x", arr("x")), ("ctx_mem", arr("ctx_1024")),
        ("w_qkv", arr("L0_attn_qkv_w")), ("b_qkv", arr("L0_attn_qkv_b")),
        ("w_gate", arr("L0_attn_gate_w")), ("b_gate", arr("L0_attn_gate_b")),
        ("ln_g", arr("L0_attn_ln_g")), ("ln_b", arr("L0_attn_ln_b")),
        ("wq_t", turned("L0_xattn_Wq")), ("bq", arr("L0_xattn_bq")),
        ("wk_t", turned("L0_xattn_Wk")), ("bk", arr("L0_xattn_bk")),
        ("wv_t", turned("L0_xattn_Wv")), ("bv", arr("L0_xattn_bv")),
        ("wo_t", turned("L0_xattn_Wo")), ("bo", arr("L0_xattn_bo")),
        ("router_t", turned("L0_ffn_gate_w")),
        ("w13", beside("L0_ffn_w1", "L0_ffn_w3")), ("w2", arr("L0_ffn_w2")),
        ("w13s", beside("L0_ffn_w1s", "L0_ffn_w3s")[0]), ("w2s", arr("L0_ffn_w2s")[0]),
    ]
    nc = _bacc.Bacc("TRN2", target_bir_lowering=False, num_devices=1)
    arrays, aps = {}, []
    for name, a in args:
        arrays[f"in_{name}"] = a
        aps.append(nc.dram_tensor(f"in_{name}", a.shape, _mybir.dt.from_np(a.dtype), kind="ExternalInput").ap())
    shape = inputs["x"].shape
    aps.append(nc.dram_tensor("out_0", shape, _mybir.dt.float32, kind="ExternalOutput").ap())
    decoder_layer_kernel(nc, *aps)
    r = _run(nc, [arrays], core_ids=[0])
    return r.results[0]["out_0"]
```
